# Optimizing a Trainium2 kernel written in Bass

```python
import numpy as np
import jax
import jax.numpy as jnp

def _softmax(x, axis=-1):
    return jax.nn.softmax(x, axis=axis)

def _gelu(x):
    return jax.nn.gelu(x, approximate=True)

def _silu(x):
    return jax.nn.silu(x)

def _sigmoid(x):
    return jax.nn.sigmoid(x)

def _layernorm(x, axis=-1, eps=1e-05):
    m = jnp.mean(x, axis=axis, keepdims=True)
    v = jnp.var(x, axis=axis, keepdims=True)
    return (x - m) / jnp.sqrt(v + eps)

def _scatter_add(tgt, idx, src, axis=0):
    return tgt.at[idx].add(src)

def _segment_sum(src, seg, n):
    return jax.ops.segment_sum(src, seg, n)
kernel_name = 'mk_gnn_resnorm_d2_gnn_r32_db1ccd'

def setup_inputs(seed: int=0):
    np.random.seed(seed)
    _w = jnp.asarray

    def _rec_inputs():
        import jax
        import jax.numpy as jnp
        _gk = jax.random.key(seed)
        x = -0.0005121 + 1.001 * jax.random.normal(jax.random.fold_in(_gk, 1), (50000, 64), jnp.float32)
        src = jax.random.randint(jax.random.fold_in(_gk, 2), (50000,), 0, 50000, jnp.int32)
        dst = jax.random.randint(jax.random.fold_in(_gk, 3), (50000,), 0, 50000, jnp.int32)
        _o = jnp.argsort(dst, stable=True)
        src = src[_o]
        dst = dst[_o]
        edge_attr_32 = -5.3897e-05 + 0.999841 * jax.random.normal(jax.random.fold_in(_gk, 12), (50000, 32), jnp.float32)
        edge_weight = jax.random.uniform(jax.random.fold_in(_gk, 13), (50000,), jnp.float32, 0.0, 0.999999)
        return (x, src, dst, edge_attr_32, edge_weight)
    x, src, dst, edge_attr_32, edge_weight = _rec_inputs()

    def _L0_gnn_setup():
        import jax, jax.numpy as jnp
        import numpy as np
        ALPHA = 0.1
        K = 10
        N_NODES = 50000
        N_EDGES = 25000
        D_FEAT = 64
        key = jax.random.key(seed)
        k1, k2, k3, k4 = jax.random.split(key, 4)
        x = jax.random.normal(k1, (N_NODES, D_FEAT), dtype=jnp.float32)
        edge_src = jax.random.randint(k2, (N_EDGES,), 0, N_NODES, dtype=jnp.int32)
        edge_dst = jax.random.randint(k3, (N_EDGES,), 0, N_NODES, dtype=jnp.int32)
        edge_weight = jax.random.uniform(k4, (N_EDGES,), dtype=jnp.float32)
        return {'x': x, 'edge_src': edge_src, 'edge_dst': edge_dst, 'edge_weight': edge_weight}
    _L0_gnn_all = _L0_gnn_setup()
    _L0_gnn_in = {k: v for k, v in _L0_gnn_all.items() if k in ()}
    del _L0_gnn_all

    def _L1_gnn_setup():
        import jax, jax.numpy as jnp
        import numpy as np
        N_NODES = 50000
        N_EDGES = 25000
        D_NODE = 64
        D_EDGE = 32
        MSG_FEATS = [128, 64]
        NODE_FEATS = [128, 64]
        LN_EPS = 1e-06

        def _he_normal(key, fan_in, fan_out):
            std = np.sqrt(2.0 / fan_in).astype(np.float32)
            return jax.random.normal(key, (fan_in, fan_out), jnp.float32) * std

        def _layernorm(x, g, b):
            m = jnp.mean(x, axis=-1, keepdims=True)
            v = jnp.mean(jnp.square(x - m), axis=-1, keepdims=True)
            return (x - m) * jax.lax.rsqrt(v + LN_EPS) * g + b

        def _mlp(x, layers):
            for W, b, g, beta in layers:
                x = _layernorm(jax.nn.relu(x @ W + b), g, beta)
            return x
        key = jax.random.key(seed)
        ks = jax.random.split(key, 8)
        inp = {}
        inp['nodes'] = jax.random.normal(ks[0], (N_NODES, D_NODE), jnp.float32)
        inp['edges'] = jax.random.normal(ks[1], (N_EDGES, D_EDGE), jnp.float32)
        inp['senders'] = jax.random.randint(ks[2], (N_EDGES,), 0, N_NODES)
        inp['receivers'] = jax.random.randint(ks[3], (N_EDGES,), 0, N_NODES)
        inp['eps'] = jax.random.normal(ks[4], (1,), jnp.float32) * 0.1

        def make_mlp(k, in_dim, feats, prefix):
            kk = jax.random.split(k, len(feats))
            d = in_dim
            for i, (ki, f) in enumerate(zip(kk, feats)):
                inp[f'{prefix}_W{i}'] = _he_normal(ki, d, f)
                inp[f'{prefix}_b{i}'] = jnp.zeros((f,), jnp.float32)
                inp[f'{prefix}_g{i}'] = jnp.ones((f,), jnp.float32)
                inp[f'{prefix}_beta{i}'] = jnp.zeros((f,), jnp.float32)
                d = f
        make_mlp(ks[5], D_NODE, MSG_FEATS, 'self')
        make_mlp(ks[6], D_NODE + D_EDGE, MSG_FEATS, 'msg')
        make_mlp(ks[7], MSG_FEATS[-1], NODE_FEATS, 'node')
        return inp
    _L1_gnn_all = _L1_gnn_setup()
    _L1_gnn_in = {k: v for k, v in _L1_gnn_all.items() if k in ('eps', 'self_W0', 'self_b0', 'self_g0', 'self_beta0', 'self_W1', 'self_b1', 'self_g1', 'self_beta1', 'msg_W0', 'msg_b0', 'msg_g0', 'msg_beta0', 'msg_W1', 'msg_b1', 'msg_g1', 'msg_beta1', 'node_W0', 'node_b0', 'node_g0', 'node_beta0', 'node_W1', 'node_b1', 'node_g1', 'node_beta1')}
    del _L1_gnn_all
    return {'x': x, 'src': src, 'dst': dst, 'edge_attr_32': edge_attr_32, 'edge_weight': edge_weight, 'L1_gnn_eps': _L1_gnn_in['eps'], 'L1_gnn_self_W0': _L1_gnn_in['self_W0'], 'L1_gnn_self_b0': _L1_gnn_in['self_b0'], 'L1_gnn_self_g0': _L1_gnn_in['self_g0'], 'L1_gnn_self_beta0': _L1_gnn_in['self_beta0'], 'L1_gnn_self_W1': _L1_gnn_in['self_W1'], 'L1_gnn_self_b1': _L1_gnn_in['self_b1'], 'L1_gnn_self_g1': _L1_gnn_in['self_g1'], 'L1_gnn_self_beta1': _L1_gnn_in['self_beta1'], 'L1_gnn_msg_W0': _L1_gnn_in['msg_W0'], 'L1_gnn_msg_b0': _L1_gnn_in['msg_b0'], 'L1_gnn_msg_g0': _L1_gnn_in['msg_g0'], 'L1_gnn_msg_beta0': _L1_gnn_in['msg_beta0'], 'L1_gnn_msg_W1': _L1_gnn_in['msg_W1'], 'L1_gnn_msg_b1': _L1_gnn_in['msg_b1'], 'L1_gnn_msg_g1': _L1_gnn_in['msg_g1'], 'L1_gnn_msg_beta1': _L1_gnn_in['msg_beta1'], 'L1_gnn_node_W0': _L1_gnn_in['node_W0'], 'L1_gnn_node_b0': _L1_gnn_in['node_b0'], 'L1_gnn_node_g0': _L1_gnn_in['node_g0'], 'L1_gnn_node_beta0': _L1_gnn_in['node_beta0'], 'L1_gnn_node_W1': _L1_gnn_in['node_W1'], 'L1_gnn_node_b1': _L1_gnn_in['node_b1'], 'L1_gnn_node_g1': _L1_gnn_in['node_g1'], 'L1_gnn_node_beta1': _L1_gnn_in['node_beta1']}

def reference(x, src, dst, edge_attr_32, edge_weight, L1_gnn_eps, L1_gnn_self_W0, L1_gnn_self_b0, L1_gnn_self_g0, L1_gnn_self_beta0, L1_gnn_self_W1, L1_gnn_self_b1, L1_gnn_self_g1, L1_gnn_self_beta1, L1_gnn_msg_W0, L1_gnn_msg_b0, L1_gnn_msg_g0, L1_gnn_msg_beta0, L1_gnn_msg_W1, L1_gnn_msg_b1, L1_gnn_msg_g1, L1_gnn_msg_beta1, L1_gnn_node_W0, L1_gnn_node_b0, L1_gnn_node_g0, L1_gnn_node_beta0, L1_gnn_node_W1, L1_gnn_node_b1, L1_gnn_node_g1, L1_gnn_node_beta1):
    import jax
    import jax.numpy as jnp

    def _L0_gnn_ref(x, edge_src, edge_dst, edge_weight):
        import jax, jax.numpy as jnp
        import numpy as np
        ALPHA = 0.1
        K = 10
        N_NODES = 50000
        N_EDGES = 25000
        D_FEAT = 64

        def step(h, _):
            msgs = h[edge_src] * edge_weight[:, None]
            agg = jax.ops.segment_sum(msgs, edge_dst, num_segments=N_NODES)
            h_new = (1.0 - ALPHA) * agg + ALPHA * x
            return (h_new, None)
        h, _ = jax.lax.scan(step, x, None, length=K)
        return h

    def _L1_gnn_ref(nodes, edges, senders, receivers, eps, self_W0, self_b0, self_g0, self_beta0, self_W1, self_b1, self_g1, self_beta1, msg_W0, msg_b0, msg_g0, msg_beta0, msg_W1, msg_b1, msg_g1, msg_beta1, node_W0, node_b0, node_g0, node_beta0, node_W1, node_b1, node_g1, node_beta1):
        import jax, jax.numpy as jnp
        import numpy as np
        N_NODES = 50000
        N_EDGES = 25000
        D_NODE = 64
        D_EDGE = 32
        MSG_FEATS = [128, 64]
        NODE_FEATS = [128, 64]
        LN_EPS = 1e-06

        def _he_normal(key, fan_in, fan_out):
            std = np.sqrt(2.0 / fan_in).astype(np.float32)
            return jax.random.normal(key, (fan_in, fan_out), jnp.float32) * std

        def _layernorm(x, g, b):
            m = jnp.mean(x, axis=-1, keepdims=True)
            v = jnp.mean(jnp.square(x - m), axis=-1, keepdims=True)
            return (x - m) * jax.lax.rsqrt(v + LN_EPS) * g + b

        def _mlp(x, layers):
            for W, b, g, beta in layers:
                x = _layernorm(jax.nn.relu(x @ W + b), g, beta)
            return x
        s = jnp.concatenate([senders, receivers], axis=0)
        r = jnp.concatenate([receivers, senders], axis=0)
        e = jnp.concatenate([edges, edges], axis=0)
        self_layers = [(self_W0, self_b0, self_g0, self_beta0), (self_W1, self_b1, self_g1, self_beta1)]
        msg_layers = [(msg_W0, msg_b0, msg_g0, msg_beta0), (msg_W1, msg_b1, msg_g1, msg_beta1)]
        node_layers = [(node_W0, node_b0, node_g0, node_beta0), (node_W1, node_b1, node_g1, node_beta1)]
        h_nodes = _mlp(nodes, self_layers)
        msg_in = jnp.concatenate([nodes[s], e], axis=-1)
        messages = _mlp(msg_in, msg_layers)
        aggr = jax.ops.segment_sum(messages, r, num_segments=N_NODES)
        return _mlp(h_nodes + eps * h_nodes + aggr, node_layers)
    x = _layernorm(x + _L0_gnn_ref(x, src, dst, edge_weight), axis=-1)
    x = _layernorm(x + _L1_gnn_ref(x, edge_attr_32, src, dst, L1_gnn_eps, L1_gnn_self_W0, L1_gnn_self_b0, L1_gnn_self_g0, L1_gnn_self_beta0, L1_gnn_self_W1, L1_gnn_self_b1, L1_gnn_self_g1, L1_gnn_self_beta1, L1_gnn_msg_W0, L1_gnn_msg_b0, L1_gnn_msg_g0, L1_gnn_msg_beta0, L1_gnn_msg_W1, L1_gnn_msg_b1, L1_gnn_msg_g1, L1_gnn_msg_beta1, L1_gnn_node_W0, L1_gnn_node_b0, L1_gnn_node_g0, L1_gnn_node_beta0, L1_gnn_node_W1, L1_gnn_node_b1, L1_gnn_node_g1, L1_gnn_node_beta1), axis=-1)
    return x

_drawn_inputs = setup_inputs


def setup_inputs(seed=0):
    import zlib

    import numpy as np

    out = dict(_drawn_inputs(seed))
    spreads = {'L1_gnn_self_b0': (0.0, 0.1),
     'L1_gnn_self_g0': (1.0, 0.2),
     'L1_gnn_self_beta0': (0.0, 0.1),
     'L1_gnn_self_b1': (0.0, 0.1),
     'L1_gnn_self_g1': (1.0, 0.2),
     'L1_gnn_self_beta1': (0.0, 0.1),
     'L1_gnn_msg_b0': (0.0, 0.1),
     'L1_gnn_msg_g0': (1.0, 0.2),
     'L1_gnn_msg_beta0': (0.0, 0.1),
     'L1_gnn_msg_b1': (0.0, 0.1),
     'L1_gnn_msg_g1': (1.0, 0.2),
     'L1_gnn_msg_beta1': (0.0, 0.1),
     'L1_gnn_node_b0': (0.0, 0.1),
     'L1_gnn_node_g0': (1.0, 0.2),
     'L1_gnn_node_beta0': (0.0, 0.1),
     'L1_gnn_node_b1': (0.0, 0.1),
     'L1_gnn_node_g1': (1.0, 0.2),
     'L1_gnn_node_beta1': (0.0, 0.1)}
    factors = {}
    for name, (base, spread) in spreads.items():
        noise = np.random.default_rng([zlib.crc32(name.encode()), seed]).standard_normal(out[name].shape)
        drawn = base * np.exp(spread * noise) if base else spread * noise
        out[name] = jnp.asarray(drawn.astype(out[name].dtype))
    for name, factor in factors.items():
        out[name] = (out[name] * factor).astype(out[name].dtype)
    return out
```

```python
import numpy as np
import concourse.bass as bass
from concourse import mybir
from contextlib import ExitStack

N = 50000
E = 50000
D = 64
DE = 32
H = 128
P = 128
T = 392
NP = P * T
FULL = N // T
REST = N - FULL * T
PAD_ID = NP - 1
U = 28
GROUPS = T // U
PAIRS = GROUPS // 2
ZROW = NP
TRASH = NP
K_STEPS = 10
ALPHA = 0.1
XD = D + 1
BIG = 1 << 22
Q = 4
ROUNDS = T // Q
TAILS = REST // (2 * Q)
assert REST % (2 * Q) == 0
NS = 3
EPS_MLP = 1e-6
EPS_OUT = 1e-5

MLPS = ("msg", "self", "node")


def build_program(nc, A, out):
    fp32, i32 = mybir.dt.float32, mybir.dt.int32
    ALU, ACT, AX = mybir.AluOpType, mybir.ActivationFunctionType, mybir.AxisListType
    OFF = bass.IndirectOffsetOnAxis
    ds = bass.ds

    def dram(name, shape, dt=fp32):
        return nc.dram_tensor(name, shape, dt).ap()

    xa = dram("xa", [NP, XD])
    run_sums = [dram(f"run_sums{i}", [NP + P, D]) for i in range(2)]
    msg_sums = dram("msg_sums", [NP + P, D])
    x1 = dram("x1", [NP, D])
    aggr_src = dram("aggr_src", [NP + P, D])
    h_self = dram("h_self", [NP, D])
    edge_attr = dram("edge_attr", [NP, DE])
    src_ids = dram("src_ids", [NP], i32)
    dst_ids = dram("dst_ids", [NP], i32)
    src_vals = dram("src_vals", [NP])
    in_rows = dram("in_rows", [NP], i32)
    node_rows = dram("node_rows", [NP], i32)
    add_rows = dram("add_rows", [NP], i32)

    def grid(table):
        return table.rearrange("(p t) d -> p t d", t=T)

    def line(table):
        return table.rearrange("(p t) -> p t", t=T)

    xa_g, x1_g, self_g, ea_g = grid(xa), grid(x1), grid(h_self), grid(edge_attr)
    run_g = [grid(t[0:NP, :]) for t in run_sums]
    msg_g, agg_g = grid(msg_sums[0:NP, :]), grid(aggr_src[0:NP, :])
    xa_flat = xa.rearrange("n (d o) -> (n d) o", o=1)
    out_g = out[0:FULL * T, :].rearrange("(p t) d -> p t d", t=T)

    ctx = ExitStack()
    with ctx:
        ctx.enter_context(nc.allow_non_contiguous_dma(reason="a column of indices beside the rows, and the partitions' next ids"))

        def sb(name, shape, dt=fp32):
            return ctx.enter_context(nc.sbuf_tensor(name, shape, dt))

        def pb(name, shape, dt=fp32):
            return ctx.enter_context(nc.psum_tensor(name, shape, dt))

        def sem(name):
            return ctx.enter_context(nc.semaphore(name))

        src_t = sb("src_t", [P, T], i32)
        dst_t = sb("dst_t", [P, T + 1], i32)
        src_f = sb("src_f", [P, T])
        dst_f = sb("dst_f", [P, T + 1])
        weight = sb("weight", [P, T])
        weight9 = sb("weight9", [P, T])
        same = sb("same", [P, T])
        lp_index = sb("lp_index", [P, T], i32)
        row_id = sb("row_id", [P, T], i32)
        lp_slot = [sb(f"lp_slot{b}", [P, U], i32) for b in range(2)]
        row_slot = [sb(f"row_slot{b}", [P, U], i32) for b in range(2)]
        src_slot = [sb(f"src_slot{b}", [P, U]) for b in range(2)]
        before = sb("before", [P, U])
        before_all = sb("before_all", [P, T])
        scratch = sb("scratch", [P, T])
        add_row_t = sb("add_row_t", [P, T], i32)
        node_row_t = sb("node_row_t", [P, T], i32)
        head_len = sb("head_len", [P, 1])
        fix_row = sb("fix_row", [P, 1], i32)
        row0 = sb("row0", [P, 1], i32)
        trash_t = sb("trash_t", [P, 1], i32)
        trash_f = sb("trash_f", [P, 1])
        gate_v = sb("gate_v", [P, 2])
        part = sb("part", [P, 1])
        carry = sb("carry", [P, D])
        carry_sel = sb("carry_sel", [P, P])
        WG_STEPS = 17
        ident = sb("ident", [P, P])
        upper = sb("upper", [P, P])
        lower = sb("lower", [P, P])
        eqm = sb("eqm", [P, P])
        center = sb("center", [P, P])
        ones = sb("ones", [P, P])
        mean_h = sb("mean_h", [P, 1])
        eps_mlp = sb("eps_mlp", [P, 1])
        eps_out = sb("eps_out", [P, 1])
        zeros = sb("zeros", [P, U * D])
        xw = sb("xw", [P, T, D])
        got = [sb(f"got{b}", [P, U, XD]) for b in range(2)]
        idx = [sb(f"idx{b}", [P, U], i32) for b in range(2)]
        idx_out = [sb(f"idx_out{b}", [P, U], i32) for b in range(2)]
        sums = [sb(f"sums{b}", [P, U, D]) for b in range(2)]
        c_mean = sb("c_mean", [P, U])
        c_sq = sb("c_sq", [P, U])
        c_sd = sb("c_sd", [P, U])
        c_rs = sb("c_rs", [P, U])
        KIN = {"msg": D + DE, "self": D, "node": D}
        w0 = {m: sb(f"w0_{m}", [KIN[m], H]) for m in MLPS}
        w1 = {m: sb(f"w1_{m}", [H, D]) for m in MLPS}
        wc = {m: sb(f"wc_{m}", [H, D]) for m in MLPS}
        cols = {m: sb(f"cols_{m}", [H, 3]) for m in MLPS}
        b1 = {m: sb(f"b1_{m}", [1, D]) for m in MLPS}
        c0 = {m: sb(f"c0_{m}", [P, D]) for m in MLPS}
        g1 = {m: sb(f"g1_{m}", [P, D]) for m in MLPS}
        beta1 = {m: sb(f"beta1_{m}", [P, D]) for m in MLPS}
        eps1 = sb("eps1", [P, 1])

        arena = xw[:, :, :].rearrange("p t d -> p (t d)")
        used = [0]

        def carve(*shape):
            size = int(np.prod(shape))
            a = arena[:, used[0]:used[0] + size]
            used[0] += size
            if len(shape) == 2:
                a = a.rearrange("p (a b) -> p a b", b=shape[1])
            return a

        xrow = [carve(U, D) for _ in range(2)]
        x_in = [[carve(Q, D + DE), carve(Q, D + DE), carve(Q, D)] for _ in range(2)]
        xt = [carve(Q * P) for _ in range(NS)]
        ht = [carve(Q * P) for _ in range(NS)]
        sq = [carve(Q * P) for _ in range(NS)]
        u = [carve(Q, D) for _ in range(NS)]
        usq = [carve(Q, D) for _ in range(NS)]
        sd1, rs1, mn, v2, sd2, rs2 = ([carve(Q) for _ in range(NS)] for _ in range(6))
        msg = [carve(Q, D) for _ in range(2)]
        msg_dst = carve(Q, D)
        msum = [carve(Q, D) for _ in range(2)]
        hself = [carve(Q, D) for _ in range(2)]
        eq = [carve(Q, P) for _ in range(2)]
        dsum = [carve(Q, D) for _ in range(2)]
        e_self, e_agg, e_got, e_x1, e_x, e_y, e_out = ([carve(Q, D) for _ in range(2)] for _ in range(7))
        assert used[0] <= T * D
        m_src = [sb(f"m_src{b}", [P, Q], i32) for b in range(2)]
        m_dst = [sb(f"m_dst{b}", [P, Q], i32) for b in range(2)]
        m_add = [sb(f"m_add{b}", [P, Q], i32) for b in range(2)]
        m_val = [sb(f"m_val{b}", [P, Q]) for b in range(2)]
        e_idx = [sb(f"e_idx{b}", [P, Q], i32) for b in range(2)]

        ps = [pb(f"ps{i}", [P, 512]) for i in range(8)]
        ps_a, ps_b = ps[0:NS], ps[NS:2 * NS]
        ps_eq, ps_sum = ps[6], ps[7]

        names = """const_pads const_zeros const_all prep ids_ready zrow_ready graph_ready in_loaded weights_loaded
            weights_mm weights_ready xa_ready copied ids_written lp_slots_ready eq_before_ps before_done before_kept
            add_rows_written nodes_loaded node_rows_written scaled0 scaled scanned carry_ps carry_ready carry_added
            c_step c_act t_done xt_ready h_done ht_ready c_done sq_ready q_done sd_ready rs_ready scaled_u u_ready
            relu_ready mean_sum mean_ready centred usq_ready var_ready sd2_ready rs2_ready normed gained out_ready
            eq_ps eq_ready dsum_ps dsum_ready adds_done e_added e_ready e_res f_sum f_mean f_cen f_sq f_var f_sd
            f_rs f_out src_slot_ready pool_passed pe_passed sp_passed""".split()
        (const_pads, const_zeros, const_all, prep, ids_ready, zrow_ready, graph_ready, in_loaded, weights_loaded,
         weights_mm, weights_ready, xa_ready, copied, ids_written, lp_slots_ready, eq_before_ps, before_done, before_kept,
         add_rows_written, nodes_loaded, node_rows_written, scaled0, scaled, scanned, carry_ps, carry_ready,
         carry_added, c_step, c_act, t_done, xt_ready, h_done, ht_ready, c_done, sq_ready, q_done, sd_ready,
         rs_ready, scaled_u, u_ready, relu_ready, mean_sum, mean_ready, centred, usq_ready, var_ready, sd2_ready,
         rs2_ready, normed, gained, out_ready, eq_ps, eq_ready, dsum_ps, dsum_ready, adds_done, e_added, e_ready,
         e_res, f_sum, f_mean, f_cen, f_sq, f_var, f_sd, f_rs, f_out, src_slot_ready, pool_passed, pe_passed, sp_passed) = [sem(n) for n in names]
        (lp_written, idx_loaded, gathered, sums_stored, idx_saved, x_loaded, x1_stored, m_idx, m_rows, m_got,
         m_add_loaded, msum_stored, self_stored, e_idx_loaded, e_loaded, e_x1_loaded, e_gathered, out_stored, tail_stored) = [
            [sem(f"{n}{b}") for b in range(2)] for n in
            ("lp_written idx_loaded gathered sums_stored idx_saved x_loaded x1_stored m_idx m_rows m_got "
             "m_add_loaded msum_stored self_stored e_idx_loaded e_loaded e_x1_loaded e_gathered out_stored tail_stored").split()]

        block = ctx.enter_context(nc.Block())

        def per_step(eng, body):
            with eng.Fori(0, (K_STEPS - 2) // 2) as pair:
                body(2 * pair + 1, 0, 1)
                body(2 * pair + 2, 1, 0)
            body(K_STEPS - 1, 0, 1)

        LAST = 1
        C_OPS = 7

        def by_pair(eng, body):
            for b in range(2):
                body(0, b, b)
            with eng.Fori(1, ROUNDS // 2) as i:
                for b in range(2):
                    body(i, b, 2 * i + b)

        def bc(a, n):
            return a.unsqueeze(2).to_broadcast([P, a.shape[1], n])

        def rows(a, q):
            return a.unsqueeze(1).to_broadcast([P, q, a.shape[1]])

        @block.sync
        def _(sp):
            sp.wait_ge(const_pads, 3)
            for t, a in ((src_t, A["src"]), (dst_t, A["dst"]), (weight, A["edge_weight"])):
                sp.dma_start(t[0:FULL, 0:T], a[0:FULL * T].rearrange("(p t) -> p t", t=T)).then_inc(in_loaded, 16)
                sp.dma_start(t[FULL:FULL + 1, 0:REST], a[FULL * T:N].rearrange("(p t) -> p t", p=1)).then_inc(in_loaded, 16)
            sp.dma_start(dst_t[0:FULL - 1, T:T + 1],
                         A["dst"][T:FULL * T].rearrange("(p t) -> p t", t=T)[:, 0:1]).then_inc(in_loaded, 16)
            sp.dma_start(dst_t[FULL - 1:FULL, T:T + 1],
                         A["dst"][FULL * T:FULL * T + 1].rearrange("(p t) -> p t", p=1)).then_inc(in_loaded, 16)
            sp.wait_ge(zrow_ready, 1)
            sp.dma_start(xa_g[:, :, D:XD].bitcast(i32), node_row_t[:, :].unsqueeze(2)).then_inc(xa_ready, 16)
            sp.dma_start(xa[0:N, 0:D], A["x"][:, :]).then_inc(xa_ready, 16)
            sp.wait_ge(const_zeros, 1)
            sp.dma_start(xa[N:N + P, 0:D], zeros[:, 0:D]).then_inc(xa_ready, 16)
            sp.dma_start(xa[N + P:NP, 0:D], zeros[0:NP - N - P, 0:D]).then_inc(xa_ready, 16)
            for t in (*run_sums, msg_sums, aggr_src):
                sp.dma_start(t[NP:NP + P, :], zeros[:, 0:D]).then_inc(copied, 16)
            sp.wait_ge(ids_ready, 1)
            sp.dma_start(line(src_ids), src_t[:, :]).then_inc(ids_written, 16)
            sp.dma_start(line(dst_ids), dst_t[:, 0:T]).then_inc(ids_written, 16)
            sp.dma_start(line(src_vals), src_f[:, :]).then_inc(ids_written, 16)
            sp.wait_ge(ids_written, 48)
            for b in range(2):
                sp.dma_start(idx[b][:, :], line(src_ids)[:, b * U:(b + 1) * U]).then_inc(idx_loaded[b], 16)
            sp.dma_start(edge_attr[0:E, :].rearrange("(a b) d -> a (b d)", b=25),
                         A["edge_attr_32"].rearrange("(a b) d -> a (b d)", b=25)).then_inc(copied, 16)
            sp.dma_start(edge_attr[N:N + P, :], zeros[:, 0:DE]).then_inc(copied, 16)
            sp.dma_start(edge_attr[N + P:NP, :], zeros[0:NP - N - P, 0:DE]).then_inc(copied, 16)
            for g in range(GROUPS):
                sp.dma_start(agg_g[:, g * U:(g + 1) * U, :],
                             zeros[:, :].rearrange("p (u d) -> p u d", d=D)).then_inc(copied, 16)
            for b in range(2):
                sp.wait_ge(lp_written[b], 16 * U * PAIRS)
            sp.dma_start(node_row_t[:, :].unsqueeze(2), xa_g[:, :, D:XD].bitcast(i32)).then_inc(nodes_loaded, 16)
            sp.wait_ge(nodes_loaded, 16)
            sp.dma_start(line(node_rows), node_row_t[:, :]).then_inc(node_rows_written, 16)
            sp.wait_ge(before_kept, GROUPS + 1)
            sp.dma_start(line(add_rows), add_row_t[:, :]).then_inc(add_rows_written, 16)

            def fill_idx(s, i, b, source):
                sp.wait_ge(gathered[b], 16 * U * (PAIRS * s + i))
                sp.dma_start(idx[b][:, :], line(source)[:, ds((2 * i + b) * U, U)]).then_inc(idx_loaded[b], 16)

            def pass0_out(i, b):
                sp.wait_ge(scanned, U * (2 * i + b + 1))
                sp.dma_start(run_g[0][:, ds((2 * i + b) * U, U), :], sums[b][:, :, :]).then_inc(sums_stored[b], 16)
                sp.wait_ge(scaled0, 3 * (2 * i + b) + 1)
                sp.sem_inc(sp_passed, 1)
                sp.dma_start(line(in_rows)[:, ds((2 * i + b) * U, U)], idx_out[b][:, :]).then_inc(idx_saved[b], 16)

            with sp.Fori(1, PAIRS) as i:
                for b in range(2):
                    fill_idx(0, i, b, src_ids)
                    pass0_out(i - 1, b)
            for b in range(2):
                pass0_out(PAIRS - 1, b)
            for b in range(2):
                sp.wait_ge(idx_saved[b], 16 * PAIRS)

            def one_step(s, source, target):
                for b in range(2):
                    sp.wait_ge(gathered[b], 16 * U * PAIRS * s)
                    sp.dma_start(idx[b][:, :], line(in_rows)[:, b * U:(b + 1) * U]).then_inc(idx_loaded[b], 16)

                def store(i, b):
                    sp.wait_ge(scanned, T * s + U * (2 * i + b + 1))
                    sp.dma_start(run_g[target][:, ds((2 * i + b) * U, U), :], sums[b][:, :, :]).then_inc(sums_stored[b], 16)

                with sp.Fori(1, PAIRS) as i:
                    for b in range(2):
                        fill_idx(s, i, b, in_rows)
                        store(i - 1, b)
                for b in range(2):
                    store(PAIRS - 1, b)

            per_step(sp, one_step)

            sp.wait_ge(node_rows_written, 16)

            def load_x(i, b):
                sp.dma_start(xrow[b], xa_g[:, ds((2 * i + b) * U, U), 0:D]).then_inc(x_loaded[b], 16)

            def store_x1(i, b):
                sp.wait_ge(c_step, C_OPS * (2 * i + b + 1))
                sp.dma_start(x1_g[:, ds((2 * i + b) * U, U), :], sums[b][:, :, :]).then_inc(x1_stored[b], 16)

            for b in range(2):
                sp.wait_ge(gathered[b], 16 * U * PAIRS * K_STEPS)
                sp.dma_start(idx[b][:, :], line(node_rows)[:, b * U:(b + 1) * U]).then_inc(idx_loaded[b], 16)
                load_x(0, b)
            with sp.Fori(1, PAIRS) as i:
                for b in range(2):
                    fill_idx(K_STEPS, i, b, node_rows)
                    store_x1(i - 1, b)
                    load_x(i, b)
            for b in range(2):
                store_x1(PAIRS - 1, b)
            for b in range(2):
                sp.wait_ge(x1_stored[b], 16 * PAIRS)
            sp.wait_ge(ids_written, 48)
            sp.wait_ge(add_rows_written, 16)
            sp.wait_ge(copied, 16 * (4 + 3 + GROUPS))

            def msg_round(i, b, r):
                first = isinstance(r, int)
                if not first:
                    sp.wait_ge(m_got[b], 16 * 2 * Q * i)
                sp.dma_start(m_src[b][:, :], line(src_ids)[:, ds(r * Q, Q)]).then_inc(m_idx[b], 16)
                sp.dma_start(m_dst[b][:, :], line(dst_ids)[:, ds(r * Q, Q)]).then_inc(m_idx[b], 16)
                if not first:
                    sp.wait_ge(t_done, NS * (r - 1))
                    sp.wait_ge(eq_ready, r - 1)
                for t in range(2):
                    sp.dma_start(x_in[b][t][:, :, D:D + DE], ea_g[:, ds(r * Q, Q), :]).then_inc(m_rows[b], 16)
                sp.dma_start(x_in[b][2], x1_g[:, ds(r * Q, Q), :]).then_inc(m_rows[b], 16)
                sp.dma_start(m_val[b][:, :], line(src_vals)[:, ds(r * Q, Q)]).then_inc(m_rows[b], 16)
                if not (isinstance(r, int) and r == 0):
                    msg_out(r - 1, 1 - b, first)

            def msg_out(r, b, first):
                if not first:
                    sp.wait_ge(adds_done, 16 * Q * (r - 1))
                sp.dma_start(m_add[b][:, :], line(add_rows)[:, ds(r * Q, Q)]).then_inc(m_add_loaded[b], 16)
                sp.wait_ge(scanned, T * K_STEPS + Q * (r + 1))
                sp.dma_start(msg_g[:, ds(r * Q, Q), :], msum[b]).then_inc(msum_stored[b], 16)
                sp.wait_ge(out_ready, NS * (r + 1))
                sp.dma_start(self_g[:, ds(r * Q, Q), :], hself[b]).then_inc(self_stored[b], 16)

            by_pair(sp, msg_round)
            msg_out(ROUNDS - 1, 1, False)
            for b in range(2):
                sp.wait_ge(msum_stored[b], 16 * ROUNDS // 2)
                sp.wait_ge(self_stored[b], 16 * ROUNDS // 2)
            sp.wait_ge(adds_done, 16 * T)

            def node_loads(i, s, first):
                if not first:
                    sp.wait_ge(e_gathered[s], 16 * Q * i)
                sp.dma_start(e_idx[s][:, :], line(node_rows)[:, ds((2 * i + s) * Q, Q)]).then_inc(e_idx_loaded[s], 16)
                if not first:
                    sp.wait_ge(e_ready, 2 * (i - 1) + s + 1)
                sp.dma_start(e_self[s], self_g[:, ds((2 * i + s) * Q, Q), :]).then_inc(e_loaded[s], 16)
                sp.dma_start(e_agg[s], agg_g[:, ds((2 * i + s) * Q, Q), :]).then_inc(e_loaded[s], 16)

            def node_x1(i, s, first):
                if not first:
                    sp.wait_ge(e_res, 2 * (i - 1) + s + 1)
                sp.dma_start(e_x1[s], x1_g[:, ds((2 * i + s) * Q, Q), :]).then_inc(e_x1_loaded[s], 16)

            def node_out(i, s):
                sp.wait_ge(f_out, 2 * i + s + 1)
                at = (2 * i + s) * Q
                sp.dma_start(out_g[0:112, ds(at, Q), :], e_out[s][0:112]).then_inc(out_stored[s], 16)
                sp.dma_start(out_g[112:FULL, ds(at, Q), :], e_out[s][112:FULL]).then_inc(out_stored[s], 16)

            def node_tail(i, s):
                sp.dma_start(out[ds(FULL * T + (2 * i + s) * Q, Q), :].rearrange("(o q) d -> o q d", o=1),
                             e_out[s][FULL:FULL + 1]).then_inc(tail_stored[s], 16)

            for s in range(2):
                node_loads(0, s, True)
                node_x1(0, s, True)
            with sp.Fori(1, TAILS + 1) as i:
                for s in range(2):
                    node_loads(i, s, False)
                    node_x1(i, s, False)
                for s in range(2):
                    node_out(i - 1, s)
                    node_tail(i - 1, s)
            with sp.Fori(TAILS + 1, ROUNDS // 2) as i:
                for s in range(2):
                    node_loads(i, s, False)
                    node_x1(i, s, False)
                for s in range(2):
                    node_out(i - 1, s)
            for s in range(2):
                node_out(ROUNDS // 2 - 1, s)
            for s in range(2):
                sp.wait_ge(out_stored[s], 32 * (ROUNDS // 2))
                sp.wait_ge(tail_stored[s], 16 * TAILS)

        @block.gpsimd
        def _(pool):
            nc.gpsimd.memset(src_t[:, :], PAD_ID).then_inc(const_pads, 1)
            nc.gpsimd.memset(dst_t[:, :], PAD_ID).then_inc(const_pads, 1)
            nc.gpsimd.memset(weight[:, :], 0.0).then_inc(const_pads, 1)
            nc.gpsimd.memset(node_row_t[:, :], ZROW).then_inc(zrow_ready, 1)
            nc.gpsimd.memset(zeros[:, :], 0.0).then_inc(const_zeros, 1)
            nc.gpsimd.iota(row_id[:, :], [[1, T]], base=0, channel_multiplier=T).then_inc(const_all, 1)
            nc.gpsimd.iota(row0[:, :], [[1, 1]], base=-1, channel_multiplier=T).then_inc(const_all, 1)
            nc.gpsimd.iota(trash_t[:, :], [[0, 1]], base=TRASH, channel_multiplier=1).then_inc(const_all, 1)
            nc.gpsimd.memset(ident[:, :], 0.0).then_inc(const_all, 1)
            nc.gpsimd.memset(ones[:, :], 1.0).then_inc(const_all, 1)
            nc.gpsimd.memset(mean_h[:, :], 1.0 / H).then_inc(const_all, 1)
            nc.gpsimd.memset(eps_mlp[:, :], EPS_MLP).then_inc(const_all, 1)
            nc.gpsimd.memset(eps_out[:, :], EPS_OUT).then_inc(const_all, 1)
            nc.gpsimd.memset(sums[1][:, :, :], 0.0).then_inc(const_all, 1)
            pool.wait_ge(const_all, 9)
            nc.gpsimd.affine_select(out=ident[:, :], in_=ident[:, :], compare_op=ALU.not_equal, fill=1.0,
                                    base=0, pattern=[[-1, P]], channel_multiplier=1).then_inc(const_all, 1)
            nc.gpsimd.affine_select(out=upper[:, :], in_=ones[:, :], compare_op=ALU.is_gt, fill=0.0,
                                    base=0, pattern=[[1, P]], channel_multiplier=-1).then_inc(const_all, 1)
            nc.gpsimd.affine_select(out=lower[:, :], in_=ones[:, :], compare_op=ALU.is_gt, fill=0.0,
                                    base=0, pattern=[[-1, P]], channel_multiplier=1).then_inc(const_all, 1)

            def passed():
                pool.sem_inc(pool_passed, 1)

            pool.wait_ge(xa_ready, 16 * 4)
            with pool.Fori(0, PAIRS) as i:
                for b in range(2):
                    pool.wait_ge(lp_slots_ready, 2 * (2 * i + b + 1))
                    passed()
                    for t in range(U):
                        pool.indirect_dma_start(xa_flat, OFF(ap=lp_slot[b][:, t:t + 1], axis=0), row_slot[b][:, t:t + 1].bitcast(fp32),
                                                None, bounds_check=NP * XD - 1, oob_is_err=False).then_inc(lp_written[b], 16)
            for b in range(2):
                pool.wait_ge(lp_written[b], 16 * U * PAIRS)

            def gather_group(table, width, s, i, b):
                pool.wait_ge(idx_loaded[b], 16 * (PAIRS * s + i + 1))
                passed()
                for t in range(U):
                    pool.indirect_dma_start(got[b][:, t, 0:width], None, table,
                                            OFF(ap=idx[b][:, t:t + 1], axis=0)).then_inc(gathered[b], 16)

            def end_of_pass(s, table):
                for b in range(2):
                    pool.wait_ge(sums_stored[b], 16 * PAIRS * (s + 1))
                pool.wait_ge(carry_ready, s + 1)
                passed()
                pool.indirect_dma_start(table, OFF(ap=fix_row[:, 0:1], axis=0), carry[:, :], None,
                                        compute_op=ALU.add).then_inc(carry_added, 16)
                pool.wait_ge(carry_added, 16 * (s + 1))
                passed()

            def one_pass(table, width, s):
                for b in range(2):
                    gather_group(table, width, s, 0, b)
                with pool.Fori(1, PAIRS) as i:
                    for b in range(2):
                        pool.wait_ge(scanned, T * s + U * (2 * i + b - 1))
                        gather_group(table, width, s, i, b)

            one_pass(xa[:, :], XD, 0)
            pool.wait_ge(graph_ready, 1)
            pool.wait_ge(copied, 16 * (4 + 3 + GROUPS))
            end_of_pass(0, run_sums[0][:, :])

            def one_step(s, source, target):
                one_pass(run_sums[source][:, :], D, s)
                end_of_pass(s, run_sums[target][:, :])

            per_step(pool, one_step)

            for b in range(2):
                gather_group(run_sums[LAST][:, :], D, K_STEPS, 0, b)
            with pool.Fori(1, PAIRS) as i:
                for b in range(2):
                    pool.wait_ge(c_step, C_OPS * (2 * i + b - 2) + 1)
                    gather_group(run_sums[LAST][:, :], D, K_STEPS, i, b)
            for b in range(2):
                pool.wait_ge(x1_stored[b], 16 * PAIRS)
            passed()

            def add_column(r, b, n, t):
                pool.wait_ge(dsum_ready, r + 1)
                pool.wait_ge(m_add_loaded[b], n)
                if not (isinstance(r, int) and r == 0 and t == 0):
                    pool.wait_ge(adds_done, 16 * (Q * r + t))
                passed()
                pool.indirect_dma_start(aggr_src[:, :], OFF(ap=m_add[b][:, t:t + 1], axis=0), dsum[b][:, t, :],
                                        None, compute_op=ALU.add).then_inc(adds_done, 16)

            def msg_round(i, b, r):
                first = isinstance(r, int)
                pool.wait_ge(m_idx[b], 32 * (i + 1))
                if not first:
                    pool.wait_ge(t_done, NS * (r - 1))
                passed()
                for t in range(Q):
                    pool.indirect_dma_start(x_in[b][0][:, t, 0:D], None, x1[:, :],
                                            OFF(ap=m_src[b][:, t:t + 1], axis=0)).then_inc(m_got[b], 16)
                    pool.indirect_dma_start(x_in[b][1][:, t, 0:D], None, x1[:, :],
                                            OFF(ap=m_dst[b][:, t:t + 1], axis=0)).then_inc(m_got[b], 16)
                    if not first:
                        add_column(r - 2, b, 16 * i, t)

            by_pair(pool, msg_round)
            for r in (ROUNDS - 2, ROUNDS - 1):
                for t in range(Q):
                    add_column(r, r % 2, 16 * ROUNDS // 2, t)
            for b in range(2):
                pool.wait_ge(msum_stored[b], 16 * ROUNDS // 2)
            pool.wait_ge(carry_ready, K_STEPS + 1)
            pool.indirect_dma_start(msg_sums[:, :], OFF(ap=fix_row[:, 0:1], axis=0), carry[:, :], None,
                                    compute_op=ALU.add).then_inc(carry_added, 16)
            pool.wait_ge(carry_added, 16 * (K_STEPS + 1))

            def node_gathers(i, s):
                pool.wait_ge(e_idx_loaded[s], 16 * (i + 1))
                passed()
                for t in range(Q):
                    pool.indirect_dma_start(e_got[s][:, t, :], None, msg_sums[:, :],
                                            OFF(ap=e_idx[s][:, t:t + 1], axis=0)).then_inc(e_gathered[s], 16)

            for s in range(2):
                node_gathers(0, s)
            with pool.Fori(1, ROUNDS // 2) as i:
                for s in range(2):
                    pool.wait_ge(e_ready, 2 * (i - 1) + s + 1)
                    node_gathers(i, s)

        @block.scalar
        def _(act):
            for m in MLPS:
                w = {k: A[f"L1_gnn_{m}_{k}"] for k in ("W0", "b0", "g0", "beta0", "W1", "b1", "g1", "beta1")}
                act.dma_start(w0[m][:, :], w["W0"]).then_inc(weights_loaded, 16)
                act.dma_start(w1[m][:, :], w["W1"]).then_inc(weights_loaded, 16)
                for c, k in enumerate(("b0", "g0", "beta0")):
                    act.dma_start(cols[m][:, c:c + 1], w[k].rearrange("(p o) -> p o", o=1)).then_inc(weights_loaded, 16)
                act.dma_start(b1[m][:, :], w["b1"].unsqueeze(0)).then_inc(weights_loaded, 16)
                act.dma_start(g1[m][:, :], w["g1"].partition_broadcast(P)).then_inc(weights_loaded, 16)
                act.dma_start(beta1[m][:, :], w["beta1"].partition_broadcast(P)).then_inc(weights_loaded, 16)
            act.dma_start(eps1[:, :], A["L1_gnn_eps"].partition_broadcast(P)).then_inc(weights_loaded, 16)
            act.wait_ge(const_all, 12)
            act.wait_ge(weights_ready, 1)

            with act.Fori(0, PAIRS) as i:
                for b in range(2):
                    g = 2 * i + b
                    act.wait_ge(x_loaded[b], 16 * (i + 1))
                    nc.scalar.activation(xrow[b], xrow[b], ACT.Copy, scale=1.0 + ALPHA).then_inc(c_act, 1)
                    act.wait_ge(c_step, C_OPS * g + 4)
                    nc.scalar.activation(xrow[b], sums[b][:, :, :], ACT.Square).then_inc(c_act, 1)
                    act.wait_ge(c_step, C_OPS * g + 5)
                    nc.scalar.activation(c_sd[:, :], c_sq[:, :], ACT.Sqrt, bias=eps_out[:, 0:1], scale=1.0 / D).then_inc(c_act, 1)

            def mlp(n, S, first, names, between, last):
                for s, m in enumerate(names):
                    act.wait_ge(t_done, n(s))
                    if not first:
                        act.wait_ge(h_done, n(s) - S)
                    K = KIN[m]
                    nc.scalar.activation(xt[s][0:K, :], ps_a[s][0:K, :], ACT.Copy).then_inc(xt_ready, 1)
                for s, m in enumerate(names):
                    act.wait_ge(h_done, n(s))
                    if not first:
                        act.wait_ge(q_done, n(s) - S)
                    nc.scalar.activation(ht[s], ps_b[s][:, :], ACT.Relu, bias=cols[m][:, 0:1]).then_inc(ht_ready, 1)
                between()
                for s, m in enumerate(names):
                    act.wait_ge(c_done, n(s))
                    nc.scalar.activation(sq[s], ps_a[s][:, :], ACT.Square).then_inc(sq_ready, 1)
                for s, m in enumerate(names):
                    act.wait_ge(q_done, n(s))
                    if not first:
                        act.wait_ge(rs_ready, n(s) - S)
                    nc.scalar.activation(sd1[s], ps_b[s][:, Q * D:Q * D + Q], ACT.Sqrt, bias=eps_mlp[:, 0:1]).then_inc(sd_ready, 1)
                for s, m in enumerate(names):
                    act.wait_ge(u_ready, n(s))
                    nc.scalar.activation(u[s], u[s], ACT.Relu).then_inc(relu_ready, 1)
                for s, m in enumerate(names):
                    act.wait_ge(centred, n(s))
                    nc.scalar.activation(usq[s], u[s], ACT.Square).then_inc(usq_ready, 1)
                for s, m in enumerate(names):
                    act.wait_ge(var_ready, n(s))
                    if not first:
                        act.wait_ge(rs2_ready, n(s) - S)
                    nc.scalar.activation(sd2[s], v2[s], ACT.Sqrt, bias=eps_mlp[:, 0:1], scale=1.0 / D).then_inc(sd2_ready, 1)
                last()

            def msg_sum(r, b):
                act.wait_ge(dsum_ps, r + 1)
                if not (isinstance(r, int) and r < 2):
                    act.wait_ge(adds_done, 16 * Q * (r - 1))
                nc.scalar.activation(dsum[b], ps_sum[:, 0:Q * D].rearrange("p (q d) -> p q d", d=D), ACT.Copy).then_inc(dsum_ready, 1)

            def msg_round(i, b, r):
                first = isinstance(r, int) and r == 0


                def between():
                    if not first:
                        msg_sum(r - 1, 1 - b)
                mlp(lambda s: NS * r + s + 1, NS, first, ("msg", "msg", "self"), between, lambda: None)

            by_pair(act, msg_round)
            msg_sum(ROUNDS - 1, 1)

            with act.Fori(0, ROUNDS // 2) as i:
                def final_norm():
                    for s in range(2):
                        act.wait_ge(f_cen, 2 * i + s + 1)
                        nc.scalar.activation(usq[s], e_y[s], ACT.Square).then_inc(f_sq, 1)
                    for s in range(2):
                        act.wait_ge(f_var, 2 * i + s + 1)
                        nc.scalar.activation(sd2[s], v2[s], ACT.Sqrt, bias=eps_out[:, 0:1], scale=1.0 / D).then_inc(f_sd, 1)
                mlp(lambda s: NS * ROUNDS + 2 * i + s + 1, 2, False, ("node", "node"), lambda: None, final_norm)

        @block.vector
        def _(dve):
            V = nc.vector
            chain = [0]

            def link(ins):
                chain[0] += 1
                ins.then_inc(prep, 1)
                dve.wait_ge(prep, chain[0])

            dve.wait_ge(in_loaded, 128)
            dve.wait_ge(const_all, 12)
            link(V.tensor_copy(src_f[:, :], src_t[:, :]))
            link(V.tensor_copy(dst_f[:, :], dst_t[:, :]))
            V.tensor_scalar(head_len[:, :], dst_f[:, 0:1], 0.0, None, ALU.mult).then_inc(ids_ready, 1)
            link(V.tensor_scalar(weight9[:, :], weight[:, :], 1.0 - ALPHA, None, ALU.mult))
            link(V.memset(same[:, :], 0.0))
            link(V.tensor_tensor(same[:, 1:T], dst_f[:, 1:T], dst_f[:, 0:T - 1], ALU.is_equal))
            link(V.tensor_tensor(scratch[:, :], dst_f[:, 0:T], dst_f[:, 1:T + 1], ALU.is_equal))
            link(V.tensor_scalar(before_all[:, :], dst_f[:, 0:T], float(XD), float(D), ALU.mult, ALU.add))
            link(V.scalar_tensor_tensor(lp_index[:, :], scratch[:, :], float(BIG), before_all[:, :], ALU.mult, ALU.add))
            dve.wait_ge(ids_ready, 1)
            link(V.tensor_tensor(scratch[:, :], dst_f[:, 0:T], dst_f[:, 0:1].to_broadcast([P, T]), ALU.is_equal))
            link(V.tensor_reduce(head_len[:, :], scratch[:, :], AX.X, ALU.add))
            link(V.tensor_tensor(fix_row[:, :], head_len[:, :], row0[:, :], ALU.add))
            link(V.tensor_copy(trash_f[:, :], trash_t[:, :]))
            link(V.tensor_scalar(center[:, :], ident[:, :], -1.0 / H, None, ALU.add))
            dve.wait_ge(weights_mm, 1)
            link(V.scalar_tensor_tensor(carry_sel[:, :], ps[0][:, 0:P], dst_f[:, T - 1:T], upper[:, :], ALU.is_equal, ALU.mult))
            V.tensor_copy(gate_v[:, 0:1], carry_sel[:, 0:1]).then_inc(graph_ready, 1)

            def lp_slots(i, b):
                g = 2 * i + b
                V.tensor_scalar(lp_slot[b][:, :], lp_index[:, ds(g * U, U)], 0.0, None, ALU.add).then_inc(lp_slots_ready, 1)
                V.tensor_scalar(row_slot[b][:, :], row_id[:, ds(g * U, U)], 0.0, None, ALU.add).then_inc(lp_slots_ready, 1)

            for b in range(2):
                lp_slots(0, b)
            dve.wait_ge(weights_loaded, 16 * 25)
            for k, m in enumerate(MLPS):
                link(V.tensor_scalar(wc[m][:, :], w1[m][:, :], cols[m][:, 1:2], None, ALU.mult))
            link(V.tensor_scalar(eps1[:, :], eps1[:, :], 1.0, None, ALU.add))
            link(V.tensor_scalar(g1["self"][:, :], g1["self"][:, :], eps1[:, 0:1], None, ALU.mult))
            link(V.tensor_scalar(beta1["self"][:, :], beta1["self"][:, :], eps1[:, 0:1], None, ALU.mult))
            dve.wait_ge(weights_mm, 3)
            for k, m in enumerate(MLPS):
                link(V.tensor_copy(c0[m][:, :], ps[1][:, k * D:(k + 1) * D]))
                link(V.tensor_copy(wc[m][:, :], ps[2][:, k * D:(k + 1) * D]))
            V.tensor_copy(gate_v[:, 1:2], wc["node"][:, 0:1]).then_inc(weights_ready, 1)

            def count_before(i, b):
                g = 2 * i + b
                V.tensor_scalar(src_slot[b][:, :], src_f[:, ds(g * U, U)], 0.0, None, ALU.add).then_inc(src_slot_ready, 1)
                dve.wait_ge(src_slot_ready, g + 1)
                if not (isinstance(i, int) and i == 0 and b == 0):
                    dve.wait_ge(before_kept, g)
                for c in range(U // Q):
                    bank = ps[6 + (b + c) % 2]
                    dve.wait_ge(eq_before_ps, U // Q * g + c + 1)
                    for t in range(Q):
                        k = c * Q + t
                        ins = V.scalar_tensor_tensor(bank[:, t * P:(t + 1) * P], bank[:, t * P:(t + 1) * P],
                                                     src_slot[b][:, k:k + 1], lower[:, :], ALU.is_equal, ALU.mult,
                                                     accum_out=before[:, k:k + 1])
                    ins.then_inc(before_done, 1)
                dve.wait_ge(before_done, U // Q * (g + 1))
                V.tensor_scalar(before_all[:, ds(g * U, U)], before[:, :], 1.0, None, ALU.min).then_inc(before_kept, 1)

            for b in range(2):
                count_before(0, b)
            with dve.Fori(1, PAIRS) as i:
                for b in range(2):
                    dve.wait_ge(lp_written[b], 16 * U * i)
                    lp_slots(i, b)
                    count_before(i, b)
            dve.wait_ge(before_kept, GROUPS)
            link(V.tensor_scalar(scratch[:, :], src_f[:, :], trash_f[:, 0:1], None, ALU.subtract))
            link(V.tensor_tensor(scratch[:, :], scratch[:, :], before_all[:, :], ALU.mult))
            V.tensor_tensor(add_row_t[:, :], src_f[:, :], scratch[:, :], ALU.subtract).then_inc(before_kept, 1)

            def scan_group(s, i, b):
                g = 2 * i + b
                if not (isinstance(i, int) and i == 0 and isinstance(s, int) and s == 0):
                    dve.wait_ge(sums_stored[b], 16 * (PAIRS * s + i))
                for t in range(U):
                    at = T * s + U * g + t
                    if not (isinstance(at, int) and at == 0):
                        dve.wait_ge(scanned, at)
                    prev = sums[b][:, t - 1, :] if t else sums[1 - b][:, U - 1, :]
                    V.scalar_tensor_tensor(sums[b][:, t, :], prev, same[:, ds(g * U + t, 1)], got[b][:, t, 0:D],
                                           ALU.mult, ALU.add).then_inc(scanned, 1)

            def pass0_group(i, b):
                g = 2 * i + b
                dve.wait_ge(gathered[b], 16 * U * (i + 1))
                if not (isinstance(i, int) and i == 0):
                    dve.wait_ge(idx_saved[b], 16 * i)
                V.tensor_copy(idx_out[b][:, :], got[b][:, :, D:XD].rearrange("p u o -> p (u o)").bitcast(i32)).then_inc(scaled0, 1)
                V.tensor_tensor(got[b][:, :, 0:D], got[b][:, :, 0:D], bc(weight[:, ds(g * U, U)], D), ALU.mult).then_inc(scaled0, 1)
                dve.wait_ge(scaled0, 3 * g + 2)
                V.tensor_scalar(xw[:, ds(g * U, U), :], got[b][:, :, 0:D], ALPHA, None, ALU.mult).then_inc(scaled0, 1)
                scan_group(0, i, b)

            def carries(s):
                dve.wait_ge(carry_ps, s + 1)
                if not (isinstance(s, int) and s == 0):
                    dve.wait_ge(carry_added, 16 * s)
                V.tensor_copy(carry[:, :], ps[0][:, 0:D]).then_inc(carry_ready, 1)

            for b in range(2):
                pass0_group(0, b)
            with dve.Fori(1, PAIRS) as i:
                for b in range(2):
                    pass0_group(i, b)
            carries(0)
            dve.wait_ge(scaled0, 3 * GROUPS)

            def one_step(s, source, target):
                with dve.Fori(0, PAIRS) as i:
                    for b in range(2):
                        g = 2 * i + b
                        done = 2 * GROUPS * (s - 1) + 2 * g
                        dve.wait_ge(gathered[b], 16 * U * (PAIRS * s + i + 1))
                        V.tensor_tensor(got[b][:, :, 0:D], got[b][:, :, 0:D], bc(weight9[:, ds(g * U, U)], D), ALU.mult).then_inc(scaled, 1)
                        dve.wait_ge(scaled, done + 1)
                        V.tensor_tensor(got[b][:, :, 0:D], got[b][:, :, 0:D], xw[:, ds(g * U, U), :], ALU.add).then_inc(scaled, 1)
                        dve.wait_ge(scaled, done + 2)
                        scan_group(s, i, b)
                carries(s)

            per_step(dve, one_step)

            def first_norm(i, b):
                    at = C_OPS * (2 * i + b)
                    dve.wait_ge(gathered[b], 16 * U * (PAIRS * K_STEPS + i + 1))
                    dve.wait_ge(c_act, 3 * (2 * i + b) + 1)
                    dve.wait_ge(sums_stored[b], 16 * PAIRS * K_STEPS)
                    if not (isinstance(i, int) and i == 0):
                        dve.wait_ge(x1_stored[b], 16 * i)
                    V.scalar_tensor_tensor(sums[b][:, :, :], got[b][:, :, 0:D], 1.0 - ALPHA, xrow[b], ALU.mult, ALU.add).then_inc(c_step, 1)
                    dve.wait_ge(c_step, at + 1)
                    V.tensor_reduce(c_mean[:, :], sums[b][:, :, :], AX.X, ALU.add).then_inc(c_step, 1)
                    dve.wait_ge(c_step, at + 2)
                    V.tensor_scalar(c_mean[:, :], c_mean[:, :], 1.0 / D, None, ALU.mult).then_inc(c_step, 1)
                    dve.wait_ge(c_step, at + 3)
                    V.tensor_tensor(sums[b][:, :, :], sums[b][:, :, :], bc(c_mean[:, :], D), ALU.subtract).then_inc(c_step, 1)
                    dve.wait_ge(c_act, 3 * (2 * i + b) + 2)
                    V.tensor_reduce(c_sq[:, :], xrow[b], AX.X, ALU.add).then_inc(c_step, 1)
                    dve.wait_ge(c_act, 3 * (2 * i + b) + 3)
                    V.reciprocal(c_rs[:, :], c_sd[:, :]).then_inc(c_step, 1)
                    dve.wait_ge(c_step, at + 6)
                    V.tensor_tensor(sums[b][:, :, :], sums[b][:, :, :], bc(c_rs[:, :], D), ALU.mult).then_inc(c_step, 1)

            for b in range(2):
                first_norm(0, b)
            with dve.Fori(1, PAIRS) as i:
                for b in range(2):
                    first_norm(i, b)

            def mlp(n, S, first, names, outs, free):
                for s, m in enumerate(names):
                    dve.wait_ge(sd_ready, n(s))
                    V.reciprocal(rs1[s], sd1[s]).then_inc(rs_ready, 1)
                for s, m in enumerate(names):
                    dve.wait_ge(rs_ready, n(s))
                    if not first:
                        dve.wait_ge(gained, n(s) - S)
                    q = ps_b[s][:, 0:Q * D].rearrange("p (q d) -> p q d", d=D)
                    V.tensor_tensor(u[s], q, bc(rs1[s], D), ALU.mult).then_inc(scaled_u, 1)
                for s, m in enumerate(names):
                    dve.wait_ge(scaled_u, n(s))
                    V.tensor_tensor(u[s], u[s], rows(c0[m][:, :], Q), ALU.add).then_inc(u_ready, 1)
                for s, m in enumerate(names):
                    dve.wait_ge(relu_ready, n(s))
                    V.tensor_reduce(mn[s], u[s], AX.X, ALU.add).then_inc(mean_sum, 1)
                for s, m in enumerate(names):
                    dve.wait_ge(mean_sum, n(s))
                    V.tensor_scalar(mn[s], mn[s], 1.0 / D, None, ALU.mult).then_inc(mean_ready, 1)
                for s, m in enumerate(names):
                    dve.wait_ge(mean_ready, n(s))
                    V.tensor_tensor(u[s], u[s], bc(mn[s], D), ALU.subtract).then_inc(centred, 1)
                for s, m in enumerate(names):
                    dve.wait_ge(usq_ready, n(s))
                    V.tensor_reduce(v2[s], usq[s], AX.X, ALU.add).then_inc(var_ready, 1)
                for s, m in enumerate(names):
                    dve.wait_ge(sd2_ready, n(s))
                    V.reciprocal(rs2[s], sd2[s]).then_inc(rs2_ready, 1)
                for s, m in enumerate(names):
                    dve.wait_ge(rs2_ready, n(s))
                    V.tensor_tensor(u[s], u[s], bc(rs2[s], D), ALU.mult).then_inc(normed, 1)
                for s, m in enumerate(names):
                    dve.wait_ge(normed, n(s))
                    free(s)
                    V.tensor_tensor(outs[s], u[s], rows(g1[m][:, :], Q), ALU.mult).then_inc(gained, 1)
                for s, m in enumerate(names):
                    dve.wait_ge(gained, n(s))
                    V.tensor_tensor(outs[s], outs[s], rows(beta1[m][:, :], Q), ALU.add).then_inc(out_ready, 1)

            dve.wait_ge(scanned, T * K_STEPS)
            link(V.memset(msum[1], 0.0))

            def msg_round(i, b, r):
                first = isinstance(r, int) and r == 0
                new = isinstance(r, int)
                dve.wait_ge(m_rows[b], 64 * (i + 1))
                dve.wait_ge(eq_ps, r + 1)
                if not new:
                    dve.wait_ge(dsum_ps, r - 1)
                V.tensor_tensor(eq[b], ps_eq[:, :].rearrange("p (q n) -> p q n", n=P), bc(m_val[b][:, :], P),
                                ALU.is_equal).then_inc(eq_ready, 1)

                def free(s):
                    if s == 0 and not first:
                        dve.wait_ge(scanned, T * K_STEPS + Q * r)
                    if s == 2 and not new:
                        dve.wait_ge(self_stored[b], 16 * i)
                mlp(lambda s: NS * r + s + 1, NS, first, ("msg", "msg", "self"), (msg_dst, msg[b], hself[b]), free)
                if not new:
                    dve.wait_ge(msum_stored[b], 16 * i)
                dve.wait_ge(out_ready, NS * r + 1)
                for t in range(Q):
                    dve.wait_ge(scanned, T * K_STEPS + Q * r + t)
                    prev = msum[b][:, t - 1, :] if t else msum[1 - b][:, Q - 1, :]
                    V.scalar_tensor_tensor(msum[b][:, t, :], prev, same[:, ds(r * Q + t, 1)] if not new else
                                           same[:, r * Q + t:r * Q + t + 1], msg_dst[:, t, :],
                                           ALU.mult, ALU.add).then_inc(scanned, 1)

            by_pair(dve, msg_round)
            carries(K_STEPS)

            def node_round(i, tails):
                n = lambda s: 2 * i + s + 1
                for s in range(2):
                    dve.wait_ge(e_loaded[s], 32 * (i + 1))
                    V.tensor_tensor(e_self[s], e_self[s], e_agg[s], ALU.add).then_inc(e_added, 1)
                for s in range(2):
                    dve.wait_ge(e_added, n(s))
                    dve.wait_ge(e_gathered[s], 16 * Q * (i + 1))
                    dve.wait_ge(t_done, NS * ROUNDS + 2 * i + s - 1)
                    V.tensor_tensor(e_x[s], e_self[s], e_got[s], ALU.add).then_inc(e_ready, 1)
                mlp(lambda s: NS * ROUNDS + 2 * i + s + 1, 2, False, ("node", "node"), e_y, lambda s: None)
                for s in range(2):
                    dve.wait_ge(out_ready, NS * ROUNDS + n(s))
                    dve.wait_ge(e_x1_loaded[s], 16 * (i + 1))
                    V.tensor_tensor(e_y[s], e_y[s], e_x1[s], ALU.add).then_inc(e_res, 1)
                for s in range(2):
                    dve.wait_ge(e_res, n(s))
                    V.tensor_reduce(mn[s], e_y[s], AX.X, ALU.add).then_inc(f_sum, 1)
                for s in range(2):
                    dve.wait_ge(f_sum, n(s))
                    V.tensor_scalar(mn[s], mn[s], 1.0 / D, None, ALU.mult).then_inc(f_mean, 1)
                for s in range(2):
                    dve.wait_ge(f_mean, n(s))
                    V.tensor_tensor(e_y[s], e_y[s], bc(mn[s], D), ALU.subtract).then_inc(f_cen, 1)
                for s in range(2):
                    dve.wait_ge(f_sq, n(s))
                    V.tensor_reduce(v2[s], usq[s], AX.X, ALU.add).then_inc(f_var, 1)
                for s in range(2):
                    dve.wait_ge(f_sd, n(s))
                    V.reciprocal(rs2[s], sd2[s]).then_inc(f_rs, 1)
                for s in range(2):
                    dve.wait_ge(f_rs, n(s))
                    if tails is not None:
                        dve.wait_ge(out_stored[s], 32 * i)
                        dve.wait_ge(tail_stored[s], 16 * tails)
                    V.tensor_tensor(e_out[s], e_y[s], bc(rs2[s], D), ALU.mult).then_inc(f_out, 1)

            node_round(0, None)
            with dve.Fori(1, TAILS + 1) as i:
                node_round(i, i)
            with dve.Fori(TAILS + 1, ROUNDS // 2) as i:
                node_round(i, TAILS)

        @block.tensor
        def _(pe):
            M = nc.tensor.matmul
            pe.wait_ge(const_all, 12)
            pe.wait_ge(ids_ready, 1)
            M(ps[0][:, 0:P], dst_f[:, 0:1].to_broadcast([P, P]), ident[:, :], start=True, stop=True).then_inc(weights_mm, 1)
            pe.wait_ge(weights_loaded, 16 * 25)
            for k, m in enumerate(MLPS):
                at = ps[1][:, k * D:(k + 1) * D]
                M(at, cols[m][:, 2:3].to_broadcast([P, P]), w1[m][:, :], start=True, stop=False)
                ins = M(at, ones[0:1, :], b1[m][:, :], start=False, stop=True)
            ins.then_inc(weights_mm, 1)
            pe.wait_ge(prep, WG_STEPS)
            for k, m in enumerate(MLPS):
                ins = M(ps[2][:, k * D:(k + 1) * D], center[:, :], wc[m][:, :], start=True, stop=True)
            ins.then_inc(weights_mm, 1)

            def src_rows(i, b):
                g = 2 * i + b
                pe.wait_ge(src_slot_ready, g + 1)
                for c in range(U // Q):
                    bank = ps[6 + (b + c) % 2]
                    if not (isinstance(i, int) and b == 0 and c < 2):
                        pe.wait_ge(before_done, U // Q * g + c - 1)
                    for t in range(Q):
                        k = c * Q + t
                        ins = M(bank[:, t * P:(t + 1) * P], src_slot[b][:, k:k + 1].to_broadcast([P, P]), ident[:, :], start=True, stop=True)
                    ins.then_inc(eq_before_ps, 1)

            for b in range(2):
                src_rows(0, b)
            with pe.Fori(1, PAIRS) as i:
                for b in range(2):
                    src_rows(i, b)

            def carries(s, tail):
                if tail is None:
                    pe.wait_ge(scanned, T * (s + 1))
                    tail = sums[1][:, U - 1, :]
                else:
                    pe.wait_ge(scanned, T * K_STEPS + T)
                if not (isinstance(s, int) and s == 0):
                    pe.wait_ge(carry_ready, s)
                M(ps[0][:, 0:D], carry_sel[:, :], tail, start=True, stop=True).then_inc(carry_ps, 1)

            pe.wait_ge(graph_ready, 1)
            carries(0, None)
            per_step(pe, lambda s, source, target: carries(s, None))
            pe.wait_ge(weights_ready, 1)
            pe.wait_ge(carry_ready, K_STEPS)
            pe.wait_ge(before_done, U // Q * GROUPS)

            def mlp(n, S, first, names, xs, ready, between):
                for s, m in enumerate(names):
                    ready(s)
                    if not first:
                        pe.wait_ge(sq_ready, n(s) - S)
                    pe.sem_inc(pe_passed, 1)
                    K = KIN[m]
                    for t in range(Q):
                        ins = nc.tensor.transpose(ps_a[s][0:K, t * P:(t + 1) * P], xs[s][:, t, :], ident[:, :])
                    ins.then_inc(t_done, 1)
                for s, m in enumerate(names):
                    pe.wait_ge(xt_ready, n(s))
                    if not first:
                        pe.wait_ge(scaled_u, n(s) - S)
                    M(ps_b[s][:, :], w0[m][:, :], xt[s][0:KIN[m], :], start=True, stop=True).then_inc(h_done, 1)
                between()
                for s, m in enumerate(names):
                    pe.wait_ge(ht_ready, n(s))
                    M(ps_a[s][:, :], center[:, :], ht[s], start=True, stop=True).then_inc(c_done, 1)
                for s, m in enumerate(names):
                    pe.wait_ge(sq_ready, n(s))
                    for t in range(Q):
                        M(ps_b[s][:, t * D:(t + 1) * D], ht[s][:, t * P:(t + 1) * P], wc[m][:, :], start=True, stop=True)
                    for t in range(Q):
                        ins = M(ps_b[s][:, Q * D + t:Q * D + t + 1], sq[s][:, t * P:(t + 1) * P], mean_h[:, :], start=True, stop=True)
                    ins.then_inc(q_done, 1)

            def column_sums(r, b):
                pe.wait_ge(out_ready, NS * r + 2)
                pe.wait_ge(eq_ready, r + 1)
                if not (isinstance(r, int) and r == 0):
                    pe.wait_ge(dsum_ready, r)
                for t in range(Q):
                    ins = M(ps_sum[:, t * D:(t + 1) * D], eq[b][:, t, :], msg[b][:, t, :], start=True, stop=True)
                ins.then_inc(dsum_ps, 1)

            def msg_round(i, b, r):
                first = isinstance(r, int) and r == 0

                def ready(s):
                    if s == 0:
                        pe.wait_ge(m_got[b], 16 * 2 * Q * (i + 1))
                        pe.wait_ge(m_rows[b], 64 * (i + 1))

                def between():
                    if not first:
                        pe.wait_ge(eq_ready, r)
                    for t in range(Q):
                        ins = M(ps_eq[:, t * P:(t + 1) * P], m_val[b][:, t:t + 1].to_broadcast([P, P]), ident[:, :], start=True, stop=True)
                    ins.then_inc(eq_ps, 1)
                    if not first:
                        column_sums(r - 1, 1 - b)
                mlp(lambda s: NS * r + s + 1, NS, first, ("msg", "msg", "self"), x_in[b], ready, between)

            by_pair(pe, msg_round)
            column_sums(ROUNDS - 1, 1)
            carries(K_STEPS, msum[1][:, Q - 1, :])
            pe.wait_ge(carry_ready, K_STEPS + 1)
            with pe.Fori(0, ROUNDS // 2) as i:
                mlp(lambda s: NS * ROUNDS + 2 * i + s + 1, 2, False, ("node", "node"), e_x,
                    lambda s: pe.wait_ge(e_ready, 2 * i + s + 1), lambda: None)


def kernel(**inputs):
    from concourse import bacc
    from concourse.bass_utils import run_bass_kernel_spmd

    nc = bacc.Bacc("TRN2", target_bir_lowering=False, num_devices=1)
    arrays, aps = {}, {}
    for name, value in inputs.items():
        a = np.ascontiguousarray(value)
        arrays[f"in_{name}"] = a
        aps[name] = nc.dram_tensor(f"in_{name}", a.shape, mybir.dt.from_np(a.dtype), kind="ExternalInput").ap()
    out = nc.dram_tensor("out_x", (N, D), mybir.dt.float32, kind="ExternalOutput").ap()
    build_program(nc, aps, out)
    result = run_bass_kernel_spmd(nc, [arrays], core_ids=[0])
    return result.results[0]["out_x"]
```

```python
import numpy as np
import concourse.bass as bass
from concourse import mybir
from contextlib import ExitStack

N = 50000
E = 50000
D = 64
DE = 32
H = 128
P = 128
T = 392
NP = P * T
FULL = N // T
REST = N - FULL * T
PAD_ID = NP - 1
U = 28
CH = 7
CHUNKS = U // CH
GROUPS = T // U
PAIRS = GROUPS // 2
ZROW = NP
TRASH = NP
K_STEPS = 10
ALPHA = 0.1
XD = D + 1
BIG = 1 << 22
Q = 4
ROUNDS = T // Q
NROUNDS = ROUNDS // 2
TAILS = REST // (2 * Q)
assert REST % (2 * Q) == 0
LEAD_M, LEAD_N = 6, 7
NS = 3
EPS_MLP = 1e-6
EPS_OUT = 1e-5

MLPS = ("msg", "self", "node")


def build_program(nc, A, out):
    fp32, i32 = mybir.dt.float32, mybir.dt.int32
    ALU, ACT, AX = mybir.AluOpType, mybir.ActivationFunctionType, mybir.AxisListType
    OFF = bass.IndirectOffsetOnAxis
    ds = bass.ds

    def dram(name, shape, dt=fp32):
        return nc.dram_tensor(name, shape, dt).ap()

    xa = dram("xa", [NP, XD])
    run_sums = [dram(f"run_sums{i}", [NP + P, D]) for i in range(2)]
    msg_sums = dram("msg_sums", [NP + P, D])
    x1 = dram("x1", [NP, D])
    aggr_src = dram("aggr_src", [NP + P, D])
    h_self = dram("h_self", [NP, D])
    edge_attr = dram("edge_attr", [NP, DE])
    src_ids = dram("src_ids", [NP], i32)
    dst_ids = dram("dst_ids", [NP], i32)
    src_vals = dram("src_vals", [NP])
    in_rows = dram("in_rows", [NP], i32)
    node_rows = dram("node_rows", [NP], i32)
    add_rows = dram("add_rows", [NP], i32)

    def grid(table):
        return table.rearrange("(p t) d -> p t d", t=T)

    def line(table):
        return table.rearrange("(p t) -> p t", t=T)

    xa_g, x1_g, self_g, ea_g = grid(xa), grid(x1), grid(h_self), grid(edge_attr)
    run_g = [grid(t[0:NP, :]) for t in run_sums]
    msg_g, agg_g = grid(msg_sums[0:NP, :]), grid(aggr_src[0:NP, :])
    xa_flat = xa.rearrange("n (d o) -> (n d) o", o=1)
    out_g = out[0:FULL * T, :].rearrange("(p t) d -> p t d", t=T)

    ctx = ExitStack()
    with ctx:
        ctx.enter_context(nc.allow_non_contiguous_dma(reason="a column of indices beside the rows, and the partitions' next ids"))

        def sb(name, shape, dt=fp32):
            return ctx.enter_context(nc.sbuf_tensor(name, shape, dt))

        def pb(name, shape, dt=fp32):
            return ctx.enter_context(nc.psum_tensor(name, shape, dt))

        def sem(name):
            return ctx.enter_context(nc.semaphore(name))

        src_t = sb("src_t", [P, T], i32)
        dst_t = sb("dst_t", [P, T + 1], i32)
        src_f = sb("src_f", [P, T])
        dst_f = sb("dst_f", [P, T + 1])
        weight = sb("weight", [P, T])
        weight9 = sb("weight9", [P, T])
        same = sb("same", [P, T])
        lp_index = sb("lp_index", [P, T], i32)
        row_id = sb("row_id", [P, T], i32)
        lp_slot = [sb(f"lp_slot{b}", [P, U], i32) for b in range(2)]
        row_slot = [sb(f"row_slot{b}", [P, U], i32) for b in range(2)]
        src_slot = [sb(f"src_slot{b}", [P, U]) for b in range(2)]
        before = sb("before", [P, U])
        before_all = sb("before_all", [P, T])
        scratch = sb("scratch", [P, T])
        add_row_t = sb("add_row_t", [P, T], i32)
        node_row_t = sb("node_row_t", [P, T], i32)
        head_len = sb("head_len", [P, 1])
        fix_row = sb("fix_row", [P, 1], i32)
        row0 = sb("row0", [P, 1], i32)
        trash_t = sb("trash_t", [P, 1], i32)
        trash_f = sb("trash_f", [P, 1])
        gate_v = sb("gate_v", [P, 2])
        part = sb("part", [P, 1])
        carry = sb("carry", [P, D])
        carry_sel = sb("carry_sel", [P, P])
        WG_STEPS = 17
        ident = sb("ident", [P, P])
        upper = sb("upper", [P, P])
        lower = sb("lower", [P, P])
        eqm = sb("eqm", [P, P])
        center = sb("center", [P, P])
        ones = sb("ones", [P, P])
        mean_h = sb("mean_h", [P, 1])
        eps_mlp = sb("eps_mlp", [P, 1])
        eps_out = sb("eps_out", [P, 1])
        zeros = sb("zeros", [P, U * D])
        xw = sb("xw", [P, T, D])
        got = [sb(f"got{b}", [P, U, XD]) for b in range(2)]
        idx = [sb(f"idx{b}", [P, U], i32) for b in range(2)]
        idx_out = [sb(f"idx_out{b}", [P, U], i32) for b in range(2)]
        sums = [sb(f"sums{b}", [P, U, D]) for b in range(2)]
        c_mean = sb("c_mean", [P, U])
        c_sq = sb("c_sq", [P, U])
        c_sd = sb("c_sd", [P, U])
        c_rs = sb("c_rs", [P, U])
        KIN = {"msg": D + DE, "self": D, "node": D}
        w0 = {m: sb(f"w0_{m}", [KIN[m], H]) for m in MLPS}
        w1 = {m: sb(f"w1_{m}", [H, D]) for m in MLPS}
        wc = {m: sb(f"wc_{m}", [H, D + 1]) for m in MLPS}
        cols = {m: sb(f"cols_{m}", [H, 3]) for m in MLPS}
        b1 = {m: sb(f"b1_{m}", [1, D]) for m in MLPS}
        c0 = {m: sb(f"c0_{m}", [P, D]) for m in MLPS}
        g1 = {m: sb(f"g1_{m}", [P, D]) for m in MLPS}
        beta1 = {m: sb(f"beta1_{m}", [P, D]) for m in MLPS}
        eps1 = sb("eps1", [P, 1])

        arena = xw[:, :, :].rearrange("p t d -> p (t d)")
        used = [0]

        def carve(*shape):
            size = int(np.prod(shape))
            a = arena[:, used[0]:used[0] + size]
            used[0] += size
            if len(shape) == 2:
                a = a.rearrange("p (a b) -> p a b", b=shape[1])
            return a

        xrow = [carve(U, D) for _ in range(2)]
        x_in = [[carve(Q, D + DE), carve(Q, D + DE), carve(Q, D)] for _ in range(2)]
        xt = [carve(Q * P) for _ in range(NS)]
        ht = [carve(Q * P) for _ in range(NS)]
        sq = [carve(Q * P) for _ in range(NS)]
        ht_more, sq_more = (x[:, :, :].rearrange("p q d -> p (q d)")[:, 0:Q * P] for x in xrow)
        u = [[carve(Q, D) for _ in range(NS)] for _ in range(2)]
        usq = [[carve(Q, D) for _ in range(NS)] for _ in range(2)]
        msq, v1, v1c, sd1, rs1, mn, v2, sd2, rs2 = ([carve(Q) for _ in range(NS)] for _ in range(9))
        msg = [carve(Q, D) for _ in range(2)]
        msg_dst = carve(Q, D)
        msum = [carve(Q, D) for _ in range(2)]
        hself = [carve(Q, D) for _ in range(2)]
        eq = [carve(Q, P) for _ in range(2)]
        dsum = [carve(Q, D) for _ in range(2)]
        e_self, e_agg, e_got, e_x1, e_x, e_y, e_sq, e_out = (
            [[carve(Q, D) for _ in range(2)] for _ in range(2)] for _ in range(8))
        f_mn, f_v2, f_sd_t, f_rs_t = ([carve(Q) for _ in range(2)] for _ in range(4))
        assert used[0] <= T * D
        m_src = [sb(f"m_src{b}", [P, Q], i32) for b in range(2)]
        m_dst = [sb(f"m_dst{b}", [P, Q], i32) for b in range(2)]
        m_add = [sb(f"m_add{b}", [P, Q], i32) for b in range(2)]
        m_val = [sb(f"m_val{b}", [P, Q]) for b in range(2)]
        e_idx = [[sb(f"e_idx{b}{s}", [P, Q], i32) for s in range(2)] for b in range(2)]

        ps = [pb(f"ps{i}", [P, 512]) for i in range(8)]
        ps_a, ps_b = ps[0:NS], ps[NS:2 * NS]
        QW = D + 2

        def bank(net, s, b):
            return ps[2 + 2 * b + s] if net is NODE else ps_b[s]

        def output(net, s, b):
            return bank(net, s, b)[:, 0:Q * QW].rearrange("p (q w) -> p q w", w=QW)

        def hidden_t(net, s, b):
            return (ht + [ht_more])[2 * b + s] if net is NODE else ht[s]

        def hidden_sq(net, s, b):
            return (sq + [sq_more])[2 * b + s] if net is NODE else sq[s]

        def depth(net):
            return 2 if net is NODE else 1

        ps_eq, ps_sum = ps[6], ps[7]

        names = """const_pads const_zeros const_all prep ids_ready zrow_ready graph_ready in_loaded weights_loaded
            weights_mm weights_ready xa_ready copied ids_written lp_slots_ready eq_before_ps before_done before_kept
            add_rows_written nodes_loaded node_rows_written scaled0 scaled scanned carry_ps carry_ready carry_added
            c_step c_act t_done xt_ready h_done ht_ready msq_ready v1_ready v1c_ready sq_ready q_done sd_ready rs_ready scaled_u u_ready
            relu_ready mean_sum centred usq_ready var_ready sd2_ready rs2_ready normed gained out_ready
            eq_ps eq_ready dsum_ps dsum_ready adds_done e_added e_ready e_res f_sum f_cen f_sq f_var f_sd
            f_rs f_out src_slot_ready pool_passed pe_passed sp_passed out_freed""".split()
        (const_pads, const_zeros, const_all, prep, ids_ready, zrow_ready, graph_ready, in_loaded, weights_loaded,
         weights_mm, weights_ready, xa_ready, copied, ids_written, lp_slots_ready, eq_before_ps, before_done, before_kept,
         add_rows_written, nodes_loaded, node_rows_written, scaled0, scaled, scanned, carry_ps, carry_ready,
         carry_added, c_step, c_act, t_done, xt_ready, h_done, ht_ready, msq_ready, v1_ready, v1c_ready, sq_ready, q_done, sd_ready,
         rs_ready, scaled_u, u_ready, relu_ready, mean_sum, centred, usq_ready, var_ready, sd2_ready,
         rs2_ready, normed, gained, out_ready, eq_ps, eq_ready, dsum_ps, dsum_ready, adds_done, e_added, e_ready,
         e_res, f_sum, f_cen, f_sq, f_var, f_sd, f_rs, f_out, src_slot_ready, pool_passed, pe_passed, sp_passed, out_freed) = [sem(n) for n in names]
        (lp_written, idx_loaded, idx_saved, x_loaded, x1_stored, m_idx, m_rows, m_val_loaded, m_got,
         m_add_loaded, msum_stored, self_stored, e_idx_loaded, e_loaded, e_x1_loaded, e_gathered, out_stored,
         tail_stored) = [
            [sem(f"{n}{b}") for b in range(2)] for n in
            ("lp_written idx_loaded idx_saved x_loaded x1_stored m_idx m_rows m_val_loaded m_got "
             "m_add_loaded msum_stored self_stored e_idx_loaded e_loaded e_x1_loaded e_gathered out_stored "
             "tail_stored").split()]
        gathered = [[sem(f"gathered{b}{c}") for c in range(CHUNKS)] for b in range(2)]
        sums_stored = [[sem(f"sums_stored{b}{c}") for c in range(CHUNKS)] for b in range(2)]

        block = ctx.enter_context(nc.Block())

        def per_step(eng, body):
            with eng.Fori(0, (K_STEPS - 2) // 2) as pair:
                body(2 * pair + 1, 0, 1)
                body(2 * pair + 2, 1, 0)
            body(K_STEPS - 1, 0, 1)

        LAST = 1
        C_OPS = 7

        def rounds(eng, total, lead, tail, body):
            for r in range(lead):
                body(r, r % 2)
            with eng.Fori(0, (total - lead) // 2) as k:
                for b in range(2):
                    body(2 * k + lead + b, (lead + b) % 2)
            for r in range(total, total + tail):
                body(r, r % 2)

        def live(x, total):
            return not isinstance(x, int) or 0 <= x < total

        def later(x, by):
            return not isinstance(x, int) or x >= by

        MSG = (0, ("msg", "msg", "self"), ROUNDS)
        NODE = (NS * ROUNDS, ("node", "node"), NROUNDS)

        def items(net, x):
            before, names, total = net
            if live(x, total):
                for s, m in enumerate(names):
                    yield s, m, before + len(names) * x + s + 1

        def since(net, x, n, d):
            return n - d * len(net[1]) if net[0] or later(x, d) else None

        def wait_old(eng, signal, value):
            if value is not None:
                eng.wait_ge(signal, value)

        M_TAIL, N_TAIL = 5, 4

        def bc(a, n):
            return a.unsqueeze(2).to_broadcast([P, a.shape[1], n])

        def rows(a, q):
            return a.unsqueeze(1).to_broadcast([P, q, a.shape[1]])

        @block.sync
        def _(sp):
            sp.wait_ge(const_pads, 3)
            for t, a in ((src_t, A["src"]), (dst_t, A["dst"]), (weight, A["edge_weight"])):
                sp.dma_start(t[0:FULL, 0:T], a[0:FULL * T].rearrange("(p t) -> p t", t=T)).then_inc(in_loaded, 16)
                sp.dma_start(t[FULL:FULL + 1, 0:REST], a[FULL * T:N].rearrange("(p t) -> p t", p=1)).then_inc(in_loaded, 16)
            sp.dma_start(dst_t[0:FULL - 1, T:T + 1],
                         A["dst"][T:FULL * T].rearrange("(p t) -> p t", t=T)[:, 0:1]).then_inc(in_loaded, 16)
            sp.dma_start(dst_t[FULL - 1:FULL, T:T + 1],
                         A["dst"][FULL * T:FULL * T + 1].rearrange("(p t) -> p t", p=1)).then_inc(in_loaded, 16)
            sp.wait_ge(zrow_ready, 1)
            sp.dma_start(xa_g[:, :, D:XD].bitcast(i32), node_row_t[:, :].unsqueeze(2)).then_inc(xa_ready, 16)
            sp.dma_start(xa[0:N, 0:D], A["x"][:, :]).then_inc(xa_ready, 16)
            sp.wait_ge(const_zeros, 1)
            sp.dma_start(xa[N:N + P, 0:D], zeros[:, 0:D]).then_inc(xa_ready, 16)
            sp.dma_start(xa[N + P:NP, 0:D], zeros[0:NP - N - P, 0:D]).then_inc(xa_ready, 16)
            for t in (*run_sums, msg_sums, aggr_src):
                sp.dma_start(t[NP:NP + P, :], zeros[:, 0:D]).then_inc(copied, 16)
            sp.wait_ge(ids_ready, 1)
            sp.dma_start(line(src_ids), src_t[:, :]).then_inc(ids_written, 16)
            sp.dma_start(line(dst_ids), dst_t[:, 0:T]).then_inc(ids_written, 16)
            sp.dma_start(line(src_vals), src_f[:, :]).then_inc(ids_written, 16)
            sp.wait_ge(ids_written, 48)
            for b in range(2):
                sp.dma_start(idx[b][:, :], line(src_ids)[:, b * U:(b + 1) * U]).then_inc(idx_loaded[b], 16)
            sp.dma_start(edge_attr[0:E, :].rearrange("(a b) d -> a (b d)", b=25),
                         A["edge_attr_32"].rearrange("(a b) d -> a (b d)", b=25)).then_inc(copied, 16)
            sp.dma_start(edge_attr[N:N + P, :], zeros[:, 0:DE]).then_inc(copied, 16)
            sp.dma_start(edge_attr[N + P:NP, :], zeros[0:NP - N - P, 0:DE]).then_inc(copied, 16)
            for g in range(GROUPS):
                sp.dma_start(agg_g[:, g * U:(g + 1) * U, :],
                             zeros[:, :].rearrange("p (u d) -> p u d", d=D)).then_inc(copied, 16)
            for b in range(2):
                sp.wait_ge(lp_written[b], 16 * U * PAIRS)
            sp.dma_start(node_row_t[:, :].unsqueeze(2), xa_g[:, :, D:XD].bitcast(i32)).then_inc(nodes_loaded, 16)
            sp.wait_ge(nodes_loaded, 16)
            sp.dma_start(line(node_rows), node_row_t[:, :]).then_inc(node_rows_written, 16)
            sp.wait_ge(before_kept, GROUPS + 1)
            sp.dma_start(line(add_rows), add_row_t[:, :]).then_inc(add_rows_written, 16)

            def fill_idx(s, i, b, source):
                for c in range(CHUNKS):
                    sp.wait_ge(gathered[b][c], 16 * CH * (PAIRS * s + i))
                sp.dma_start(idx[b][:, :], line(source)[:, ds((2 * i + b) * U, U)]).then_inc(idx_loaded[b], 16)

            def store_sums(table, s, i, b):
                for c in range(CHUNKS):
                    sp.wait_ge(scanned, T * s + U * (2 * i + b) + CH * (c + 1))
                    sp.dma_start(run_g[table][:, ds((2 * i + b) * U + c * CH, CH), :],
                                 sums[b][:, c * CH:(c + 1) * CH, :]).then_inc(sums_stored[b][c], 16)

            def pass0_out(i, b):
                store_sums(0, 0, i, b)
                sp.wait_ge(scaled0, 3 * (2 * i + b) + 1)
                sp.sem_inc(sp_passed, 1)
                sp.dma_start(line(in_rows)[:, ds((2 * i + b) * U, U)], idx_out[b][:, :]).then_inc(idx_saved[b], 16)

            with sp.Fori(1, PAIRS) as i:
                for b in range(2):
                    fill_idx(0, i, b, src_ids)
                    pass0_out(i - 1, b)
            for b in range(2):
                pass0_out(PAIRS - 1, b)
            for b in range(2):
                sp.wait_ge(idx_saved[b], 16 * PAIRS)

            def one_step(s, source, target):
                for b in range(2):
                    for c in range(CHUNKS):
                        sp.wait_ge(gathered[b][c], 16 * CH * PAIRS * s)
                    sp.dma_start(idx[b][:, :], line(in_rows)[:, b * U:(b + 1) * U]).then_inc(idx_loaded[b], 16)

                with sp.Fori(1, PAIRS) as i:
                    for b in range(2):
                        fill_idx(s, i, b, in_rows)
                        store_sums(target, s, i - 1, b)
                for b in range(2):
                    store_sums(target, s, PAIRS - 1, b)

            per_step(sp, one_step)

            sp.wait_ge(node_rows_written, 16)

            def load_x(i, b):
                sp.dma_start(xrow[b], xa_g[:, ds((2 * i + b) * U, U), 0:D]).then_inc(x_loaded[b], 16)

            def store_x1(i, b):
                sp.wait_ge(c_step, C_OPS * (2 * i + b + 1))
                sp.dma_start(x1_g[:, ds((2 * i + b) * U, U), :], sums[b][:, :, :]).then_inc(x1_stored[b], 16)

            for b in range(2):
                for c in range(CHUNKS):
                    sp.wait_ge(gathered[b][c], 16 * CH * PAIRS * K_STEPS)
                sp.dma_start(idx[b][:, :], line(node_rows)[:, b * U:(b + 1) * U]).then_inc(idx_loaded[b], 16)
                load_x(0, b)
            with sp.Fori(1, PAIRS) as i:
                for b in range(2):
                    fill_idx(K_STEPS, i, b, node_rows)
                    store_x1(i - 1, b)
                    load_x(i, b)
            for b in range(2):
                store_x1(PAIRS - 1, b)
            for b in range(2):
                sp.wait_ge(x1_stored[b], 16 * PAIRS)
            sp.wait_ge(ids_written, 48)
            sp.wait_ge(add_rows_written, 16)
            sp.wait_ge(copied, 16 * (4 + 3 + GROUPS))

            def msg_round(r, b):
                if live(r, ROUNDS):
                    if later(r, 2):
                        sp.wait_ge(m_got[b], 16 * Q * (r - b))
                    sp.dma_start(m_src[b][:, :], line(src_ids)[:, ds(r * Q, Q)]).then_inc(m_idx[b], 16)
                    sp.dma_start(m_dst[b][:, :], line(dst_ids)[:, ds(r * Q, Q)]).then_inc(m_idx[b], 16)
                    if later(r, 2):
                        sp.wait_ge(t_done, NS * (r - 1))
                    for t in range(2):
                        sp.dma_start(x_in[b][t][:, :, D:D + DE], ea_g[:, ds(r * Q, Q), :]).then_inc(m_rows[b], 16)
                    sp.dma_start(x_in[b][2], x1_g[:, ds(r * Q, Q), :]).then_inc(m_rows[b], 16)
                y = r - 2
                if live(y, ROUNDS):
                    if later(y, 2):
                        sp.wait_ge(eq_ready, y - 1)
                    sp.dma_start(m_val[b][:, :], line(src_vals)[:, ds(y * Q, Q)]).then_inc(m_val_loaded[b], 16)
                y = r - 4
                if live(y, ROUNDS):
                    if later(y, 2):
                        sp.wait_ge(adds_done, 16 * Q * (y - 1))
                        sp.sem_inc(sp_passed, 1)
                    sp.dma_start(m_add[b][:, :], line(add_rows)[:, ds(y * Q, Q)]).then_inc(m_add_loaded[b], 16)
                    sp.wait_ge(scanned, T * K_STEPS + Q * (y + 1))
                    sp.dma_start(msg_g[:, ds(y * Q, Q), :], msum[b]).then_inc(msum_stored[b], 16)
                    sp.wait_ge(out_ready, NS * (y + 1))
                    sp.dma_start(self_g[:, ds(y * Q, Q), :], hself[b]).then_inc(self_stored[b], 16)

            rounds(sp, ROUNDS, LEAD_M, 4, msg_round)
            for b in range(2):
                sp.wait_ge(msum_stored[b], 16 * ROUNDS // 2)
                sp.wait_ge(self_stored[b], 16 * ROUNDS // 2)
            sp.wait_ge(adds_done, 16 * T)

            def node_round(r, b):
                if live(r, NROUNDS):
                    if later(r, 2):
                        sp.wait_ge(e_ready, 2 * (r - 1))
                    for s in range(2):
                        at = (2 * r + s) * Q
                        sp.dma_start(e_idx[b][s][:, :], line(node_rows)[:, ds(at, Q)]).then_inc(e_idx_loaded[b], 16)
                        sp.dma_start(e_self[b][s], self_g[:, ds(at, Q), :]).then_inc(e_loaded[b], 16)
                        sp.dma_start(e_agg[b][s], agg_g[:, ds(at, Q), :]).then_inc(e_loaded[b], 16)
                y = r - 2
                if live(y, NROUNDS):
                    if later(y, 2):
                        sp.wait_ge(e_res, 2 * (y - 1))
                    for s in range(2):
                        sp.dma_start(e_x1[b][s], x1_g[:, ds((2 * y + s) * Q, Q), :]).then_inc(e_x1_loaded[b], 16)
                y = r - 5
                if live(y, NROUNDS):
                    for s in range(2):
                        sp.wait_ge(f_out, 2 * y + s + 1)
                        at = (2 * y + s) * Q
                        for p0, p1 in ((0, 112), (112, FULL)):
                            sp.dma_start(out_g[p0:p1, ds(at, Q), :], e_out[1 - b][s][p0:p1]).then_inc(out_stored[1 - b], 16)

            def node_tail(y, b):
                for s in range(2):
                    sp.dma_start(out[ds(FULL * T + (2 * y + s) * Q, Q), :].rearrange("(o q) d -> o q d", o=1),
                                 e_out[b][s][FULL:FULL + 1]).then_inc(tail_stored[b], 16)

            def free_out(y, b, tails):
                if live(y, NROUNDS):
                    sp.wait_ge(out_stored[b], 32 * (y - b + 2))
                    sp.sem_inc(sp_passed, 1)
                    if tails:
                        sp.wait_ge(tail_stored[b], 16 * (y - b + 2))
                    sp.sem_inc(out_freed, 1)

            def with_tail(r, b):
                node_round(r, b)
                if live(r - 5, TAILS):
                    node_tail(r - 5, 1 - b)
                free_out(r - 6, b, live(r - 6, TAILS))

            def without_tail(r, b):
                node_round(r, b)
                free_out(r - 6, b, False)

            for r in range(LEAD_N):
                with_tail(r, r % 2)
            pairs, odd = divmod(TAILS + 5 - LEAD_N, 2)
            with sp.Fori(0, pairs) as k:
                for b in range(2):
                    with_tail(2 * k + LEAD_N + b, (LEAD_N + b) % 2)
            first = LEAD_N + 2 * pairs
            for r in range(first, first + odd):
                with_tail(r, r % 2)
            first += odd
            for b in range(2):
                sp.wait_ge(tail_stored[b], 16 * 2 * ((TAILS + 1 - b) // 2))
            with sp.Fori(0, (NROUNDS - first) // 2) as k:
                for b in range(2):
                    without_tail(2 * k + first + b, (first + b) % 2)
            for r in range(first + (NROUNDS - first) // 2 * 2, NROUNDS + 5):
                without_tail(r, r % 2)
            for b in range(2):
                sp.wait_ge(out_stored[b], 16 * 4 * ((NROUNDS + 1 - b) // 2))

        @block.gpsimd
        def _(pool):
            nc.gpsimd.memset(src_t[:, :], PAD_ID).then_inc(const_pads, 1)
            nc.gpsimd.memset(dst_t[:, :], PAD_ID).then_inc(const_pads, 1)
            nc.gpsimd.memset(weight[:, :], 0.0).then_inc(const_pads, 1)
            nc.gpsimd.memset(node_row_t[:, :], ZROW).then_inc(zrow_ready, 1)
            nc.gpsimd.memset(zeros[:, :], 0.0).then_inc(const_zeros, 1)
            nc.gpsimd.iota(row_id[:, :], [[1, T]], base=0, channel_multiplier=T).then_inc(const_all, 1)
            nc.gpsimd.iota(row0[:, :], [[1, 1]], base=-1, channel_multiplier=T).then_inc(const_all, 1)
            nc.gpsimd.iota(trash_t[:, :], [[0, 1]], base=TRASH, channel_multiplier=1).then_inc(const_all, 1)
            nc.gpsimd.memset(ident[:, :], 0.0).then_inc(const_all, 1)
            nc.gpsimd.memset(ones[:, :], 1.0).then_inc(const_all, 1)
            nc.gpsimd.memset(mean_h[:, :], 1.0 / H).then_inc(const_all, 1)
            nc.gpsimd.memset(eps_mlp[:, :], EPS_MLP).then_inc(const_all, 1)
            nc.gpsimd.memset(eps_out[:, :], EPS_OUT).then_inc(const_all, 1)
            nc.gpsimd.memset(sums[1][:, :, :], 0.0).then_inc(const_all, 1)
            pool.wait_ge(const_all, 9)
            nc.gpsimd.affine_select(out=ident[:, :], in_=ident[:, :], compare_op=ALU.not_equal, fill=1.0,
                                    base=0, pattern=[[-1, P]], channel_multiplier=1).then_inc(const_all, 1)
            nc.gpsimd.affine_select(out=upper[:, :], in_=ones[:, :], compare_op=ALU.is_gt, fill=0.0,
                                    base=0, pattern=[[1, P]], channel_multiplier=-1).then_inc(const_all, 1)
            nc.gpsimd.affine_select(out=lower[:, :], in_=ones[:, :], compare_op=ALU.is_gt, fill=0.0,
                                    base=0, pattern=[[-1, P]], channel_multiplier=1).then_inc(const_all, 1)

            def passed():
                pool.sem_inc(pool_passed, 1)

            pool.wait_ge(xa_ready, 16 * 4)
            with pool.Fori(0, PAIRS) as i:
                for b in range(2):
                    pool.wait_ge(lp_slots_ready, 2 * (2 * i + b + 1))
                    passed()
                    for t in range(U):
                        pool.indirect_dma_start(xa_flat, OFF(ap=lp_slot[b][:, t:t + 1], axis=0), row_slot[b][:, t:t + 1].bitcast(fp32),
                                                None, bounds_check=NP * XD - 1, oob_is_err=False).then_inc(lp_written[b], 16)
            for b in range(2):
                pool.wait_ge(lp_written[b], 16 * U * PAIRS)

            def gather_group(table, width, s, i, b):
                pool.wait_ge(idx_loaded[b], 16 * (PAIRS * s + i + 1))
                passed()
                for t in range(U):
                    pool.indirect_dma_start(got[b][:, t, 0:width], None, table,
                                            OFF(ap=idx[b][:, t:t + 1], axis=0)).then_inc(gathered[b][t // CH], 16)

            def end_of_pass(s, table):
                for b in range(2):
                    for c in range(CHUNKS):
                        pool.wait_ge(sums_stored[b][c], 16 * PAIRS * (s + 1))
                pool.wait_ge(carry_ready, s + 1)
                passed()
                pool.indirect_dma_start(table, OFF(ap=fix_row[:, 0:1], axis=0), carry[:, :], None,
                                        compute_op=ALU.add).then_inc(carry_added, 16)
                pool.wait_ge(carry_added, 16 * (s + 1))
                passed()

            def one_pass(table, width, s):
                for b in range(2):
                    gather_group(table, width, s, 0, b)
                with pool.Fori(1, PAIRS) as i:
                    for b in range(2):
                        pool.wait_ge(scanned, T * s + U * (2 * i + b - 1))
                        gather_group(table, width, s, i, b)

            one_pass(xa[:, :], XD, 0)
            pool.wait_ge(graph_ready, 1)
            pool.wait_ge(copied, 16 * (4 + 3 + GROUPS))
            end_of_pass(0, run_sums[0][:, :])

            def one_step(s, source, target):
                one_pass(run_sums[source][:, :], D, s)
                end_of_pass(s, run_sums[target][:, :])

            per_step(pool, one_step)

            for b in range(2):
                gather_group(run_sums[LAST][:, :], D, K_STEPS, 0, b)
            with pool.Fori(1, PAIRS) as i:
                for b in range(2):
                    pool.wait_ge(c_step, C_OPS * (2 * i + b - 2) + 1)
                    gather_group(run_sums[LAST][:, :], D, K_STEPS, i, b)
            for b in range(2):
                pool.wait_ge(x1_stored[b], 16 * PAIRS)
            passed()

            def msg_round(r, b):
                y = r - 5
                if live(r, ROUNDS):
                    pool.wait_ge(m_idx[b], 16 * (r - b + 2))
                    if later(r, 2):
                        pool.wait_ge(t_done, NS * (r - 1))
                    passed()
                for t in range(Q):
                    if live(r, ROUNDS):
                        pool.indirect_dma_start(x_in[b][0][:, t, 0:D], None, x1[:, :],
                                                OFF(ap=m_src[b][:, t:t + 1], axis=0)).then_inc(m_got[b], 16)
                        pool.indirect_dma_start(x_in[b][1][:, t, 0:D], None, x1[:, :],
                                                OFF(ap=m_dst[b][:, t:t + 1], axis=0)).then_inc(m_got[b], 16)
                    if live(y, ROUNDS):
                        pool.wait_ge(dsum_ready, y + 1)
                        pool.wait_ge(m_add_loaded[1 - b], 8 * (y - (1 - b) + 2))
                        if not (isinstance(y, int) and y == 0 and t == 0):
                            pool.wait_ge(adds_done, 16 * (Q * y + t))
                        passed()
                        pool.indirect_dma_start(aggr_src[:, :], OFF(ap=m_add[1 - b][:, t:t + 1], axis=0),
                                                dsum[1 - b][:, t, :], None, compute_op=ALU.add).then_inc(adds_done, 16)

            rounds(pool, ROUNDS, LEAD_M, M_TAIL, msg_round)
            for b in range(2):
                pool.wait_ge(msum_stored[b], 16 * ROUNDS // 2)
            pool.wait_ge(carry_ready, K_STEPS + 1)
            pool.indirect_dma_start(msg_sums[:, :], OFF(ap=fix_row[:, 0:1], axis=0), carry[:, :], None,
                                    compute_op=ALU.add).then_inc(carry_added, 16)
            pool.wait_ge(carry_added, 16 * (K_STEPS + 1))

            def node_gathers(r, b):
                pool.wait_ge(e_idx_loaded[b], 16 * (r - b + 2))
                if later(r, 2):
                    pool.wait_ge(e_ready, 2 * (r - 1))
                passed()
                for s in range(2):
                    for t in range(Q):
                        pool.indirect_dma_start(e_got[b][s][:, t, :], None, msg_sums[:, :],
                                                OFF(ap=e_idx[b][s][:, t:t + 1], axis=0)).then_inc(e_gathered[b], 16)

            rounds(pool, NROUNDS, LEAD_N, 0, node_gathers)

        @block.scalar
        def _(act):
            for m in MLPS:
                w = {k: A[f"L1_gnn_{m}_{k}"] for k in ("W0", "b0", "g0", "beta0", "W1", "b1", "g1", "beta1")}
                act.dma_start(w0[m][:, :], w["W0"]).then_inc(weights_loaded, 16)
                act.dma_start(w1[m][:, :], w["W1"]).then_inc(weights_loaded, 16)
                for c, k in enumerate(("b0", "g0", "beta0")):
                    act.dma_start(cols[m][:, c:c + 1], w[k].rearrange("(p o) -> p o", o=1)).then_inc(weights_loaded, 16)
                act.dma_start(b1[m][:, :], w["b1"].unsqueeze(0)).then_inc(weights_loaded, 16)
                act.dma_start(g1[m][:, :], w["g1"].partition_broadcast(P)).then_inc(weights_loaded, 16)
                act.dma_start(beta1[m][:, :], w["beta1"].partition_broadcast(P)).then_inc(weights_loaded, 16)
            act.dma_start(eps1[:, :], A["L1_gnn_eps"].partition_broadcast(P)).then_inc(weights_loaded, 16)
            act.wait_ge(const_all, 12)
            act.wait_ge(weights_ready, 1)

            with act.Fori(0, PAIRS) as i:
                for b in range(2):
                    g = 2 * i + b
                    act.wait_ge(x_loaded[b], 16 * (i + 1))
                    nc.scalar.activation(xrow[b], xrow[b], ACT.Copy, scale=1.0 + ALPHA).then_inc(c_act, 1)
                    act.wait_ge(c_step, C_OPS * g + 4)
                    nc.scalar.activation(xrow[b], sums[b][:, :, :], ACT.Square).then_inc(c_act, 1)
                    act.wait_ge(c_step, C_OPS * g + 5)
                    nc.scalar.activation(c_sd[:, :], c_sq[:, :], ACT.Sqrt, bias=eps_out[:, 0:1], scale=1.0 / D).then_inc(c_act, 1)

            def transposed_rows(net, x):
                for s, m, n in items(net, x):
                    act.wait_ge(t_done, n)
                    wait_old(act, h_done, since(net, x, n, 1))
                    nc.scalar.activation(xt[s][0:KIN[m], :], ps_a[s][0:KIN[m], :], ACT.Copy).then_inc(xt_ready, 1)

            def hidden(net, x, b):
                for s, m, n in items(net, x):
                    act.wait_ge(h_done, n)
                    wait_old(act, q_done, since(net, x, n, depth(net)))
                    nc.scalar.activation(hidden_t(net, s, b), bank(net, s, b)[:, :], ACT.Relu, bias=cols[m][:, 0:1]).then_inc(ht_ready, 1)

            def squares(net, x, b):
                for s, m, n in items(net, x):
                    act.wait_ge(ht_ready, n)
                    nc.scalar.activation(hidden_sq(net, s, b), hidden_t(net, s, b), ACT.Square).then_inc(sq_ready, 1)

            def mean_squares(net, x, b):
                for s, m, n in items(net, x):
                    act.wait_ge(q_done, n)
                    wait_old(act, v1_ready, since(net, x, n, 1))
                    nc.scalar.activation(msq[s], output(net, s, b)[:, :, D], ACT.Square).then_inc(msq_ready, 1)

            def hidden_dev(net, x):
                for s, m, n in items(net, x):
                    act.wait_ge(v1c_ready, n)
                    wait_old(act, rs_ready, since(net, x, n, 1))
                    nc.scalar.activation(sd1[s], v1c[s], ACT.Sqrt, bias=eps_mlp[:, 0:1]).then_inc(sd_ready, 1)

            def relu(net, x, b):
                for s, m, n in items(net, x):
                    act.wait_ge(u_ready, n)
                    nc.scalar.activation(u[b][s], u[b][s], ACT.Relu).then_inc(relu_ready, 1)

            def u_squares(net, x, b):
                for s, m, n in items(net, x):
                    act.wait_ge(centred, n)
                    wait_old(act, var_ready, since(net, x, n, 2))
                    nc.scalar.activation(usq[b][s], u[b][s], ACT.Square).then_inc(usq_ready, 1)

            def u_dev(net, x):
                for s, m, n in items(net, x):
                    act.wait_ge(var_ready, n)
                    wait_old(act, rs2_ready, since(net, x, n, 1))
                    nc.scalar.activation(sd2[s], v2[s], ACT.Sqrt, bias=eps_mlp[:, 0:1], scale=1.0 / D).then_inc(sd2_ready, 1)

            def msg_sum(y, b):
                if live(y, ROUNDS):
                    act.wait_ge(dsum_ps, y + 1)
                    if later(y, 2):
                        act.wait_ge(adds_done, 16 * Q * (y - 1))
                    nc.scalar.activation(dsum[b], ps_sum[:, 0:Q * D].rearrange("p (q d) -> p q d", d=D), ACT.Copy).then_inc(dsum_ready, 1)

            def msg_round(r, b):
                mean_squares(MSG, r - 1, 1 - b)
                transposed_rows(MSG, r)
                hidden_dev(MSG, r - 1)
                u_dev(MSG, r - 2)
                relu(MSG, r - 1, 1 - b)
                hidden(MSG, r, b)
                squares(MSG, r, b)
                u_squares(MSG, r - 1, 1 - b)
                msg_sum(r - 3, 1 - b)

            rounds(act, ROUNDS, LEAD_M, M_TAIL, msg_round)

            def final_squares(y, b):
                if live(y, NROUNDS):
                    for s in range(2):
                        act.wait_ge(f_cen, 2 * y + s + 1)
                        if later(y, 2):
                            act.wait_ge(f_var, 2 * (y - 2) + s + 1)
                        nc.scalar.activation(e_sq[b][s], e_y[b][s], ACT.Square).then_inc(f_sq, 1)

            def final_dev(y):
                if live(y, NROUNDS):
                    for s in range(2):
                        act.wait_ge(f_var, 2 * y + s + 1)
                        if later(y, 1):
                            act.wait_ge(f_rs, 2 * (y - 1) + s + 1)
                        nc.scalar.activation(f_sd_t[s], f_v2[s], ACT.Sqrt, bias=eps_out[:, 0:1], scale=1.0 / D).then_inc(f_sd, 1)

            def node_round(r, b):
                mean_squares(NODE, r - 2, b)
                transposed_rows(NODE, r)
                hidden_dev(NODE, r - 2)
                u_dev(NODE, r - 3)
                relu(NODE, r - 2, b)
                final_dev(r - 4)
                hidden(NODE, r, b)
                squares(NODE, r, b)
                u_squares(NODE, r - 2, b)
                final_squares(r - 3, 1 - b)

            rounds(act, NROUNDS, LEAD_N, N_TAIL, node_round)

        @block.vector
        def _(dve):
            V = nc.vector
            chain = [0]

            def link(ins):
                chain[0] += 1
                ins.then_inc(prep, 1)
                dve.wait_ge(prep, chain[0])

            dve.wait_ge(in_loaded, 128)
            dve.wait_ge(const_all, 12)
            link(V.tensor_copy(src_f[:, :], src_t[:, :]))
            link(V.tensor_copy(dst_f[:, :], dst_t[:, :]))
            V.tensor_scalar(head_len[:, :], dst_f[:, 0:1], 0.0, None, ALU.mult).then_inc(ids_ready, 1)
            link(V.tensor_scalar(weight9[:, :], weight[:, :], 1.0 - ALPHA, None, ALU.mult))
            link(V.memset(same[:, :], 0.0))
            link(V.tensor_tensor(same[:, 1:T], dst_f[:, 1:T], dst_f[:, 0:T - 1], ALU.is_equal))
            link(V.tensor_tensor(scratch[:, :], dst_f[:, 0:T], dst_f[:, 1:T + 1], ALU.is_equal))
            link(V.tensor_scalar(before_all[:, :], dst_f[:, 0:T], float(XD), float(D), ALU.mult, ALU.add))
            link(V.scalar_tensor_tensor(lp_index[:, :], scratch[:, :], float(BIG), before_all[:, :], ALU.mult, ALU.add))
            dve.wait_ge(ids_ready, 1)
            link(V.tensor_tensor(scratch[:, :], dst_f[:, 0:T], dst_f[:, 0:1].to_broadcast([P, T]), ALU.is_equal))
            link(V.tensor_reduce(head_len[:, :], scratch[:, :], AX.X, ALU.add))
            link(V.tensor_tensor(fix_row[:, :], head_len[:, :], row0[:, :], ALU.add))
            link(V.tensor_copy(trash_f[:, :], trash_t[:, :]))
            link(V.tensor_scalar(center[:, :], ident[:, :], -1.0 / H, None, ALU.add))
            dve.wait_ge(weights_mm, 1)
            link(V.scalar_tensor_tensor(carry_sel[:, :], ps[0][:, 0:P], dst_f[:, T - 1:T], upper[:, :], ALU.is_equal, ALU.mult))
            V.tensor_copy(gate_v[:, 0:1], carry_sel[:, 0:1]).then_inc(graph_ready, 1)

            def lp_slots(i, b):
                g = 2 * i + b
                V.tensor_scalar(lp_slot[b][:, :], lp_index[:, ds(g * U, U)], 0.0, None, ALU.add).then_inc(lp_slots_ready, 1)
                V.tensor_scalar(row_slot[b][:, :], row_id[:, ds(g * U, U)], 0.0, None, ALU.add).then_inc(lp_slots_ready, 1)

            for b in range(2):
                lp_slots(0, b)
            dve.wait_ge(weights_loaded, 16 * 25)
            for k, m in enumerate(MLPS):
                link(V.tensor_scalar(wc[m][:, 0:D], w1[m][:, :], cols[m][:, 1:2], None, ALU.mult))
            link(V.tensor_scalar(eps1[:, :], eps1[:, :], 1.0, None, ALU.add))
            link(V.tensor_scalar(g1["self"][:, :], g1["self"][:, :], eps1[:, 0:1], None, ALU.mult))
            link(V.tensor_scalar(beta1["self"][:, :], beta1["self"][:, :], eps1[:, 0:1], None, ALU.mult))
            dve.wait_ge(weights_mm, 3)
            for k, m in enumerate(MLPS):
                link(V.tensor_copy(c0[m][:, :], ps[1][:, k * D:(k + 1) * D]))
                link(V.tensor_copy(wc[m][:, 0:D], ps[2][:, k * D:(k + 1) * D]))
                link(V.tensor_copy(wc[m][:, D:D + 1], mean_h[:, :]))
            V.tensor_copy(gate_v[:, 1:2], wc["node"][:, 0:1]).then_inc(weights_ready, 1)

            def count_before(i, b):
                g = 2 * i + b
                V.tensor_scalar(src_slot[b][:, :], src_f[:, ds(g * U, U)], 0.0, None, ALU.add).then_inc(src_slot_ready, 1)
                dve.wait_ge(src_slot_ready, g + 1)
                if not (isinstance(i, int) and i == 0 and b == 0):
                    dve.wait_ge(before_kept, g)
                for c in range(U // Q):
                    bank = ps[6 + (b + c) % 2]
                    dve.wait_ge(eq_before_ps, U // Q * g + c + 1)
                    for t in range(Q):
                        k = c * Q + t
                        ins = V.scalar_tensor_tensor(bank[:, t * P:(t + 1) * P], bank[:, t * P:(t + 1) * P],
                                                     src_slot[b][:, k:k + 1], lower[:, :], ALU.is_equal, ALU.mult,
                                                     accum_out=before[:, k:k + 1])
                    ins.then_inc(before_done, 1)
                dve.wait_ge(before_done, U // Q * (g + 1))
                V.tensor_scalar(before_all[:, ds(g * U, U)], before[:, :], 1.0, None, ALU.min).then_inc(before_kept, 1)

            for b in range(2):
                count_before(0, b)
            with dve.Fori(1, PAIRS) as i:
                for b in range(2):
                    dve.wait_ge(lp_written[b], 16 * U * i)
                    lp_slots(i, b)
                    count_before(i, b)
            dve.wait_ge(before_kept, GROUPS)
            link(V.tensor_scalar(scratch[:, :], src_f[:, :], trash_f[:, 0:1], None, ALU.subtract))
            link(V.tensor_tensor(scratch[:, :], scratch[:, :], before_all[:, :], ALU.mult))
            V.tensor_tensor(add_row_t[:, :], src_f[:, :], scratch[:, :], ALU.subtract).then_inc(before_kept, 1)

            def scan_chunk(s, i, b, c):
                g = 2 * i + b
                if not (isinstance(i, int) and i == 0 and isinstance(s, int) and s == 0):
                    dve.wait_ge(sums_stored[b][c], 16 * (PAIRS * s + i))
                for t in range(c * CH, c * CH + CH):
                    at = T * s + U * g + t
                    if not (isinstance(at, int) and at == 0):
                        dve.wait_ge(scanned, at)
                    prev = sums[b][:, t - 1, :] if t else sums[1 - b][:, U - 1, :]
                    V.scalar_tensor_tensor(sums[b][:, t, :], prev, same[:, ds(g * U + t, 1)], got[b][:, t, 0:D],
                                           ALU.mult, ALU.add).then_inc(scanned, 1)

            def pass0_group(i, b):
                g = 2 * i + b
                for c in range(CHUNKS):
                    dve.wait_ge(gathered[b][c], 16 * CH * (i + 1))
                if not (isinstance(i, int) and i == 0):
                    dve.wait_ge(idx_saved[b], 16 * i)
                V.tensor_copy(idx_out[b][:, :], got[b][:, :, D:XD].rearrange("p u o -> p (u o)").bitcast(i32)).then_inc(scaled0, 1)
                V.tensor_tensor(got[b][:, :, 0:D], got[b][:, :, 0:D], bc(weight[:, ds(g * U, U)], D), ALU.mult).then_inc(scaled0, 1)
                dve.wait_ge(scaled0, 3 * g + 2)
                V.tensor_scalar(xw[:, ds(g * U, U), :], got[b][:, :, 0:D], ALPHA, None, ALU.mult).then_inc(scaled0, 1)
                for c in range(CHUNKS):
                    scan_chunk(0, i, b, c)

            def carries(s):
                dve.wait_ge(carry_ps, s + 1)
                if not (isinstance(s, int) and s == 0):
                    dve.wait_ge(carry_added, 16 * s)
                V.tensor_copy(carry[:, :], ps[0][:, 0:D]).then_inc(carry_ready, 1)

            for b in range(2):
                pass0_group(0, b)
            with dve.Fori(1, PAIRS) as i:
                for b in range(2):
                    pass0_group(i, b)
            carries(0)
            dve.wait_ge(scaled0, 3 * GROUPS)

            def one_step(s, source, target):
                with dve.Fori(0, PAIRS) as i:
                    for b in range(2):
                        g = 2 * i + b
                        for c in range(CHUNKS):
                            done = 2 * CHUNKS * (GROUPS * (s - 1) + g) + 2 * c
                            at = ds(g * U + c * CH, CH)
                            rows_c = got[b][:, c * CH:(c + 1) * CH, 0:D]
                            dve.wait_ge(gathered[b][c], 16 * CH * (PAIRS * s + i + 1))
                            V.tensor_tensor(rows_c, rows_c, bc(weight9[:, at], D), ALU.mult).then_inc(scaled, 1)
                            dve.wait_ge(scaled, done + 1)
                            V.tensor_tensor(rows_c, rows_c, xw[:, at, :], ALU.add).then_inc(scaled, 1)
                            dve.wait_ge(scaled, done + 2)
                            scan_chunk(s, i, b, c)
                carries(s)

            per_step(dve, one_step)

            def first_norm(i, b):
                    at = C_OPS * (2 * i + b)
                    for c in range(CHUNKS):
                        dve.wait_ge(gathered[b][c], 16 * CH * (PAIRS * K_STEPS + i + 1))
                    dve.wait_ge(c_act, 3 * (2 * i + b) + 1)
                    for c in range(CHUNKS):
                        dve.wait_ge(sums_stored[b][c], 16 * PAIRS * K_STEPS)
                    if not (isinstance(i, int) and i == 0):
                        dve.wait_ge(x1_stored[b], 16 * i)
                    V.scalar_tensor_tensor(sums[b][:, :, :], got[b][:, :, 0:D], 1.0 - ALPHA, xrow[b], ALU.mult, ALU.add).then_inc(c_step, 1)
                    dve.wait_ge(c_step, at + 1)
                    V.tensor_reduce(c_mean[:, :], sums[b][:, :, :], AX.X, ALU.add).then_inc(c_step, 1)
                    dve.wait_ge(c_step, at + 2)
                    V.tensor_scalar(c_mean[:, :], c_mean[:, :], 1.0 / D, None, ALU.mult).then_inc(c_step, 1)
                    dve.wait_ge(c_step, at + 3)
                    V.tensor_tensor(sums[b][:, :, :], sums[b][:, :, :], bc(c_mean[:, :], D), ALU.subtract).then_inc(c_step, 1)
                    dve.wait_ge(c_act, 3 * (2 * i + b) + 2)
                    V.tensor_reduce(c_sq[:, :], xrow[b], AX.X, ALU.add).then_inc(c_step, 1)
                    dve.wait_ge(c_act, 3 * (2 * i + b) + 3)
                    V.reciprocal(c_rs[:, :], c_sd[:, :]).then_inc(c_step, 1)
                    dve.wait_ge(c_step, at + 6)
                    V.tensor_tensor(sums[b][:, :, :], sums[b][:, :, :], bc(c_rs[:, :], D), ALU.mult).then_inc(c_step, 1)

            for b in range(2):
                first_norm(0, b)
            with dve.Fori(1, PAIRS) as i:
                for b in range(2):
                    first_norm(i, b)

            def hidden_var(net, x, b):
                for s, m, n in items(net, x):
                    dve.wait_ge(msq_ready, n)
                    V.scalar_tensor_tensor(v1[s], msq[s], -1.0, output(net, s, b)[:, :, D + 1], ALU.mult, ALU.add).then_inc(v1_ready, 1)
                for s, m, n in items(net, x):
                    dve.wait_ge(v1_ready, n)
                    wait_old(dve, sd_ready, since(net, x, n, 1))
                    V.tensor_scalar(v1c[s], v1[s], 0.0, None, ALU.max).then_inc(v1c_ready, 1)

            def hidden_rs(net, x):
                for s, m, n in items(net, x):
                    dve.wait_ge(sd_ready, n)
                    V.reciprocal(rs1[s], sd1[s]).then_inc(rs_ready, 1)

            def affine(net, x, b):
                for s, m, n in items(net, x):
                    dve.wait_ge(rs_ready, n)
                    wait_old(dve, gained, since(net, x, n, 2))
                    V.tensor_tensor(u[b][s], output(net, s, b)[:, :, 0:D], bc(rs1[s], D), ALU.mult).then_inc(scaled_u, 1)
                for s, m, n in items(net, x):
                    dve.wait_ge(scaled_u, n)
                    V.tensor_tensor(u[b][s], u[b][s], rows(c0[m][:, :], Q), ALU.add).then_inc(u_ready, 1)

            def u_sums(net, x, b):
                for s, m, n in items(net, x):
                    dve.wait_ge(relu_ready, n)
                    V.tensor_reduce(mn[s], u[b][s], AX.X, ALU.add).then_inc(mean_sum, 1)

            def u_centre(net, x, b):
                for s, m, n in items(net, x):
                    dve.wait_ge(mean_sum, n)
                    V.scalar_tensor_tensor(u[b][s], bc(mn[s], D), -1.0 / D, u[b][s], ALU.mult, ALU.add).then_inc(centred, 1)

            def u_vars(net, x, b):
                for s, m, n in items(net, x):
                    dve.wait_ge(usq_ready, n)
                    wait_old(dve, sd2_ready, since(net, x, n, 1))
                    V.tensor_reduce(v2[s], usq[b][s], AX.X, ALU.add).then_inc(var_ready, 1)

            def u_rs(net, x):
                for s, m, n in items(net, x):
                    dve.wait_ge(sd2_ready, n)
                    V.reciprocal(rs2[s], sd2[s]).then_inc(rs2_ready, 1)

            def gain(net, x, b, outs, free):
                for s, m, n in items(net, x):
                    dve.wait_ge(rs2_ready, n)
                    free(s)
                    for t in range(Q):
                        ins = V.scalar_tensor_tensor(outs[s][:, t, :], u[b][s][:, t, :], rs2[s][:, t:t + 1], g1[m][:, :],
                                                     ALU.mult, ALU.mult)
                    ins.then_inc(gained, 1)

            def bias(net, x, outs):
                for s, m, n in items(net, x):
                    dve.wait_ge(gained, n)
                    V.tensor_tensor(outs[s], outs[s], rows(beta1[m][:, :], Q), ALU.add).then_inc(out_ready, 1)

            dve.wait_ge(scanned, T * K_STEPS)
            link(V.memset(msum[1], 0.0))

            def msg_scan(y, b):
                if live(y, ROUNDS):
                    if later(y, 2):
                        dve.wait_ge(msum_stored[b], 8 * (y - b))
                    dve.wait_ge(out_ready, NS * y + 1)
                    for t in range(Q):
                        dve.wait_ge(scanned, T * K_STEPS + Q * y + t)
                        prev = msum[b][:, t - 1, :] if t else msum[1 - b][:, Q - 1, :]
                        V.scalar_tensor_tensor(msum[b][:, t, :], prev, same[:, ds(y * Q + t, 1)], msg_dst[:, t, :],
                                               ALU.mult, ALU.add).then_inc(scanned, 1)

            def equal_src(y, b):
                if live(y, ROUNDS):
                    dve.wait_ge(m_val_loaded[b], 8 * (y - b + 2))
                    dve.wait_ge(eq_ps, y + 1)
                    if later(y, 2):
                        dve.wait_ge(dsum_ps, y - 1)
                    V.tensor_tensor(eq[b], ps_eq[:, :].rearrange("p (q n) -> p q n", n=P), bc(m_val[b][:, :], P),
                                    ALU.is_equal).then_inc(eq_ready, 1)

            def msg_round(r, b):
                y = r - 2
                outs = (msg_dst, msg[b], hself[b])

                def free(s):
                    if s == 0 and later(y, 1):
                        dve.wait_ge(scanned, T * K_STEPS + Q * y)
                    if s == 1 and later(y, 2):
                        dve.wait_ge(dsum_ps, y - 1)
                    if s == 2 and later(y, 2):
                        dve.wait_ge(self_stored[b], 8 * (y - b))
                hidden_var(MSG, r - 1, 1 - b)
                u_vars(MSG, y, b)
                hidden_rs(MSG, r - 1)
                affine(MSG, r - 1, 1 - b)
                u_rs(MSG, y)
                gain(MSG, y, b, outs, free)
                u_sums(MSG, r - 1, 1 - b)
                bias(MSG, y, outs)
                u_centre(MSG, r - 1, 1 - b)
                msg_scan(y, b)
                equal_src(y, b)

            rounds(dve, ROUNDS, LEAD_M, M_TAIL, msg_round)
            carries(K_STEPS)

            def node_inputs(r, b):
                if live(r, NROUNDS):
                    for s in range(2):
                        dve.wait_ge(e_loaded[b], 32 * (r - b + 2))
                        V.tensor_tensor(e_self[b][s], e_self[b][s], e_agg[b][s], ALU.add).then_inc(e_added, 1)
                    for s in range(2):
                        dve.wait_ge(e_added, 2 * r + s + 1)
                        dve.wait_ge(e_gathered[b], 16 * Q * (r - b + 2))
                        if later(r, 2):
                            dve.wait_ge(t_done, NS * ROUNDS + 2 * (r - 2) + s + 1)
                        V.tensor_tensor(e_x[b][s], e_self[b][s], e_got[b][s], ALU.add).then_inc(e_ready, 1)

            def residual(y, b):
                if live(y, NROUNDS):
                    for s in range(2):
                        dve.wait_ge(out_ready, NS * ROUNDS + 2 * y + s + 1)
                        dve.wait_ge(e_x1_loaded[b], 16 * (y - b + 2))
                        V.tensor_tensor(e_y[b][s], e_y[b][s], e_x1[b][s], ALU.add).then_inc(e_res, 1)
                    for s in range(2):
                        dve.wait_ge(e_res, 2 * y + s + 1)
                        V.tensor_reduce(f_mn[s], e_y[b][s], AX.X, ALU.add).then_inc(f_sum, 1)
                    for s in range(2):
                        dve.wait_ge(f_sum, 2 * y + s + 1)
                        V.scalar_tensor_tensor(e_y[b][s], bc(f_mn[s], D), -1.0 / D, e_y[b][s], ALU.mult, ALU.add).then_inc(f_cen, 1)

            def final_vars(y, b):
                if live(y, NROUNDS):
                    for s in range(2):
                        dve.wait_ge(f_sq, 2 * y + s + 1)
                        if later(y, 1):
                            dve.wait_ge(f_sd, 2 * (y - 1) + s + 1)
                        V.tensor_reduce(f_v2[s], e_sq[b][s], AX.X, ALU.add).then_inc(f_var, 1)

            def final_norm(y, b):
                if live(y, NROUNDS):
                    for s in range(2):
                        dve.wait_ge(f_sd, 2 * y + s + 1)
                        V.reciprocal(f_rs_t[s], f_sd_t[s]).then_inc(f_rs, 1)
                    for s in range(2):
                        dve.wait_ge(f_rs, 2 * y + s + 1)
                        if later(y, 2):
                            dve.wait_ge(out_freed, y - 1)
                        V.tensor_tensor(e_out[b][s], e_y[b][s], bc(f_rs_t[s], D), ALU.mult).then_inc(f_out, 1)

            def node_round(r, b):
                node_inputs(r, b)
                hidden_var(NODE, r - 2, b)
                final_vars(r - 4, b)
                hidden_rs(NODE, r - 2)
                u_vars(NODE, r - 3, 1 - b)
                affine(NODE, r - 2, b)
                u_rs(NODE, r - 3)
                gain(NODE, r - 3, 1 - b, e_y[1 - b], lambda s: None)
                final_norm(r - 4, b)
                bias(NODE, r - 3, e_y[1 - b])
                u_sums(NODE, r - 2, b)
                residual(r - 3, 1 - b)
                u_centre(NODE, r - 2, b)

            rounds(dve, NROUNDS, LEAD_N, N_TAIL, node_round)

        @block.tensor
        def _(pe):
            M = nc.tensor.matmul
            pe.wait_ge(const_all, 12)
            pe.wait_ge(ids_ready, 1)
            M(ps[0][:, 0:P], dst_f[:, 0:1].to_broadcast([P, P]), ident[:, :], start=True, stop=True).then_inc(weights_mm, 1)
            pe.wait_ge(weights_loaded, 16 * 25)
            for k, m in enumerate(MLPS):
                at = ps[1][:, k * D:(k + 1) * D]
                M(at, cols[m][:, 2:3].to_broadcast([P, P]), w1[m][:, :], start=True, stop=False)
                ins = M(at, ones[0:1, :], b1[m][:, :], start=False, stop=True)
            ins.then_inc(weights_mm, 1)
            pe.wait_ge(prep, WG_STEPS)
            for k, m in enumerate(MLPS):
                ins = M(ps[2][:, k * D:(k + 1) * D], center[:, :], wc[m][:, 0:D], start=True, stop=True)
            ins.then_inc(weights_mm, 1)

            def src_rows(i, b):
                g = 2 * i + b
                pe.wait_ge(src_slot_ready, g + 1)
                for c in range(U // Q):
                    bank = ps[6 + (b + c) % 2]
                    if not (isinstance(i, int) and b == 0 and c < 2):
                        pe.wait_ge(before_done, U // Q * g + c - 1)
                    for t in range(Q):
                        k = c * Q + t
                        ins = nc.tensor.transpose(bank[:, t * P:(t + 1) * P], src_slot[b][:, k:k + 1].to_broadcast([P, P]), ident[:, :])
                    ins.then_inc(eq_before_ps, 1)

            for b in range(2):
                src_rows(0, b)
            with pe.Fori(1, PAIRS) as i:
                for b in range(2):
                    src_rows(i, b)

            def carries(s, tail):
                if tail is None:
                    pe.wait_ge(scanned, T * (s + 1))
                    tail = sums[1][:, U - 1, :]
                else:
                    pe.wait_ge(scanned, T * K_STEPS + T)
                if not (isinstance(s, int) and s == 0):
                    pe.wait_ge(carry_ready, s)
                M(ps[0][:, 0:D], carry_sel[:, :], tail, start=True, stop=True).then_inc(carry_ps, 1)

            pe.wait_ge(graph_ready, 1)
            carries(0, None)
            per_step(pe, lambda s, source, target: carries(s, None))
            pe.wait_ge(weights_ready, 1)
            pe.wait_ge(carry_ready, K_STEPS)
            pe.wait_ge(before_done, U // Q * GROUPS)

            def transposes(net, x, xs, ready):
                for s, m, n in items(net, x):
                    ready(s)
                    wait_old(pe, xt_ready, since(net, x, n, 1))
                    pe.sem_inc(pe_passed, 1)
                    for t in range(Q):
                        ins = nc.tensor.transpose(ps_a[s][0:KIN[m], t * P:(t + 1) * P], xs[s][:, t, :], ident[:, :])
                    ins.then_inc(t_done, 1)

            def hidden(net, x, b):
                for s, m, n in items(net, x):
                    pe.wait_ge(xt_ready, n)
                    wait_old(pe, scaled_u, since(net, x, n, depth(net)))
                    M(bank(net, s, b)[:, :], w0[m][:, :], xt[s][0:KIN[m], :], start=True, stop=True).then_inc(h_done, 1)

            def second_layer(net, x, b):
                for s, m, n in items(net, x):
                    pe.wait_ge(ht_ready, n)
                    for t in range(Q):
                        M(output(net, s, b)[:, t, 0:D + 1], hidden_t(net, s, b)[:, t * P:(t + 1) * P], wc[m][:, :], start=True, stop=True)

            def hidden_squares(net, x, b):
                for s, m, n in items(net, x):
                    pe.wait_ge(sq_ready, n)
                    for t in range(Q):
                        ins = M(output(net, s, b)[:, t, D + 1:D + 2], hidden_sq(net, s, b)[:, t * P:(t + 1) * P], mean_h[:, :], start=True, stop=True)
                    ins.then_inc(q_done, 1)

            def src_columns(y, b):
                if live(y, ROUNDS):
                    pe.wait_ge(m_val_loaded[b], 8 * (y - b + 2))
                    if later(y, 1):
                        pe.wait_ge(eq_ready, y)
                    for t in range(Q):
                        ins = nc.tensor.transpose(ps_eq[:, t * P:(t + 1) * P], m_val[b][:, t:t + 1].to_broadcast([P, P]), ident[:, :])
                    ins.then_inc(eq_ps, 1)

            def column_sums(y, b):
                if live(y, ROUNDS):
                    pe.wait_ge(out_ready, NS * y + 2)
                    pe.wait_ge(eq_ready, y + 1)
                    if later(y, 1):
                        pe.wait_ge(dsum_ready, y)
                    for t in range(Q):
                        ins = M(ps_sum[:, t * D:(t + 1) * D], eq[b][:, t, :], msg[b][:, t, :], start=True, stop=True)
                    ins.then_inc(dsum_ps, 1)

            def msg_round(r, b):
                def ready(s):
                    pe.wait_ge(m_got[b], 16 * Q * (r - b + 2))
                    pe.wait_ge(m_rows[b], 24 * (r - b + 2))
                src_columns(r - 2, b)
                transposes(MSG, r, x_in[b], ready)
                hidden(MSG, r, b)
                column_sums(r - 3, 1 - b)
                second_layer(MSG, r, b)
                hidden_squares(MSG, r, b)

            rounds(pe, ROUNDS, LEAD_M, M_TAIL, msg_round)
            carries(K_STEPS, msum[1][:, Q - 1, :])
            pe.wait_ge(carry_ready, K_STEPS + 1)

            def node_round(r, b):
                transposes(NODE, r, e_x[b], lambda s: pe.wait_ge(e_ready, 2 * r + s + 1))
                second_layer(NODE, r - 1, 1 - b)
                hidden(NODE, r, b)
                hidden_squares(NODE, r - 1, 1 - b)

            rounds(pe, NROUNDS, LEAD_N, N_TAIL, node_round)


def kernel(**inputs):
    from concourse import bacc
    from concourse.bass_utils import run_bass_kernel_spmd

    nc = bacc.Bacc("TRN2", target_bir_lowering=False, num_devices=1)
    arrays, aps = {}, {}
    for name, value in inputs.items():
        a = np.ascontiguousarray(value)
        arrays[f"in_{name}"] = a
        aps[name] = nc.dram_tensor(f"in_{name}", a.shape, mybir.dt.from_np(a.dtype), kind="ExternalInput").ap()
    out = nc.dram_tensor("out_x", (N, D), mybir.dt.float32, kind="ExternalOutput").ap()
    build_program(nc, aps, out)
    result = run_bass_kernel_spmd(nc, [arrays], core_ids=[0])
    return result.results[0]["out_x"]
```

```python
import numpy as np
import concourse.bass as bass
from concourse import mybir
from contextlib import ExitStack

N = 50000
E = 50000
D = 64
DE = 32
H = 128
P = 128
T = 392
NP = P * T
FULL = N // T
REST = N - FULL * T
PAD_ID = NP - 1
U = 28
CH = 4
CHUNKS = U // CH
GROUPS = T // U
PAIRS = GROUPS // 2
ZROW = NP
TRASH = NP
K_STEPS = 10
ALPHA = 0.1
XD = D + 1
BIG = 1 << 22
Q = 4
ROUNDS = T // Q
NROUNDS = ROUNDS // 2
TAILS = REST // (2 * Q)
assert REST % (2 * Q) == 0
LEAD_M, LEAD_N = 8, 9
NS = 2
ADD_LAG = 6
SELF_R = 2 * U // (NS * Q)
assert PAIRS % 2 == 1 and SELF_R == 7 and U == 28
X_PARTS = 20
EPS_MLP = 1e-6
EPS_OUT = 1e-5

MLPS = ("msg", "self", "node")


def build_program(nc, A, out):
    fp32, i32 = mybir.dt.float32, mybir.dt.int32
    ALU, ACT, AX = mybir.AluOpType, mybir.ActivationFunctionType, mybir.AxisListType
    OFF = bass.IndirectOffsetOnAxis
    ds = bass.ds

    def dram(name, shape, dt=fp32):
        return nc.dram_tensor(name, shape, dt).ap()

    xa = dram("xa", [NP, XD])
    run_sums = [dram(f"run_sums{i}", [NP + P, D]) for i in range(2)]
    msg_sums = dram("msg_sums", [NP + P, D])
    x1 = dram("x1", [NP, D])
    aggr_src = dram("aggr_src", [NP + P, D])
    edge_attr = dram("edge_attr", [NP, DE])
    src_ids = dram("src_ids", [NP], i32)
    dst_ids = dram("dst_ids", [NP], i32)
    src_vals = dram("src_vals", [NP])
    in_rows = dram("in_rows", [NP], i32)
    node_rows = dram("node_rows", [NP], i32)
    add_rows = dram("add_rows", [NP], i32)

    def grid(table):
        return table.rearrange("(p t) d -> p t d", t=T)

    def line(table):
        return table.rearrange("(p t) -> p t", t=T)

    xa_g, x1_g, ea_g = grid(xa), grid(x1), grid(edge_attr)
    run_g = [grid(t[0:NP, :]) for t in run_sums]
    msg_g, agg_g = grid(msg_sums[0:NP, :]), grid(aggr_src[0:NP, :])
    xa_flat = xa.rearrange("n (d o) -> (n d) o", o=1)
    out_g = out[0:FULL * T, :].rearrange("(p t) d -> p t d", t=T)

    ctx = ExitStack()
    with ctx:
        ctx.enter_context(nc.allow_non_contiguous_dma(reason="a column of indices beside the rows, and the partitions' next ids"))

        def sb(name, shape, dt=fp32):
            return ctx.enter_context(nc.sbuf_tensor(name, shape, dt))

        def pb(name, shape, dt=fp32):
            return ctx.enter_context(nc.psum_tensor(name, shape, dt))

        def sem(name):
            return ctx.enter_context(nc.semaphore(name))

        src_t = sb("src_t", [P, T], i32)
        dst_t = sb("dst_t", [P, T + 1], i32)
        src_f = sb("src_f", [P, T])
        dst_f = sb("dst_f", [P, T + 1])
        weight = sb("weight", [P, T])
        weight9 = sb("weight9", [P, T])
        same = sb("same", [P, T])
        lp_index = sb("lp_index", [P, T], i32)
        row_id = sb("row_id", [P, T], i32)
        lp_slot = [sb(f"lp_slot{b}", [P, U], i32) for b in range(2)]
        row_slot = [sb(f"row_slot{b}", [P, U], i32) for b in range(2)]
        src_slot = [sb(f"src_slot{b}", [P, U]) for b in range(2)]
        before = sb("before", [P, U])
        before_all = sb("before_all", [P, T])
        scratch = sb("scratch", [P, T])
        add_row_t = sb("add_row_t", [P, T], i32)
        node_row_t = sb("node_row_t", [P, T], i32)
        head_len = sb("head_len", [P, 1])
        fix_row = sb("fix_row", [P, 1], i32)
        row0 = sb("row0", [P, 1], i32)
        trash_t = sb("trash_t", [P, 1], i32)
        trash_f = sb("trash_f", [P, 1])
        gate_v = sb("gate_v", [P, 2])
        carry = sb("carry", [P, D])
        carry_sel = sb("carry_sel", [P, P])
        WG_STEPS = 17
        ident = sb("ident", [P, P])
        upper = sb("upper", [P, P])
        lower = sb("lower", [P, P])
        center = sb("center", [P, P])
        ones = sb("ones", [P, P])
        mean_h = sb("mean_h", [P, 1])
        eps_mlp = sb("eps_mlp", [P, 1])
        eps_out = sb("eps_out", [P, 1])
        zeros = sb("zeros", [P, U * D])
        xw = sb("xw", [P, T, D])
        got = [sb(f"got{b}", [P, U, XD]) for b in range(2)]
        idx = [sb(f"idx{b}", [P, U], i32) for b in range(2)]
        idx_out = [sb(f"idx_out{b}", [P, U], i32) for b in range(2)]
        sums = [sb(f"sums{b}", [P, U, D]) for b in range(2)]
        c_mean = sb("c_mean", [P, U])
        c_sq = sb("c_sq", [P, U])
        c_sd = sb("c_sd", [P, U])
        c_rs = sb("c_rs", [P, U])
        KIN = {"msg": D + DE, "self": D, "node": D}
        w0 = {m: sb(f"w0_{m}", [KIN[m] if m == "msg" else NS * D, H]) for m in MLPS}
        w1 = {m: sb(f"w1_{m}", [H, D]) for m in MLPS}
        wc = {m: sb(f"wc_{m}", [H, D + 1]) for m in MLPS}
        cols = {m: sb(f"cols_{m}", [H, 3]) for m in MLPS}
        b1 = {m: sb(f"b1_{m}", [1, D]) for m in MLPS}
        c0 = {m: sb(f"c0_{m}", [P, D]) for m in MLPS}
        g1 = {m: sb(f"g1_{m}", [P, D]) for m in MLPS}
        beta1 = {m: sb(f"beta1_{m}", [P, D]) for m in MLPS}
        eps1 = sb("eps1", [P, 1])

        arena = xw[:, :, :].rearrange("p t d -> p (t d)")
        used = [0]

        def carve(*shape):
            size = int(np.prod(shape))
            a = arena[:, used[0]:used[0] + size]
            used[0] += size
            if len(shape) == 2:
                a = a.rearrange("p (a b) -> p a b", b=shape[1])
            return a

        xrow = [carve(U, D) for _ in range(2)]
        x_in = [[carve(Q, D + DE), carve(Q, D + DE)] for _ in range(2)]
        xt = [carve(Q * P) for _ in range(NS)]
        ht, sq = ([[carve(Q * P) for _ in range(NS)] for _ in range(2)] for _ in range(2))
        u, usq = ([carve(NS * Q, D) for _ in range(2)] for _ in range(2))
        msq, v1, v1c, sd1, rs1, mn, v2, sd2, rs2 = (carve(NS * Q) for _ in range(9))
        messages = [carve(NS * Q, D) for _ in range(2)]
        msum = [carve(Q, D) for _ in range(2)]
        eq = [carve(Q, P) for _ in range(2)]
        dsum = [carve(Q, D) for _ in range(2)]
        e_agg, e_got, e_x1, e_x, e_y, e_sq, e_out = ([carve(NS * Q, D) for _ in range(2)] for _ in range(7))
        f_mn, f_v2, f_sd_t, f_rs_t = (carve(NS * Q) for _ in range(4))
        assert used[0] <= T * D
        m_src = [sb(f"m_src{b}", [P, Q], i32) for b in range(2)]
        m_dst = [sb(f"m_dst{b}", [P, Q], i32) for b in range(2)]
        m_add = [sb(f"m_add{b}", [P, Q], i32) for b in range(2)]
        m_val = [sb(f"m_val{b}", [P, Q]) for b in range(2)]
        e_idx = [sb(f"e_idx{b}", [P, NS * Q], i32) for b in range(2)]

        ps = [pb(f"ps{i}", [P, 512]) for i in range(8)]
        ps_a = ps[0:NS]
        QW = D + 2

        def bank(s, b):
            return ps[NS + NS * b + s]

        def output(s, b):
            return bank(s, b)[:, 0:Q * QW].rearrange("p (q w) -> p q w", w=QW)

        ps_eq, ps_sum = ps[6], ps[7]

        names = """const_pads const_zeros const_all prep ids_ready zrow_ready graph_ready in_loaded weights_loaded
            weights_mm weights_ready row_col_ready xa_ready copied ids_written lp_slots_ready eq_before_ps before_done before_kept
            add_rows_written nodes_loaded node_rows_written scaled0 scaled scanned carry_ps carry_ready carry_added
            c_step c_act t_done xt_ready h_done ht_ready msq_ready v1_ready v1c_ready sq_ready q_done sd_ready rs_ready scaled_u u_ready
            relu_ready mean_sum centred usq_ready var_ready sd2_ready rs2_ready normed gained out_ready
            eq_ps eq_ready dsum_ps dsum_ready adds_done e_ready e_res f_sum f_cen f_sq f_var f_sd
            f_rs f_out src_slot_ready pool_passed pe_passed sp_passed out_freed""".split()
        (const_pads, const_zeros, const_all, prep, ids_ready, zrow_ready, graph_ready, in_loaded, weights_loaded,
         weights_mm, weights_ready, row_col_ready, xa_ready, copied, ids_written, lp_slots_ready, eq_before_ps, before_done, before_kept,
         add_rows_written, nodes_loaded, node_rows_written, scaled0, scaled, scanned, carry_ps, carry_ready,
         carry_added, c_step, c_act, t_done, xt_ready, h_done, ht_ready, msq_ready, v1_ready, v1c_ready, sq_ready, q_done, sd_ready,
         rs_ready, scaled_u, u_ready, relu_ready, mean_sum, centred, usq_ready, var_ready, sd2_ready,
         rs2_ready, normed, gained, out_ready, eq_ps, eq_ready, dsum_ps, dsum_ready, adds_done, e_ready,
         e_res, f_sum, f_cen, f_sq, f_var, f_sd, f_rs, f_out, src_slot_ready, pool_passed, pe_passed, sp_passed, out_freed) = [sem(n) for n in names]
        (lp_written, idx_loaded, idx_saved, x_loaded, x1_stored, m_idx, m_rows, m_val_loaded, m_got,
         m_add_loaded, msum_stored, self_stored, e_idx_loaded, e_loaded, e_x1_loaded, e_gathered, out_stored,
         tail_stored, self_loaded, x_copied) = [
            [sem(f"{n}{b}") for b in range(2)] for n in
            ("lp_written idx_loaded idx_saved x_loaded x1_stored m_idx m_rows m_val_loaded m_got "
             "m_add_loaded msum_stored self_stored e_idx_loaded e_loaded e_x1_loaded e_gathered out_stored "
             "tail_stored self_loaded x_copied").split()]
        gathered = [[sem(f"gathered{b}{c}") for c in range(CHUNKS)] for b in range(2)]
        sums_stored = [[sem(f"sums_stored{b}{c}") for c in range(CHUNKS)] for b in range(2)]

        block = ctx.enter_context(nc.Block())

        def per_step(eng, body):
            with eng.Fori(0, (K_STEPS - 2) // 2) as pair:
                body(2 * pair + 1, 0, 1)
                body(2 * pair + 2, 1, 0)
            body(K_STEPS - 1, 0, 1)

        LAST = 1
        C_OPS = 7

        def rounds(eng, total, lead, tail, body, start=0):
            for r in range(start, lead):
                body(r, r % 2)
            with eng.Fori(0, (total - lead) // 2) as k:
                for b in range(2):
                    body(2 * k + lead + b, (lead + b) % 2)
            for r in range(total, total + tail):
                body(r, r % 2)

        def live(x, total):
            return not isinstance(x, int) or 0 <= x < total

        def later(x, by):
            return not isinstance(x, int) or x >= by

        SELF = (0, ("self", "self"), NROUNDS)
        MSG = (NS * NROUNDS, ("msg", "msg"), ROUNDS)
        NODE = (NS * (NROUNDS + ROUNDS), ("node", "node"), NROUNDS)

        def items(net, x):
            before, names, total = net
            if live(x, total):
                for s, m in enumerate(names):
                    yield s, m, before + len(names) * x + s + 1

        def both(net, x):
            before, names, total = net
            if live(x, total):
                yield names[0], before + NS * (x + 1)

        def half(net, a, s):
            if net is MSG:
                return a[:, s * Q:(s + 1) * Q]
            if len(a.shape) == 2:
                return a.rearrange("p (q s) -> p s q", s=NS)[:, s]
            return a.rearrange("p (q s) d -> p s q d", s=NS)[:, s]

        def since(net, x, n, d):
            return n - d * NS if later(x, d) else net[0] or None

        def wait_old(eng, signal, value):
            if value is not None:
                eng.wait_ge(signal, value)

        S_TAIL, M_TAIL, N_TAIL = 4, ADD_LAG, 4

        def norm_and_self(eng, body):
            for c in range(SELF_R):
                body(0, c, None, 0)
            for c in range(SELF_R):
                body(1, c, c, c % 2)
            with eng.Fori(0, (PAIRS - 3) // 2) as k:
                for n in range(2 * SELF_R):
                    body(2 * k + 2 + n // SELF_R, n % SELF_R, 2 * SELF_R * k + SELF_R + n, (SELF_R + n) % 2)
            for n in range(SELF_R):
                r = (PAIRS - 2) * SELF_R + n
                body(PAIRS - 1, n, r, r % 2)
            for r in range((PAIRS - 1) * SELF_R, NROUNDS + S_TAIL):
                body(None, r - (PAIRS - 1) * SELF_R, r, r % 2)

        def bc(a, n):
            return a.unsqueeze(2).to_broadcast([P, a.shape[1], n])

        def rows(a, q):
            return a.unsqueeze(1).to_broadcast([P, q, a.shape[1]])

        @block.sync
        def _(sp):
            sp.wait_ge(const_pads, 3)
            for t, a in ((src_t, A["src"]), (dst_t, A["dst"]), (weight, A["edge_weight"])):
                sp.dma_start(t[0:FULL, 0:T], a[0:FULL * T].rearrange("(p t) -> p t", t=T)).then_inc(in_loaded, 16)
                sp.dma_start(t[FULL:FULL + 1, 0:REST], a[FULL * T:N].rearrange("(p t) -> p t", p=1)).then_inc(in_loaded, 16)
            sp.dma_start(dst_t[0:FULL - 1, T:T + 1],
                         A["dst"][T:FULL * T].rearrange("(p t) -> p t", t=T)[:, 0:1]).then_inc(in_loaded, 16)
            sp.dma_start(dst_t[FULL - 1:FULL, T:T + 1],
                         A["dst"][FULL * T:FULL * T + 1].rearrange("(p t) -> p t", p=1)).then_inc(in_loaded, 16)
            sp.wait_ge(zrow_ready, 1)
            sp.dma_start(xa_g[:, :, D:XD].bitcast(i32), node_row_t[:, :].unsqueeze(2)).then_inc(row_col_ready, 16)
            sp.wait_ge(const_zeros, 1)
            sp.dma_start(xa[N:N + P, 0:D], zeros[:, 0:D]).then_inc(xa_ready, 16)
            sp.dma_start(xa[N + P:NP, 0:D], zeros[0:NP - N - P, 0:D]).then_inc(xa_ready, 16)
            for t in (*run_sums, msg_sums, aggr_src):
                sp.dma_start(t[NP:NP + P, :], zeros[:, 0:D]).then_inc(copied, 16)
            sp.wait_ge(ids_ready, 1)
            sp.dma_start(line(src_ids), src_t[:, :]).then_inc(ids_written, 16)
            sp.dma_start(line(dst_ids), dst_t[:, 0:T]).then_inc(ids_written, 16)
            sp.dma_start(line(src_vals), src_f[:, :]).then_inc(ids_written, 16)
            sp.wait_ge(ids_written, 48)
            for b in range(2):
                sp.dma_start(idx[b][:, :], line(src_ids)[:, b * U:(b + 1) * U]).then_inc(idx_loaded[b], 16)
            sp.wait_ge(weights_loaded, 16 * 27)
            step = N // X_PARTS
            for k in range(X_PARTS):
                if k >= 2:
                    sp.wait_ge(x_copied[k % 2], 16 * (k // 2))
                    sp.sem_inc(sp_passed, 1)
                sp.dma_start(xa[k * step:(k + 1) * step, 0:D], A["x"][k * step:(k + 1) * step, :]).then_inc(x_copied[k % 2], 16)
            sp.dma_start(edge_attr[0:E, :].rearrange("(a b) d -> a (b d)", b=25),
                         A["edge_attr_32"].rearrange("(a b) d -> a (b d)", b=25)).then_inc(copied, 16)
            sp.dma_start(edge_attr[N:N + P, :], zeros[:, 0:DE]).then_inc(copied, 16)
            sp.dma_start(edge_attr[N + P:NP, :], zeros[0:NP - N - P, 0:DE]).then_inc(copied, 16)
            for b in range(2):
                sp.wait_ge(lp_written[b], 16 * U * PAIRS)
            sp.dma_start(node_row_t[:, :].unsqueeze(2), xa_g[:, :, D:XD].bitcast(i32)).then_inc(nodes_loaded, 16)
            sp.wait_ge(nodes_loaded, 16)
            sp.dma_start(line(node_rows), node_row_t[:, :]).then_inc(node_rows_written, 16)
            sp.wait_ge(before_kept, GROUPS + 1)
            sp.dma_start(line(add_rows), add_row_t[:, :]).then_inc(add_rows_written, 16)

            def fill_idx(s, i, b, source):
                for c in range(CHUNKS):
                    sp.wait_ge(gathered[b][c], 16 * CH * (PAIRS * s + i))
                sp.dma_start(idx[b][:, :], line(source)[:, ds((2 * i + b) * U, U)]).then_inc(idx_loaded[b], 16)

            def store_sums(table, s, i, b):
                for c in range(CHUNKS):
                    sp.wait_ge(scanned, T * s + U * (2 * i + b) + CH * (c + 1))
                    sp.dma_start(run_g[table][:, ds((2 * i + b) * U + c * CH, CH), :],
                                 sums[b][:, c * CH:(c + 1) * CH, :]).then_inc(sums_stored[b][c], 16)

            def pass0_out(i, b):
                store_sums(0, 0, i, b)
                sp.wait_ge(scaled0, 3 * (2 * i + b) + 1)
                sp.sem_inc(sp_passed, 1)
                sp.dma_start(line(in_rows)[:, ds((2 * i + b) * U, U)], idx_out[b][:, :]).then_inc(idx_saved[b], 16)

            with sp.Fori(1, PAIRS) as i:
                for b in range(2):
                    fill_idx(0, i, b, src_ids)
                    pass0_out(i - 1, b)
            for b in range(2):
                pass0_out(PAIRS - 1, b)
            for b in range(2):
                sp.wait_ge(idx_saved[b], 16 * PAIRS)

            def one_step(s, source, target):
                for b in range(2):
                    for c in range(CHUNKS):
                        sp.wait_ge(gathered[b][c], 16 * CH * PAIRS * s)
                    sp.dma_start(idx[b][:, :], line(in_rows)[:, b * U:(b + 1) * U]).then_inc(idx_loaded[b], 16)

                with sp.Fori(1, PAIRS) as i:
                    for b in range(2):
                        fill_idx(s, i, b, in_rows)
                        store_sums(target, s, i - 1, b)
                for b in range(2):
                    store_sums(target, s, PAIRS - 1, b)

            per_step(sp, one_step)

            sp.wait_ge(node_rows_written, 16)

            def load_x(i, b):
                sp.dma_start(xrow[b], xa_g[:, ds((2 * i + b) * U, U), 0:D]).then_inc(x_loaded[b], 16)

            def store_x1(i, b):
                sp.wait_ge(c_step, C_OPS * (2 * i + b + 1))
                sp.dma_start(x1_g[:, ds((2 * i + b) * U, U), :], sums[b][:, :, :]).then_inc(x1_stored[b], 16)

            for b in range(2):
                for c in range(CHUNKS):
                    sp.wait_ge(gathered[b][c], 16 * CH * PAIRS * K_STEPS)
                sp.dma_start(idx[b][:, :], line(node_rows)[:, b * U:(b + 1) * U]).then_inc(idx_loaded[b], 16)
                load_x(0, b)

            def norm_part(i, c):
                if c == 0 and later(i, 1):
                    sp.wait_ge(x1_stored[0], 16 * i)
                    sp.sem_inc(sp_passed, 1)
                if c == 1:
                    if live(i + 1, PAIRS):
                        fill_idx(K_STEPS, i + 1, 0, node_rows)
                    if later(i, 1):
                        store_x1(i - 1, 1)
                        load_x(i, 1)
                if c == 3 and later(i, 1):
                    sp.wait_ge(x1_stored[1], 16 * i)
                    sp.sem_inc(sp_passed, 1)
                if c == 4:
                    store_x1(i, 0)
                    if live(i + 1, PAIRS):
                        load_x(i + 1, 0)
                        fill_idx(K_STEPS, i + 1, 1, node_rows)

            def self_round(r, b):
                if live(r, NROUNDS):
                    if later(r, 2):
                        sp.wait_ge(t_done, NS * (r - 1))
                    sp.sem_inc(sp_passed, 1)
                    sp.dma_start(e_x[b], x1_g[:, ds(NS * Q * r, NS * Q), :]).then_inc(self_loaded[b], 16)
                y = r - 4
                if live(y, NROUNDS):
                    sp.wait_ge(out_ready, NS * (y + 1))
                    sp.dma_start(agg_g[:, ds(NS * Q * y, NS * Q), :], e_y[b]).then_inc(self_stored[b], 16)

            def msg_round(r, b):
                if live(r, ROUNDS):
                    if later(r, 2):
                        sp.wait_ge(m_got[b], 16 * Q * (r - b))
                    sp.dma_start(m_src[b][:, :], line(src_ids)[:, ds(r * Q, Q)]).then_inc(m_idx[b], 16)
                    sp.dma_start(m_dst[b][:, :], line(dst_ids)[:, ds(r * Q, Q)]).then_inc(m_idx[b], 16)
                    if later(r, 2):
                        sp.wait_ge(t_done, MSG[0] + NS * (r - 1))
                    for t in range(2):
                        sp.dma_start(x_in[b][t][:, :, D:D + DE], ea_g[:, ds(r * Q, Q), :]).then_inc(m_rows[b], 16)
                y = r - 3
                if live(y, ROUNDS):
                    if later(y, 2):
                        sp.wait_ge(eq_ready, y - 1)
                    sp.dma_start(m_val[1 - b][:, :], line(src_vals)[:, ds(y * Q, Q)]).then_inc(m_val_loaded[1 - b], 16)
                y = r - ADD_LAG + 1
                o = (b - ADD_LAG + 1) % 2
                if live(y, ROUNDS):
                    if later(y, 2):
                        sp.wait_ge(adds_done, 16 * Q * (y - 1))
                        sp.sem_inc(sp_passed, 1)
                    sp.dma_start(m_add[o][:, :], line(add_rows)[:, ds(y * Q, Q)]).then_inc(m_add_loaded[o], 16)
                y = r - 5
                if live(y, ROUNDS):
                    sp.wait_ge(scanned, T * K_STEPS + Q * (y + 1))
                    sp.dma_start(msg_g[:, ds(y * Q, Q), :], msum[1 - b]).then_inc(msum_stored[1 - b], 16)

            sp.wait_ge(ids_written, 48)
            sp.wait_ge(add_rows_written, 16)
            sp.wait_ge(copied, 16 * (4 + 3))

            def norm_self_round(i, c, r, b):
                if i is not None:
                    norm_part(i, c)
                elif c == 0:
                    sp.wait_ge(x1_stored[0], 16 * PAIRS)
                elif c == 1:
                    store_x1(PAIRS - 1, 1)
                elif c == 3:
                    sp.wait_ge(x1_stored[1], 16 * PAIRS)
                elif c == 5:
                    for m in range(2):
                        msg_round(m, m)
                if r is not None:
                    if isinstance(r, int) and r == NROUNDS + 2:
                        msg_round(2, 0)
                    self_round(r, b)

            norm_and_self(sp, norm_self_round)
            rounds(sp, ROUNDS, LEAD_M, M_TAIL, msg_round, start=3)
            for b in range(2):
                sp.wait_ge(msum_stored[b], 16 * ROUNDS // 2)
            sp.wait_ge(adds_done, 16 * T)

            def node_round(r, b):
                if live(r, NROUNDS):
                    if later(r, 2):
                        sp.wait_ge(e_ready, r - 1)
                    at = ds(NS * Q * r, NS * Q)
                    sp.dma_start(e_idx[b][:, :], line(node_rows)[:, at]).then_inc(e_idx_loaded[b], 16)
                    sp.dma_start(e_agg[b], agg_g[:, at, :]).then_inc(e_loaded[b], 16)
                y = r - 3
                if live(y, NROUNDS):
                    if later(y, 2):
                        sp.wait_ge(e_res, y - 1)
                    sp.dma_start(e_x1[1 - b], x1_g[:, ds(NS * Q * y, NS * Q), :]).then_inc(e_x1_loaded[1 - b], 16)
                y = r - 6
                if live(y, NROUNDS):
                    sp.wait_ge(f_out, y + 1)
                    for p0, p1 in ((0, 112), (112, FULL)):
                        sp.dma_start(out_g[p0:p1, ds(NS * Q * y, NS * Q), :], e_out[b][p0:p1]).then_inc(out_stored[b], 16)

            def node_tail(y, b):
                sp.dma_start(out[ds(FULL * T + NS * Q * y, NS * Q), :].rearrange("(o q) d -> o q d", o=1),
                             e_out[b][FULL:FULL + 1]).then_inc(tail_stored[b], 16)

            def free_out(y, b, tails):
                if live(y, NROUNDS):
                    sp.wait_ge(out_stored[b], 16 * (y - b + 2))
                    sp.sem_inc(sp_passed, 1)
                    if tails:
                        sp.wait_ge(tail_stored[b], 8 * (y - b + 2))
                    sp.sem_inc(out_freed, 1)

            def with_tail(r, b):
                node_round(r, b)
                if live(r - 6, TAILS):
                    node_tail(r - 6, b)
                free_out(r - 7, 1 - b, live(r - 7, TAILS))

            def without_tail(r, b):
                node_round(r, b)
                free_out(r - 7, 1 - b, False)

            for r in range(LEAD_N):
                with_tail(r, r % 2)
            pairs, odd = divmod(TAILS + 6 - LEAD_N, 2)
            with sp.Fori(0, pairs) as k:
                for b in range(2):
                    with_tail(2 * k + LEAD_N + b, (LEAD_N + b) % 2)
            first = LEAD_N + 2 * pairs
            for r in range(first, first + odd):
                with_tail(r, r % 2)
            first += odd
            for b in range(2):
                sp.wait_ge(tail_stored[b], 16 * ((TAILS + 1 - b) // 2))
            with sp.Fori(0, (NROUNDS - first) // 2) as k:
                for b in range(2):
                    without_tail(2 * k + first + b, (first + b) % 2)
            for r in range(first + (NROUNDS - first) // 2 * 2, NROUNDS + 6):
                without_tail(r, r % 2)
            for b in range(2):
                sp.wait_ge(out_stored[b], 16 * 2 * ((NROUNDS + 1 - b) // 2))

        @block.gpsimd
        def _(pool):
            nc.gpsimd.memset(src_t[:, :], PAD_ID).then_inc(const_pads, 1)
            nc.gpsimd.memset(dst_t[:, :], PAD_ID).then_inc(const_pads, 1)
            nc.gpsimd.memset(weight[:, :], 0.0).then_inc(const_pads, 1)
            nc.gpsimd.memset(node_row_t[:, :], ZROW).then_inc(zrow_ready, 1)
            nc.gpsimd.memset(zeros[:, :], 0.0).then_inc(const_zeros, 1)
            nc.gpsimd.iota(row_id[:, :], [[1, T]], base=0, channel_multiplier=T).then_inc(const_all, 1)
            nc.gpsimd.iota(row0[:, :], [[1, 1]], base=-1, channel_multiplier=T).then_inc(const_all, 1)
            nc.gpsimd.iota(trash_t[:, :], [[0, 1]], base=TRASH, channel_multiplier=1).then_inc(const_all, 1)
            nc.gpsimd.memset(ident[:, :], 0.0).then_inc(const_all, 1)
            nc.gpsimd.memset(ones[:, :], 1.0).then_inc(const_all, 1)
            nc.gpsimd.memset(mean_h[:, :], 1.0 / H).then_inc(const_all, 1)
            nc.gpsimd.memset(eps_mlp[:, :], EPS_MLP).then_inc(const_all, 1)
            nc.gpsimd.memset(eps_out[:, :], EPS_OUT).then_inc(const_all, 1)
            nc.gpsimd.memset(sums[1][:, :, :], 0.0).then_inc(const_all, 1)
            pool.wait_ge(const_all, 9)
            nc.gpsimd.affine_select(out=ident[:, :], in_=ident[:, :], compare_op=ALU.not_equal, fill=1.0,
                                    base=0, pattern=[[-1, P]], channel_multiplier=1).then_inc(const_all, 1)
            nc.gpsimd.affine_select(out=upper[:, :], in_=ones[:, :], compare_op=ALU.is_gt, fill=0.0,
                                    base=0, pattern=[[1, P]], channel_multiplier=-1).then_inc(const_all, 1)
            nc.gpsimd.affine_select(out=lower[:, :], in_=ones[:, :], compare_op=ALU.is_gt, fill=0.0,
                                    base=0, pattern=[[-1, P]], channel_multiplier=1).then_inc(const_all, 1)

            def passed():
                pool.sem_inc(pool_passed, 1)

            pool.wait_ge(row_col_ready, 16)
            with pool.Fori(0, PAIRS) as i:
                for b in range(2):
                    pool.wait_ge(lp_slots_ready, 2 * (2 * i + b + 1))
                    passed()
                    for t in range(U):
                        pool.indirect_dma_start(xa_flat, OFF(ap=lp_slot[b][:, t:t + 1], axis=0), row_slot[b][:, t:t + 1].bitcast(fp32),
                                                None, bounds_check=NP * XD - 1, oob_is_err=False).then_inc(lp_written[b], 16)
            for b in range(2):
                pool.wait_ge(lp_written[b], 16 * U * PAIRS)

            def gather_group(table, width, s, i, b):
                pool.wait_ge(idx_loaded[b], 16 * (PAIRS * s + i + 1))
                passed()
                for t in range(U):
                    pool.indirect_dma_start(got[b][:, t, 0:width], None, table,
                                            OFF(ap=idx[b][:, t:t + 1], axis=0)).then_inc(gathered[b][t // CH], 16)

            def end_of_pass(s, table):
                for b in range(2):
                    for c in range(CHUNKS):
                        pool.wait_ge(sums_stored[b][c], 16 * PAIRS * (s + 1))
                pool.wait_ge(carry_ready, s + 1)
                passed()
                pool.indirect_dma_start(table, OFF(ap=fix_row[:, 0:1], axis=0), carry[:, :], None,
                                        compute_op=ALU.add).then_inc(carry_added, 16)
                pool.wait_ge(carry_added, 16 * (s + 1))
                passed()

            def one_pass(table, width, s):
                for b in range(2):
                    gather_group(table, width, s, 0, b)
                with pool.Fori(1, PAIRS) as i:
                    for b in range(2):
                        pool.wait_ge(scanned, T * s + U * (2 * i + b - 1))
                        gather_group(table, width, s, i, b)

            pool.wait_ge(xa_ready, 16 * 2)
            for b in range(2):
                pool.wait_ge(x_copied[b], 16 * X_PARTS // 2)
            passed()
            one_pass(xa[:, :], XD, 0)
            pool.wait_ge(graph_ready, 1)
            pool.wait_ge(copied, 16 * (4 + 3))
            end_of_pass(0, run_sums[0][:, :])

            def one_step(s, source, target):
                one_pass(run_sums[source][:, :], D, s)
                end_of_pass(s, run_sums[target][:, :])

            per_step(pool, one_step)

            for b in range(2):
                gather_group(run_sums[LAST][:, :], D, K_STEPS, 0, b)
            with pool.Fori(1, PAIRS) as i:
                for b in range(2):
                    pool.wait_ge(c_step, C_OPS * (2 * i + b - 2) + 1)
                    gather_group(run_sums[LAST][:, :], D, K_STEPS, i, b)
            for b in range(2):
                pool.wait_ge(x1_stored[b], 16 * PAIRS)
            passed()

            def msg_round(r, b):
                y = r - ADD_LAG
                o = (b - ADD_LAG) % 2
                if live(r, ROUNDS):
                    pool.wait_ge(m_idx[b], 16 * (r - b + 2))
                    if later(r, 2):
                        pool.wait_ge(t_done, MSG[0] + NS * (r - 1))
                    passed()
                for t in range(Q):
                    if live(r, ROUNDS):
                        pool.indirect_dma_start(x_in[b][0][:, t, 0:D], None, x1[:, :],
                                                OFF(ap=m_src[b][:, t:t + 1], axis=0)).then_inc(m_got[b], 16)
                        pool.indirect_dma_start(x_in[b][1][:, t, 0:D], None, x1[:, :],
                                                OFF(ap=m_dst[b][:, t:t + 1], axis=0)).then_inc(m_got[b], 16)
                    if live(y, ROUNDS):
                        pool.wait_ge(dsum_ready, y + 1)
                        pool.wait_ge(m_add_loaded[o], 8 * (y - o + 2))
                        if isinstance(y, int) and y == 0 and t == 0:
                            for h in range(2):
                                pool.wait_ge(self_stored[h], 16 * ((NROUNDS + 1 - h) // 2))
                        else:
                            pool.wait_ge(adds_done, 16 * (Q * y + t))
                        passed()
                        pool.indirect_dma_start(aggr_src[:, :], OFF(ap=m_add[o][:, t:t + 1], axis=0),
                                                dsum[o][:, t, :], None, compute_op=ALU.add).then_inc(adds_done, 16)

            rounds(pool, ROUNDS, LEAD_M, M_TAIL, msg_round)
            for b in range(2):
                pool.wait_ge(msum_stored[b], 16 * ROUNDS // 2)
            pool.wait_ge(carry_ready, K_STEPS + 1)
            pool.indirect_dma_start(msg_sums[:, :], OFF(ap=fix_row[:, 0:1], axis=0), carry[:, :], None,
                                    compute_op=ALU.add).then_inc(carry_added, 16)
            pool.wait_ge(carry_added, 16 * (K_STEPS + 1))

            def node_gathers(r, b):
                pool.wait_ge(e_idx_loaded[b], 8 * (r - b + 2))
                if later(r, 2):
                    pool.wait_ge(e_ready, r - 1)
                passed()
                for t in range(NS * Q):
                    pool.indirect_dma_start(e_got[b][:, t, :], None, msg_sums[:, :],
                                            OFF(ap=e_idx[b][:, t:t + 1], axis=0)).then_inc(e_gathered[b], 16)

            rounds(pool, NROUNDS, LEAD_N, 0, node_gathers)

        @block.scalar
        def _(act):
            for m in MLPS:
                w = {k: A[f"L1_gnn_{m}_{k}"] for k in ("W0", "b0", "g0", "beta0", "W1", "b1", "g1", "beta1")}
                act.dma_start(w0[m][0:KIN[m], :], w["W0"]).then_inc(weights_loaded, 16)
                if m != "msg":
                    act.dma_start(w0[m][D:2 * D, :], w["W0"]).then_inc(weights_loaded, 16)
                act.dma_start(w1[m][:, :], w["W1"]).then_inc(weights_loaded, 16)
                for c, k in enumerate(("b0", "g0", "beta0")):
                    act.dma_start(cols[m][:, c:c + 1], w[k].rearrange("(p o) -> p o", o=1)).then_inc(weights_loaded, 16)
                act.dma_start(b1[m][:, :], w["b1"].unsqueeze(0)).then_inc(weights_loaded, 16)
                act.dma_start(g1[m][:, :], w["g1"].partition_broadcast(P)).then_inc(weights_loaded, 16)
                act.dma_start(beta1[m][:, :], w["beta1"].partition_broadcast(P)).then_inc(weights_loaded, 16)
            act.dma_start(eps1[:, :], A["L1_gnn_eps"].partition_broadcast(P)).then_inc(weights_loaded, 16)
            act.wait_ge(const_all, 12)
            act.wait_ge(weights_ready, 1)

            def scaled_x(i, b):
                act.wait_ge(x_loaded[b], 16 * (i + 1))
                nc.scalar.activation(xrow[b], xrow[b], ACT.Copy, scale=1.0 + ALPHA).then_inc(c_act, 1)

            def norm_squares(i, b):
                act.wait_ge(c_step, C_OPS * (2 * i + b) + 4)
                nc.scalar.activation(xrow[b], sums[b][:, :, :], ACT.Square).then_inc(c_act, 1)

            def norm_dev(i, b):
                act.wait_ge(c_step, C_OPS * (2 * i + b) + 5)
                nc.scalar.activation(c_sd[:, :], c_sq[:, :], ACT.Sqrt, bias=eps_out[:, 0:1], scale=1.0 / D).then_inc(c_act, 1)

            def norm_part(i, c):
                if i is None:
                    return
                if c == 0:
                    scaled_x(i, 0)
                if c == 2:
                    norm_squares(i, 0)
                if c == 3:
                    norm_dev(i, 0)
                    scaled_x(i, 1)
                if c == 5:
                    norm_squares(i, 1)
                if c == 6:
                    norm_dev(i, 1)

            def transposed_rows(net, x):
                if net is MSG:
                    for s, m, n in items(net, x):
                        act.wait_ge(t_done, n)
                        wait_old(act, h_done, since(net, x, n, 1))
                        nc.scalar.activation(xt[s][0:KIN[m], :], ps_a[s][0:KIN[m], :], ACT.Copy).then_inc(xt_ready, 1)
                else:
                    for m, n in both(net, x):
                        act.wait_ge(t_done, n)
                        wait_old(act, h_done, since(net, x, n, 1))
                        nc.scalar.activation(xt[0], ps_a[0][:, :], ACT.Copy).then_inc(xt_ready, NS)

            def hidden(net, x, b):
                for s, m, n in items(net, x):
                    act.wait_ge(h_done, n)
                    wait_old(act, q_done, since(net, x, n, 2))
                    nc.scalar.activation(ht[b][s], bank(s, b)[:, :], ACT.Relu, bias=cols[m][:, 0:1]).then_inc(ht_ready, 1)

            def squares(net, x, b):
                for s, m, n in items(net, x):
                    act.wait_ge(ht_ready, n)
                    nc.scalar.activation(sq[b][s], ht[b][s], ACT.Square).then_inc(sq_ready, 1)

            def mean_squares(net, x, b):
                for s, m, n in items(net, x):
                    act.wait_ge(q_done, n)
                    wait_old(act, v1_ready, since(net, x, n, 1))
                    nc.scalar.activation(half(net, msq, s), output(s, b)[:, :, D], ACT.Square).then_inc(msq_ready, 1)

            def hidden_dev(net, x):
                for m, n in both(net, x):
                    act.wait_ge(v1c_ready, n)
                    wait_old(act, rs_ready, since(net, x, n, 1))
                    nc.scalar.activation(sd1, v1c, ACT.Sqrt, bias=eps_mlp[:, 0:1]).then_inc(sd_ready, NS)

            def relu(net, x, b):
                for m, n in both(net, x):
                    act.wait_ge(u_ready, n)
                    nc.scalar.activation(u[b], u[b], ACT.Relu).then_inc(relu_ready, NS)

            def u_squares(net, x, b):
                for m, n in both(net, x):
                    act.wait_ge(centred, n)
                    wait_old(act, var_ready, since(net, x, n, 2))
                    nc.scalar.activation(usq[b], u[b], ACT.Square).then_inc(usq_ready, NS)

            def u_dev(net, x):
                for m, n in both(net, x):
                    act.wait_ge(var_ready, n)
                    wait_old(act, rs2_ready, since(net, x, n, 1))
                    nc.scalar.activation(sd2, v2, ACT.Sqrt, bias=eps_mlp[:, 0:1], scale=1.0 / D).then_inc(sd2_ready, NS)

            def msg_sum(y, b):
                if live(y, ROUNDS):
                    act.wait_ge(dsum_ps, y + 1)
                    if later(y, 2):
                        act.wait_ge(adds_done, 16 * Q * (y - 1))
                    nc.scalar.activation(dsum[b], ps_sum[:, 0:Q * D].rearrange("p (q d) -> p q d", d=D), ACT.Copy).then_inc(dsum_ready, 1)

            def norm_self_round(i, c, r, b):
                if r is not None:
                    mean_squares(SELF, r - 2, b)
                    transposed_rows(SELF, r)
                    u_dev(SELF, r - 3)
                    hidden_dev(SELF, r - 2)
                    relu(SELF, r - 2, b)
                norm_part(i, c)
                if r is not None:
                    hidden(SELF, r, b)
                    squares(SELF, r, b)
                    u_squares(SELF, r - 2, b)

            norm_and_self(act, norm_self_round)

            def msg_round(r, b):
                mean_squares(MSG, r - 2, b)
                transposed_rows(MSG, r)
                u_dev(MSG, r - 3)
                hidden_dev(MSG, r - 2)
                relu(MSG, r - 2, b)
                msg_sum(r - 4, b)
                hidden(MSG, r, b)
                squares(MSG, r, b)
                u_squares(MSG, r - 2, b)

            rounds(act, ROUNDS, LEAD_M, M_TAIL, msg_round)

            def final_squares(y, b):
                if live(y, NROUNDS):
                    act.wait_ge(f_cen, y + 1)
                    if later(y, 2):
                        act.wait_ge(f_var, y - 1)
                    nc.scalar.activation(e_sq[b], e_y[b], ACT.Square).then_inc(f_sq, 1)

            def final_dev(y):
                if live(y, NROUNDS):
                    act.wait_ge(f_var, y + 1)
                    if later(y, 1):
                        act.wait_ge(f_rs, y)
                    nc.scalar.activation(f_sd_t, f_v2, ACT.Sqrt, bias=eps_out[:, 0:1], scale=1.0 / D).then_inc(f_sd, 1)

            def node_round(r, b):
                mean_squares(NODE, r - 2, b)
                transposed_rows(NODE, r)
                u_dev(NODE, r - 3)
                hidden_dev(NODE, r - 2)
                relu(NODE, r - 2, b)
                final_dev(r - 4)
                hidden(NODE, r, b)
                squares(NODE, r, b)
                u_squares(NODE, r - 2, b)
                final_squares(r - 3, 1 - b)

            rounds(act, NROUNDS, LEAD_N, N_TAIL, node_round)

        @block.vector
        def _(dve):
            V = nc.vector
            chain = [0]

            def link(ins):
                chain[0] += 1
                ins.then_inc(prep, 1)
                dve.wait_ge(prep, chain[0])

            dve.wait_ge(in_loaded, 128)
            dve.wait_ge(const_all, 12)
            link(V.tensor_copy(src_f[:, :], src_t[:, :]))
            link(V.tensor_copy(dst_f[:, :], dst_t[:, :]))
            V.tensor_scalar(head_len[:, :], dst_f[:, 0:1], 0.0, None, ALU.mult).then_inc(ids_ready, 1)
            link(V.tensor_scalar(weight9[:, :], weight[:, :], 1.0 - ALPHA, None, ALU.mult))
            link(V.memset(same[:, :], 0.0))
            link(V.tensor_tensor(same[:, 1:T], dst_f[:, 1:T], dst_f[:, 0:T - 1], ALU.is_equal))
            link(V.tensor_tensor(scratch[:, :], dst_f[:, 0:T], dst_f[:, 1:T + 1], ALU.is_equal))
            link(V.tensor_scalar(before_all[:, :], dst_f[:, 0:T], float(XD), float(D), ALU.mult, ALU.add))
            link(V.scalar_tensor_tensor(lp_index[:, :], scratch[:, :], float(BIG), before_all[:, :], ALU.mult, ALU.add))
            dve.wait_ge(ids_ready, 1)
            link(V.tensor_tensor(scratch[:, :], dst_f[:, 0:T], dst_f[:, 0:1].to_broadcast([P, T]), ALU.is_equal))
            link(V.tensor_reduce(head_len[:, :], scratch[:, :], AX.X, ALU.add))
            link(V.tensor_tensor(fix_row[:, :], head_len[:, :], row0[:, :], ALU.add))
            link(V.tensor_copy(trash_f[:, :], trash_t[:, :]))
            link(V.tensor_scalar(center[:, :], ident[:, :], -1.0 / H, None, ALU.add))
            dve.wait_ge(weights_mm, 1)
            link(V.scalar_tensor_tensor(carry_sel[:, :], ps[0][:, 0:P], dst_f[:, T - 1:T], upper[:, :], ALU.is_equal, ALU.mult))
            V.tensor_copy(gate_v[:, 0:1], carry_sel[:, 0:1]).then_inc(graph_ready, 1)

            def lp_slots(i, b):
                g = 2 * i + b
                V.tensor_scalar(lp_slot[b][:, :], lp_index[:, ds(g * U, U)], 0.0, None, ALU.add).then_inc(lp_slots_ready, 1)
                V.tensor_scalar(row_slot[b][:, :], row_id[:, ds(g * U, U)], 0.0, None, ALU.add).then_inc(lp_slots_ready, 1)

            for b in range(2):
                lp_slots(0, b)
            dve.wait_ge(weights_loaded, 16 * 27)
            for k, m in enumerate(MLPS):
                link(V.tensor_scalar(wc[m][:, 0:D], w1[m][:, :], cols[m][:, 1:2], None, ALU.mult))
            link(V.tensor_scalar(eps1[:, :], eps1[:, :], 1.0, None, ALU.add))
            link(V.tensor_scalar(g1["self"][:, :], g1["self"][:, :], eps1[:, 0:1], None, ALU.mult))
            link(V.tensor_scalar(beta1["self"][:, :], beta1["self"][:, :], eps1[:, 0:1], None, ALU.mult))
            dve.wait_ge(weights_mm, 3)
            for k, m in enumerate(MLPS):
                link(V.tensor_copy(c0[m][:, :], ps[1][:, k * D:(k + 1) * D]))
                link(V.tensor_copy(wc[m][:, 0:D], ps[2][:, k * D:(k + 1) * D]))
                link(V.tensor_copy(wc[m][:, D:D + 1], mean_h[:, :]))
            V.tensor_copy(gate_v[:, 1:2], wc["node"][:, 0:1]).then_inc(weights_ready, 1)

            def count_before(i, b):
                g = 2 * i + b
                V.tensor_scalar(src_slot[b][:, :], src_f[:, ds(g * U, U)], 0.0, None, ALU.add).then_inc(src_slot_ready, 1)
                dve.wait_ge(src_slot_ready, g + 1)
                if not (isinstance(i, int) and i == 0 and b == 0):
                    dve.wait_ge(before_kept, g)
                for c in range(U // Q):
                    bank = ps[6 + (b + c) % 2]
                    dve.wait_ge(eq_before_ps, U // Q * g + c + 1)
                    for t in range(Q):
                        k = c * Q + t
                        ins = V.scalar_tensor_tensor(bank[:, t * P:(t + 1) * P], bank[:, t * P:(t + 1) * P],
                                                     src_slot[b][:, k:k + 1], lower[:, :], ALU.is_equal, ALU.mult,
                                                     accum_out=before[:, k:k + 1])
                    ins.then_inc(before_done, 1)
                dve.wait_ge(before_done, U // Q * (g + 1))
                V.tensor_scalar(before_all[:, ds(g * U, U)], before[:, :], 1.0, None, ALU.min).then_inc(before_kept, 1)

            for b in range(2):
                count_before(0, b)
            with dve.Fori(1, PAIRS) as i:
                for b in range(2):
                    dve.wait_ge(lp_written[b], 16 * U * i)
                    lp_slots(i, b)
                    count_before(i, b)
            dve.wait_ge(before_kept, GROUPS)
            link(V.tensor_scalar(scratch[:, :], src_f[:, :], trash_f[:, 0:1], None, ALU.subtract))
            link(V.tensor_tensor(scratch[:, :], scratch[:, :], before_all[:, :], ALU.mult))
            V.tensor_tensor(add_row_t[:, :], src_f[:, :], scratch[:, :], ALU.subtract).then_inc(before_kept, 1)

            def scan_chunk(s, i, b, c):
                g = 2 * i + b
                if not (isinstance(i, int) and i == 0 and isinstance(s, int) and s == 0):
                    dve.wait_ge(sums_stored[b][c], 16 * (PAIRS * s + i))
                for t in range(c * CH, c * CH + CH):
                    at = T * s + U * g + t
                    if not (isinstance(at, int) and at == 0):
                        dve.wait_ge(scanned, at)
                    prev = sums[b][:, t - 1, :] if t else sums[1 - b][:, U - 1, :]
                    V.scalar_tensor_tensor(sums[b][:, t, :], prev, same[:, ds(g * U + t, 1)], got[b][:, t, 0:D],
                                           ALU.mult, ALU.add).then_inc(scanned, 1)

            def pass0_group(i, b):
                g = 2 * i + b
                for c in range(CHUNKS):
                    dve.wait_ge(gathered[b][c], 16 * CH * (i + 1))
                if not (isinstance(i, int) and i == 0):
                    dve.wait_ge(idx_saved[b], 16 * i)
                V.tensor_copy(idx_out[b][:, :], got[b][:, :, D:XD].rearrange("p u o -> p (u o)").bitcast(i32)).then_inc(scaled0, 1)
                V.tensor_tensor(got[b][:, :, 0:D], got[b][:, :, 0:D], bc(weight[:, ds(g * U, U)], D), ALU.mult).then_inc(scaled0, 1)
                dve.wait_ge(scaled0, 3 * g + 2)
                V.tensor_scalar(xw[:, ds(g * U, U), :], got[b][:, :, 0:D], ALPHA, None, ALU.mult).then_inc(scaled0, 1)
                for c in range(CHUNKS):
                    scan_chunk(0, i, b, c)

            def carries(s):
                dve.wait_ge(carry_ps, s + 1)
                if not (isinstance(s, int) and s == 0):
                    dve.wait_ge(carry_added, 16 * s)
                V.tensor_copy(carry[:, :], ps[0][:, 0:D]).then_inc(carry_ready, 1)

            for b in range(2):
                pass0_group(0, b)
            with dve.Fori(1, PAIRS) as i:
                for b in range(2):
                    pass0_group(i, b)
            carries(0)
            dve.wait_ge(scaled0, 3 * GROUPS)

            def one_step(s, source, target):
                with dve.Fori(0, PAIRS) as i:
                    for b in range(2):
                        g = 2 * i + b
                        for c in range(CHUNKS):
                            done = 2 * CHUNKS * (GROUPS * (s - 1) + g) + 2 * c
                            at = ds(g * U + c * CH, CH)
                            rows_c = got[b][:, c * CH:(c + 1) * CH, 0:D]
                            dve.wait_ge(gathered[b][c], 16 * CH * (PAIRS * s + i + 1))
                            V.tensor_tensor(rows_c, rows_c, bc(weight9[:, at], D), ALU.mult).then_inc(scaled, 1)
                            dve.wait_ge(scaled, done + 1)
                            V.tensor_tensor(rows_c, rows_c, xw[:, at, :], ALU.add).then_inc(scaled, 1)
                            dve.wait_ge(scaled, done + 2)
                            scan_chunk(s, i, b, c)
                carries(s)

            per_step(dve, one_step)

            def norm_step(i, b, k):
                g = 2 * i + b
                if k:
                    if k not in (4, 5):
                        dve.wait_ge(c_step, C_OPS * g + k)
                else:
                    for c in range(CHUNKS):
                        dve.wait_ge(gathered[b][c], 16 * CH * (PAIRS * K_STEPS + i + 1))
                    dve.wait_ge(c_act, 3 * g + 1)
                    for c in range(CHUNKS):
                        dve.wait_ge(sums_stored[b][c], 16 * PAIRS * K_STEPS)
                    if later(i, 1):
                        dve.wait_ge(x1_stored[b], 16 * i)
                    ins = V.scalar_tensor_tensor(sums[b][:, :, :], got[b][:, :, 0:D], 1.0 - ALPHA, xrow[b], ALU.mult, ALU.add)
                if k == 1:
                    ins = V.tensor_reduce(c_mean[:, :], sums[b][:, :, :], AX.X, ALU.add)
                if k == 2:
                    ins = V.tensor_scalar(c_mean[:, :], c_mean[:, :], 1.0 / D, None, ALU.mult)
                if k == 3:
                    ins = V.tensor_tensor(sums[b][:, :, :], sums[b][:, :, :], bc(c_mean[:, :], D), ALU.subtract)
                if k == 4:
                    dve.wait_ge(c_act, 3 * g + 2)
                    ins = V.tensor_reduce(c_sq[:, :], xrow[b], AX.X, ALU.add)
                if k == 5:
                    dve.wait_ge(c_act, 3 * g + 3)
                    ins = V.reciprocal(c_rs[:, :], c_sd[:, :])
                if k == 6:
                    ins = V.tensor_tensor(sums[b][:, :, :], sums[b][:, :, :], bc(c_rs[:, :], D), ALU.mult)
                ins.then_inc(c_step, 1)

            NORM_PARTS = (((0, 0), (0, 1)), ((0, 2), (0, 3)), ((0, 4),), ((0, 5), (0, 6), (1, 0)),
                          ((1, 1), (1, 2), (1, 3)), ((1, 4),), ((1, 5), (1, 6)))

            def hidden_var(net, x, b):
                for s, m, n in items(net, x):
                    dve.wait_ge(msq_ready, n)
                    V.scalar_tensor_tensor(half(net, v1, s), half(net, msq, s), -1.0, output(s, b)[:, :, D + 1], ALU.mult, ALU.add).then_inc(v1_ready, 1)

            def hidden_var_0(net, x):
                for m, n in both(net, x):
                    dve.wait_ge(v1_ready, n)
                    wait_old(dve, sd_ready, since(net, x, n, 1))
                    V.tensor_scalar(v1c, v1, 0.0, None, ALU.max).then_inc(v1c_ready, NS)

            def hidden_rs(net, x):
                for m, n in both(net, x):
                    dve.wait_ge(sd_ready, n)
                    V.reciprocal(rs1, sd1).then_inc(rs_ready, NS)

            def scale_hidden(net, x, b):
                for s, m, n in items(net, x):
                    dve.wait_ge(rs_ready, n)
                    wait_old(dve, normed, since(net, x, n, 2))
                    V.tensor_tensor(half(net, u[b], s), output(s, b)[:, :, 0:D], bc(half(net, rs1, s), D), ALU.mult).then_inc(scaled_u, 1)

            def add_c0(net, x, b):
                for m, n in both(net, x):
                    dve.wait_ge(scaled_u, n)
                    V.tensor_tensor(u[b], u[b], rows(c0[m][:, :], NS * Q), ALU.add).then_inc(u_ready, NS)

            def u_sums(net, x, b):
                for m, n in both(net, x):
                    dve.wait_ge(relu_ready, n)
                    V.tensor_reduce(mn, u[b], AX.X, ALU.add).then_inc(mean_sum, NS)

            def u_centre(net, x, b):
                for m, n in both(net, x):
                    dve.wait_ge(mean_sum, n)
                    V.scalar_tensor_tensor(u[b], bc(mn, D), -1.0 / D, u[b], ALU.mult, ALU.add).then_inc(centred, NS)

            def u_vars(net, x, b):
                for m, n in both(net, x):
                    dve.wait_ge(usq_ready, n)
                    wait_old(dve, sd2_ready, since(net, x, n, 1))
                    V.tensor_reduce(v2, usq[b], AX.X, ALU.add).then_inc(var_ready, NS)

            def u_rs(net, x):
                for m, n in both(net, x):
                    dve.wait_ge(sd2_ready, n)
                    V.reciprocal(rs2, sd2).then_inc(rs2_ready, NS)

            def norm(net, x, b, outs, free):
                for m, n in both(net, x):
                    dve.wait_ge(rs2_ready, n)
                    free()
                    V.tensor_tensor(outs, u[b], bc(rs2, D), ALU.mult).then_inc(normed, NS)

            def gain(net, x, outs):
                for m, n in both(net, x):
                    dve.wait_ge(normed, n)
                    V.tensor_tensor(outs, outs, rows(g1[m][:, :], NS * Q), ALU.mult).then_inc(gained, NS)

            def bias(net, x, outs):
                for m, n in both(net, x):
                    dve.wait_ge(gained, n)
                    V.tensor_tensor(outs, outs, rows(beta1[m][:, :], NS * Q), ALU.add).then_inc(out_ready, NS)

            def self_free(y, b):
                def free():
                    if later(y, 2):
                        dve.wait_ge(self_stored[b], 8 * (y - b))
                return free

            def norm_self_round(i, c, r, b):
                if r is not None:
                    hidden_var(SELF, r - 2, b)
                    u_vars(SELF, r - 3, 1 - b)
                    hidden_var_0(SELF, r - 2)
                    u_rs(SELF, r - 3)
                    hidden_rs(SELF, r - 2)
                    norm(SELF, r - 3, 1 - b, e_y[1 - b], self_free(r - 3, 1 - b))
                    scale_hidden(SELF, r - 2, b)
                    gain(SELF, r - 3, e_y[1 - b])
                    add_c0(SELF, r - 2, b)
                    bias(SELF, r - 3, e_y[1 - b])
                    u_sums(SELF, r - 2, b)
                    u_centre(SELF, r - 2, b)
                if i is not None:
                    for h, k in NORM_PARTS[c]:
                        norm_step(i, h, k)

            norm_and_self(dve, norm_self_round)
            dve.wait_ge(scanned, T * K_STEPS)
            link(V.memset(msum[1], 0.0))

            def msg_scan(y, b, t):
                if live(y, ROUNDS):
                    if t == 0:
                        if later(y, 2):
                            dve.wait_ge(msum_stored[b], 8 * (y - b))
                        dve.wait_ge(out_ready, MSG[0] + NS * (y + 1))
                    dve.wait_ge(scanned, T * K_STEPS + Q * y + t)
                    prev = msum[b][:, t - 1, :] if t else msum[1 - b][:, Q - 1, :]
                    V.scalar_tensor_tensor(msum[b][:, t, :], prev, same[:, ds(y * Q + t, 1)], messages[b][:, t, :],
                                           ALU.mult, ALU.add).then_inc(scanned, 1)

            def equal_src(y, b):
                if live(y, ROUNDS):
                    dve.wait_ge(m_val_loaded[b], 8 * (y - b + 2))
                    dve.wait_ge(eq_ps, y + 1)
                    if later(y, 2):
                        dve.wait_ge(dsum_ps, y - 1)
                    V.tensor_tensor(eq[b], ps_eq[:, :].rearrange("p (q n) -> p q n", n=P), bc(m_val[b][:, :], P),
                                    ALU.is_equal).then_inc(eq_ready, 1)

            def msg_round(r, b):
                y, o = r - 3, 1 - b
                outs = messages[o]

                def free():
                    if later(y, 2):
                        dve.wait_ge(scanned, T * K_STEPS + Q * (y - 1))
                        dve.wait_ge(dsum_ps, y - 1)
                hidden_var(MSG, r - 2, b)
                u_vars(MSG, y, o)
                hidden_var_0(MSG, r - 2)
                equal_src(y, o)
                u_rs(MSG, y)
                hidden_rs(MSG, r - 2)
                norm(MSG, y, o, outs, free)
                scale_hidden(MSG, r - 2, b)
                gain(MSG, y, outs)
                add_c0(MSG, r - 2, b)
                bias(MSG, y, outs)
                u_sums(MSG, r - 2, b)
                msg_scan(y, o, 0)
                u_centre(MSG, r - 2, b)
                for t in range(1, Q):
                    msg_scan(y, o, t)

            rounds(dve, ROUNDS, LEAD_M, M_TAIL, msg_round)
            carries(K_STEPS)

            def node_inputs(r, b):
                if live(r, NROUNDS):
                    dve.wait_ge(e_loaded[b], 8 * (r - b + 2))
                    dve.wait_ge(e_gathered[b], 16 * Q * (r - b + 2))
                    if later(r, 2):
                        dve.wait_ge(t_done, NODE[0] + NS * (r - 1))
                    V.tensor_tensor(e_x[b], e_agg[b], e_got[b], ALU.add).then_inc(e_ready, 1)

            def residual(y, b):
                if live(y, NROUNDS):
                    dve.wait_ge(out_ready, NODE[0] + NS * (y + 1))
                    dve.wait_ge(e_x1_loaded[b], 8 * (y - b + 2))
                    V.tensor_tensor(e_y[b], e_y[b], e_x1[b], ALU.add).then_inc(e_res, 1)

            def final_sums(y, b):
                if live(y, NROUNDS):
                    dve.wait_ge(e_res, y + 1)
                    V.tensor_reduce(f_mn, e_y[b], AX.X, ALU.add).then_inc(f_sum, 1)

            def final_centre(y, b):
                if live(y, NROUNDS):
                    dve.wait_ge(f_sum, y + 1)
                    V.scalar_tensor_tensor(e_y[b], bc(f_mn, D), -1.0 / D, e_y[b], ALU.mult, ALU.add).then_inc(f_cen, 1)

            def final_vars(y, b):
                if live(y, NROUNDS):
                    dve.wait_ge(f_sq, y + 1)
                    if later(y, 1):
                        dve.wait_ge(f_sd, y)
                    V.tensor_reduce(f_v2, e_sq[b], AX.X, ALU.add).then_inc(f_var, 1)

            def final_rs(y):
                if live(y, NROUNDS):
                    dve.wait_ge(f_sd, y + 1)
                    V.reciprocal(f_rs_t, f_sd_t).then_inc(f_rs, 1)

            def final_norm(y, b):
                if live(y, NROUNDS):
                    dve.wait_ge(f_rs, y + 1)
                    if later(y, 2):
                        dve.wait_ge(out_freed, y - 1)
                    V.tensor_tensor(e_out[b], e_y[b], bc(f_rs_t, D), ALU.mult).then_inc(f_out, 1)

            def node_round(r, b):
                o = 1 - b
                node_inputs(r, b)
                hidden_var(NODE, r - 2, b)
                u_vars(NODE, r - 3, o)
                hidden_var_0(NODE, r - 2)
                final_vars(r - 4, b)
                u_rs(NODE, r - 3)
                hidden_rs(NODE, r - 2)
                norm(NODE, r - 3, o, e_y[o], lambda: None)
                scale_hidden(NODE, r - 2, b)
                gain(NODE, r - 3, e_y[o])
                add_c0(NODE, r - 2, b)
                bias(NODE, r - 3, e_y[o])
                final_rs(r - 4)
                residual(r - 3, o)
                u_sums(NODE, r - 2, b)
                final_sums(r - 3, o)
                u_centre(NODE, r - 2, b)
                final_centre(r - 3, o)
                final_norm(r - 4, b)

            rounds(dve, NROUNDS, LEAD_N, N_TAIL, node_round)

        @block.tensor
        def _(pe):
            M = nc.tensor.matmul
            pe.wait_ge(const_all, 12)
            pe.wait_ge(ids_ready, 1)
            M(ps[0][:, 0:P], dst_f[:, 0:1].to_broadcast([P, P]), ident[:, :], start=True, stop=True).then_inc(weights_mm, 1)
            pe.wait_ge(weights_loaded, 16 * 27)
            for k, m in enumerate(MLPS):
                at = ps[1][:, k * D:(k + 1) * D]
                M(at, cols[m][:, 2:3].to_broadcast([P, P]), w1[m][:, :], start=True, stop=False)
                ins = M(at, ones[0:1, :], b1[m][:, :], start=False, stop=True)
            ins.then_inc(weights_mm, 1)
            pe.wait_ge(prep, WG_STEPS)
            for k, m in enumerate(MLPS):
                ins = M(ps[2][:, k * D:(k + 1) * D], center[:, :], wc[m][:, 0:D], start=True, stop=True)
            ins.then_inc(weights_mm, 1)

            def src_rows(i, b):
                g = 2 * i + b
                pe.wait_ge(src_slot_ready, g + 1)
                for c in range(U // Q):
                    bank = ps[6 + (b + c) % 2]
                    if not (isinstance(i, int) and b == 0 and c < 2):
                        pe.wait_ge(before_done, U // Q * g + c - 1)
                    for t in range(Q):
                        k = c * Q + t
                        ins = nc.tensor.transpose(bank[:, t * P:(t + 1) * P], src_slot[b][:, k:k + 1].to_broadcast([P, P]), ident[:, :])
                    ins.then_inc(eq_before_ps, 1)

            for b in range(2):
                src_rows(0, b)
            with pe.Fori(1, PAIRS) as i:
                for b in range(2):
                    src_rows(i, b)

            def carries(s, tail):
                if tail is None:
                    pe.wait_ge(scanned, T * (s + 1))
                    tail = sums[1][:, U - 1, :]
                else:
                    pe.wait_ge(scanned, T * K_STEPS + T)
                if not (isinstance(s, int) and s == 0):
                    pe.wait_ge(carry_ready, s)
                M(ps[0][:, 0:D], carry_sel[:, :], tail, start=True, stop=True).then_inc(carry_ps, 1)

            pe.wait_ge(graph_ready, 1)
            carries(0, None)
            per_step(pe, lambda s, source, target: carries(s, None))
            pe.wait_ge(weights_ready, 1)
            pe.wait_ge(carry_ready, K_STEPS)
            pe.wait_ge(before_done, U // Q * GROUPS)

            def transposes(x, xs, ready):
                for s, m, n in items(MSG, x):
                    ready(s)
                    wait_old(pe, xt_ready, since(MSG, x, n, 1))
                    pe.sem_inc(pe_passed, 1)
                    for t in range(Q):
                        ins = nc.tensor.transpose(ps_a[s][0:KIN[m], t * P:(t + 1) * P], xs[s][:, t, :], ident[:, :])
                    ins.then_inc(t_done, 1)

            def pair_transposes(net, x, xs):
                for m, n in both(net, x):
                    wait_old(pe, xt_ready, since(net, x, n, 1))
                    for t in range(Q):
                        ins = nc.tensor.transpose(ps_a[0][:, t * P:(t + 1) * P],
                                                  xs[:, NS * t:NS * (t + 1), :].rearrange("p s d -> p (s d)"), ident[:, :])
                    ins.then_inc(t_done, NS)

            def hidden(net, x, b):
                for s, m, n in items(net, x):
                    pe.wait_ge(xt_ready, n)
                    wait_old(pe, scaled_u, since(net, x, n, 2))
                    if net is MSG:
                        weights, rows_t = w0[m][:, :], xt[s][0:KIN[m], :]
                    else:
                        weights, rows_t = w0[m][s * D:(s + 1) * D, :], xt[0][s * D:(s + 1) * D, :]
                    M(bank(s, b)[:, :], weights, rows_t, start=True, stop=True).then_inc(h_done, 1)

            def second_layer(net, x, b):
                for s, m, n in items(net, x):
                    pe.wait_ge(ht_ready, n)
                    for t in range(Q):
                        M(output(s, b)[:, t, 0:D + 1], ht[b][s][:, t * P:(t + 1) * P], wc[m][:, :], start=True, stop=True)

            def hidden_squares(net, x, b):
                for s, m, n in items(net, x):
                    pe.wait_ge(sq_ready, n)
                    for t in range(Q):
                        ins = M(output(s, b)[:, t, D + 1:D + 2], sq[b][s][:, t * P:(t + 1) * P], mean_h[:, :], start=True, stop=True)
                    ins.then_inc(q_done, 1)

            def src_columns(y, b):
                if live(y, ROUNDS):
                    pe.wait_ge(m_val_loaded[b], 8 * (y - b + 2))
                    if later(y, 1):
                        pe.wait_ge(eq_ready, y)
                    for t in range(Q):
                        ins = nc.tensor.transpose(ps_eq[:, t * P:(t + 1) * P], m_val[b][:, t:t + 1].to_broadcast([P, P]), ident[:, :])
                    ins.then_inc(eq_ps, 1)

            def column_sums(y, b):
                if live(y, ROUNDS):
                    pe.wait_ge(out_ready, MSG[0] + NS * y + 2)
                    pe.wait_ge(eq_ready, y + 1)
                    if later(y, 1):
                        pe.wait_ge(dsum_ready, y)
                    for t in range(Q):
                        ins = M(ps_sum[:, t * D:(t + 1) * D], eq[b][:, t, :], messages[b][:, Q + t, :], start=True, stop=True)
                    ins.then_inc(dsum_ps, 1)

            def norm_self_round(i, c, r, b):
                if r is not None:
                    if live(r, NROUNDS):
                        pe.wait_ge(self_loaded[b], 8 * (r - b + 2))
                    pair_transposes(SELF, r, e_x[b])
                    second_layer(SELF, r - 1, 1 - b)
                    hidden(SELF, r, b)
                    hidden_squares(SELF, r - 1, 1 - b)

            norm_and_self(pe, norm_self_round)

            def msg_round(r, b):
                def ready(s):
                    pe.wait_ge(m_got[b], 16 * Q * (r - b + 2))
                    pe.wait_ge(m_rows[b], 16 * (r - b + 2))
                transposes(r, x_in[b], ready)
                src_columns(r - 3, 1 - b)
                second_layer(MSG, r - 1, 1 - b)
                hidden(MSG, r, b)
                column_sums(r - 4, b)
                hidden_squares(MSG, r - 1, 1 - b)

            rounds(pe, ROUNDS, LEAD_M, M_TAIL, msg_round)
            carries(K_STEPS, msum[1][:, Q - 1, :])
            pe.wait_ge(carry_ready, K_STEPS + 1)

            def node_round(r, b):
                if live(r, NROUNDS):
                    pe.wait_ge(e_ready, r + 1)
                pair_transposes(NODE, r, e_x[b])
                second_layer(NODE, r - 1, 1 - b)
                hidden(NODE, r, b)
                hidden_squares(NODE, r - 1, 1 - b)

            rounds(pe, NROUNDS, LEAD_N, N_TAIL, node_round)


def kernel(**inputs):
    from concourse import bacc
    from concourse.bass_utils import run_bass_kernel_spmd

    nc = bacc.Bacc("TRN2", target_bir_lowering=False, num_devices=1)
    arrays, aps = {}, {}
    for name, value in inputs.items():
        a = np.ascontiguousarray(value)
        arrays[f"in_{name}"] = a
        aps[name] = nc.dram_tensor(f"in_{name}", a.shape, mybir.dt.from_np(a.dtype), kind="ExternalInput").ap()
    out = nc.dram_tensor("out_x", (N, D), mybir.dt.float32, kind="ExternalOutput").ap()
    build_program(nc, aps, out)
    result = run_bass_kernel_spmd(nc, [arrays], core_ids=[0])
    return result.results[0]["out_x"]
```
